# Optimizing a Trainium2 kernel written in Bass

```python
import numpy as np
import jax
import jax.numpy as jnp

def _softmax(x, axis=-1):
    return jax.nn.softmax(x, axis=axis)

def _gelu(x):
    return jax.nn.gelu(x, approximate=True)

def _silu(x):
    return jax.nn.silu(x)

def _sigmoid(x):
    return jax.nn.sigmoid(x)

def _layernorm(x, axis=-1, eps=1e-05):
    m = jnp.mean(x, axis=axis, keepdims=True)
    v = jnp.var(x, axis=axis, keepdims=True)
    return (x - m) / jnp.sqrt(v + eps)

def _scatter_add(tgt, idx, src, axis=0):
    return tgt.at[idx].add(src)

def _segment_sum(src, seg, n):
    return jax.ops.segment_sum(src, seg, n)
kernel_name = 'mk_gnn_preln_d2_gnn_r64_c1830c'

def setup_inputs(seed: int=0):
    np.random.seed(seed)
    _w = jnp.asarray

    def _rec_inputs():
        import jax
        import jax.numpy as jnp
        _gk = jax.random.key(seed)
        x = -0.0001126 + 1 * jax.random.normal(jax.random.fold_in(_gk, 1), (10000, 768), jnp.float32)
        src = jax.random.randint(jax.random.fold_in(_gk, 2), (2500,), 0, 10000, jnp.int32)
        dst = jax.random.randint(jax.random.fold_in(_gk, 3), (2500,), 0, 10000, jnp.int32)
        _o = jnp.argsort(dst, stable=True)
        src = src[_o]
        dst = dst[_o]
        return (x, src, dst)
    x, src, dst = _rec_inputs()

    def _L0_gnn_setup():
        import jax, jax.numpy as jnp
        import numpy as np
        N_NODES = 10000
        N_EDGES = 100000
        DIM = 768
        NEG_SLOPE = 0.2

        def gat_conv(x, src, dst, W, att_src, att_dst, bias, num_nodes):
            h = x @ W
            a_s = h @ att_src
            a_d = h @ att_dst
            e = jax.nn.leaky_relu(a_s[src] + a_d[dst], NEG_SLOPE)
            m = jax.ops.segment_max(e, dst, num_segments=num_nodes)
            e = jnp.exp(e - m[dst])
            denom = jax.ops.segment_sum(e, dst, num_segments=num_nodes)
            alpha = e / denom[dst]
            msg = alpha[:, None] * h[src]
            out = jax.ops.segment_sum(msg, dst, num_segments=num_nodes)
            return out + bias
        key = jax.random.key(seed)
        ks = jax.random.split(key, 12)
        s = 1.0 / np.sqrt(DIM)
        inp = {'x': jax.random.normal(ks[0], (N_NODES, DIM), dtype=jnp.float32), 'edge_index': jax.random.randint(ks[1], (2, N_EDGES), 0, N_NODES, dtype=jnp.int64), 'W1': jax.random.normal(ks[2], (DIM, DIM), dtype=jnp.float32) * s, 'att_src1': jax.random.normal(ks[3], (DIM,), dtype=jnp.float32) * s, 'att_dst1': jax.random.normal(ks[4], (DIM,), dtype=jnp.float32) * s, 'b1': jnp.zeros((DIM,), dtype=jnp.float32), 'W2': jax.random.normal(ks[5], (DIM, DIM), dtype=jnp.float32) * s, 'att_src2': jax.random.normal(ks[6], (DIM,), dtype=jnp.float32) * s, 'att_dst2': jax.random.normal(ks[7], (DIM,), dtype=jnp.float32) * s, 'b2': jnp.zeros((DIM,), dtype=jnp.float32)}
        return inp
    _L0_gnn_all = _L0_gnn_setup()
    _L0_gnn_in = {k: v for k, v in _L0_gnn_all.items() if k in ('W1', 'att_src1', 'att_dst1', 'b1', 'W2', 'att_src2', 'att_dst2', 'b2')}
    del _L0_gnn_all

    def _L1_gnn_setup():
        import jax, jax.numpy as jnp
        import numpy as np
        N_NODES = 10000
        D = 768
        N_EDGES = 2500

        def gcn_conv(x, W, b, src, dst, n_nodes):
            h = x @ W
            deg = jax.ops.segment_sum(jnp.ones_like(dst, dtype=h.dtype), dst, num_segments=n_nodes)
            dinv = jnp.where(deg > 0, jax.lax.rsqrt(deg), 0.0)
            norm = dinv[src] * dinv[dst]
            msgs = h[src] * norm[:, None]
            out = jax.ops.segment_sum(msgs, dst, num_segments=n_nodes)
            return out + b

        def add_self_loops(edge_index, n_nodes):
            loop = jnp.arange(n_nodes, dtype=edge_index.dtype)
            src = jnp.concatenate([edge_index[0], loop])
            dst = jnp.concatenate([edge_index[1], loop])
            return (src, dst)
        key = jax.random.key(seed)
        k1, k2, k3, k4 = jax.random.split(key, 4)
        x = jax.random.normal(k1, (N_NODES, D), dtype=jnp.float32)
        edge_index = jax.random.randint(k2, (2, N_EDGES), 0, N_NODES, dtype=jnp.int32)
        glorot = float(np.sqrt(6.0 / (D + D)))
        W1 = jax.random.uniform(k3, (D, D), jnp.float32, -glorot, glorot)
        W2 = jax.random.uniform(k4, (D, D), jnp.float32, -glorot, glorot)
        b1 = jnp.zeros((D,), jnp.float32)
        b2 = jnp.zeros((D,), jnp.float32)
        return {'x': x, 'W1': W1, 'b1': b1, 'W2': W2, 'b2': b2, 'edge_index': edge_index}
    _L1_gnn_all = _L1_gnn_setup()
    _L1_gnn_in = {k: v for k, v in _L1_gnn_all.items() if k in ('W1', 'b1', 'W2', 'b2')}
    del _L1_gnn_all
    return {'x': x, 'src': src, 'dst': dst, 'L0_gnn_W1': _L0_gnn_in['W1'], 'L0_gnn_att_src1': _L0_gnn_in['att_src1'], 'L0_gnn_att_dst1': _L0_gnn_in['att_dst1'], 'L0_gnn_b1': _L0_gnn_in['b1'], 'L0_gnn_W2': _L0_gnn_in['W2'], 'L0_gnn_att_src2': _L0_gnn_in['att_src2'], 'L0_gnn_att_dst2': _L0_gnn_in['att_dst2'], 'L0_gnn_b2': _L0_gnn_in['b2'], 'L1_gnn_W1': _L1_gnn_in['W1'], 'L1_gnn_b1': _L1_gnn_in['b1'], 'L1_gnn_W2': _L1_gnn_in['W2'], 'L1_gnn_b2': _L1_gnn_in['b2']}

def reference(x, src, dst, L0_gnn_W1, L0_gnn_att_src1, L0_gnn_att_dst1, L0_gnn_b1, L0_gnn_W2, L0_gnn_att_src2, L0_gnn_att_dst2, L0_gnn_b2, L1_gnn_W1, L1_gnn_b1, L1_gnn_W2, L1_gnn_b2):
    import jax
    import jax.numpy as jnp

    def _L0_gnn_ref(x, edge_index, W1, att_src1, att_dst1, b1, W2, att_src2, att_dst2, b2):
        import jax, jax.numpy as jnp
        import numpy as np
        N_NODES = 10000
        N_EDGES = 100000
        DIM = 768
        NEG_SLOPE = 0.2

        def gat_conv(x, src, dst, W, att_src, att_dst, bias, num_nodes):
            h = x @ W
            a_s = h @ att_src
            a_d = h @ att_dst
            e = jax.nn.leaky_relu(a_s[src] + a_d[dst], NEG_SLOPE)
            m = jax.ops.segment_max(e, dst, num_segments=num_nodes)
            e = jnp.exp(e - m[dst])
            denom = jax.ops.segment_sum(e, dst, num_segments=num_nodes)
            alpha = e / denom[dst]
            msg = alpha[:, None] * h[src]
            out = jax.ops.segment_sum(msg, dst, num_segments=num_nodes)
            return out + bias
        n = x.shape[0]
        loops = jnp.arange(n, dtype=edge_index.dtype)
        src = jnp.concatenate([edge_index[0], loops])
        dst = jnp.concatenate([edge_index[1], loops])
        h = gat_conv(x, src, dst, W1, att_src1, att_dst1, b1, n)
        h = jax.nn.relu(h)
        out = gat_conv(h, src, dst, W2, att_src2, att_dst2, b2, n)
        return out

    def _L1_gnn_ref(x, W1, b1, W2, b2, edge_index):
        import jax, jax.numpy as jnp
        import numpy as np
        N_NODES = 10000
        D = 768
        N_EDGES = 2500

        def gcn_conv(x, W, b, src, dst, n_nodes):
            h = x @ W
            deg = jax.ops.segment_sum(jnp.ones_like(dst, dtype=h.dtype), dst, num_segments=n_nodes)
            dinv = jnp.where(deg > 0, jax.lax.rsqrt(deg), 0.0)
            norm = dinv[src] * dinv[dst]
            msgs = h[src] * norm[:, None]
            out = jax.ops.segment_sum(msgs, dst, num_segments=n_nodes)
            return out + b

        def add_self_loops(edge_index, n_nodes):
            loop = jnp.arange(n_nodes, dtype=edge_index.dtype)
            src = jnp.concatenate([edge_index[0], loop])
            dst = jnp.concatenate([edge_index[1], loop])
            return (src, dst)
        n = x.shape[0]
        src, dst = add_self_loops(edge_index, n)
        h = gcn_conv(x, W1, b1, src, dst, n)
        h = jax.nn.relu(h)
        out = gcn_conv(h, W2, b2, src, dst, n)
        return out
    edge_index = jnp.stack([src, dst])
    h = jnp.maximum(_layernorm(x, axis=-1), 0.0)
    x = x + _L0_gnn_ref(h, edge_index, L0_gnn_W1, L0_gnn_att_src1, L0_gnn_att_dst1, L0_gnn_b1, L0_gnn_W2, L0_gnn_att_src2, L0_gnn_att_dst2, L0_gnn_b2)
    h = jnp.maximum(_layernorm(x, axis=-1), 0.0)
    x = x + _L1_gnn_ref(h, L1_gnn_W1, L1_gnn_b1, L1_gnn_W2, L1_gnn_b2, edge_index)
    return x

_drawn_inputs = setup_inputs


def setup_inputs(seed=0):
    import zlib

    import numpy as np

    out = dict(_drawn_inputs(seed))
    spreads = {'L0_gnn_b1': (0.0, 0.1),
     'L0_gnn_b2': (0.0, 0.1),
     'L1_gnn_b1': (0.0, 0.1),
     'L1_gnn_b2': (0.0, 0.1)}
    factors = {'L0_gnn_att_src1': 3.496,
     'L0_gnn_att_dst1': 8.0,
     'L0_gnn_att_src2': 6.991,
     'L0_gnn_att_dst2': 8.0}
    for name, (base, spread) in spreads.items():
        noise = np.random.default_rng([zlib.crc32(name.encode()), seed]).standard_normal(out[name].shape)
        drawn = base * np.exp(spread * noise) if base else spread * noise
        out[name] = jnp.asarray(drawn.astype(out[name].dtype))
    for name, factor in factors.items():
        out[name] = (out[name] * factor).astype(out[name].dtype)
    return out
```

```python
from contextlib import ExitStack

import concourse.bass as bass
from concourse import mybir

P = 128
F32 = mybir.dt.float32
F16 = mybir.dt.float16
I32 = mybir.dt.int32
ALU = mybir.AluOpType
ACT = mybir.ActivationFunctionType
AX_X = mybir.AxisListType.X
RMAX = bass.bass_isa.ReduceOp.max

NEG_SLOPE = 0.2
EPS = 1e-5
TINY = 1e-30
FAR = 1e30
EXPONENT = 0x7F800000


class Tile:

    def __init__(self, phase, at, i=None, step=4):
        self.phase, self.at, self.i, self.step = phase, at, i, step

    def plus(self, k):
        return Tile(self.phase, self.at + k, self.i, self.step)

    def count(self, before, every=1):
        c = (before + self.at) // every
        return c if self.i is None else self.i * (self.step // every) + c

    @property
    def g(self):
        return self.count(self.phase["g0"])

    @property
    def slot(self):
        return (self.phase["g0"] + self.at) % 2

    @property
    def slot4(self):
        return (self.phase["g0"] + self.at) % 4

    @property
    def slot_uses(self):
        return self.count(self.phase["g0"], 2)

    @property
    def later_uses(self):
        return self.count(self.phase["g0"] - self.phase["nt"], 2)

    @property
    def pos(self):
        return self.count(self.phase["first"])

    @property
    def layer_uses(self):
        return (self.phase["first"] + self.at) // 2 if self.i is None else self.i * (self.step // 2) + (self.phase["first"] + self.at) // 2


def wait(e, sem, value):
    if not isinstance(value, int) or value > 0:
        e.wait_ge(sem, value)


def run_windows(e, phase, window, between=None):
    n = phase["n"]
    t = -4
    starts = {start: (turns, side) for start, turns, side in phase["loops"]}
    while t <= n:
        if t in starts:
            turns, side = starts[t]
            with e.Fori(0, turns) as i:
                for r in range(4):
                    window(Tile(phase, t + r, i), lambda k: True, side, i, r)
            t += 4 * turns
            if between and t == phase.get("between"):
                between()
            continue
        window(Tile(phase, t), lambda k, t=t: 0 <= t + k < n, None, None, 0)
        t += 1


def build(nc, x, src, dst, w, att_src, att_dst, bias, out):
    N, D = x.shape
    E = src.shape[0]
    KC = D // P
    HALF = D // 2
    NT = -(-N // P)
    NP = NT * P
    LAST = N - (NT - 1) * P
    EC = -(-E // P)
    ER = -(-E // EC)
    assert ER * EC == E and EC * P == -(-E // P) * P
    EP = EC * P
    SLOTS = P - 1
    ET = EC
    assert ET * SLOTS >= E and (ET - 1) * SLOTS < E
    PAD = NP - 1
    assert PAD >= N
    FREE = (NP - E - 1) // P
    MIXED = NT - FREE
    AGG = NP
    ROWS = NP + ET * P
    COLS = 10
    SHARE = [(0, 1, 2), (3, 4, 5), (6, 7), (8, 9)]

    phases = {}
    g = 0
    for layer in (1, 2, 3, 4):
        if layer == 1:
            phases["1"] = dict(layer=1, n=NT, g0=0, first=0, mixed=False, between=42,
                               loops=[(2, 10, "rank"), (42, 5, "order+mask"), (62, 3, "order")])
            g = NT
            continue
        phases[f"{layer}f"] = dict(layer=layer, n=FREE, g0=g, first=0, mixed=False,
                                   loops=[(2, ET // 2, "edges"), (2 + 2 * ET, (FREE - 6 - 2 * ET) // 4, None)])
        phases[f"{layer}m"] = dict(layer=layer, n=MIXED, g0=g + FREE, first=FREE, mixed=True,
                                   loops=[(2, (MIXED - 6) // 4, None)])
        g += NT
    for ph in phases.values():
        ph["nt"] = NT
        ph["edge0"] = {1: 0, 2: 0, 3: ET, 4: 2 * ET}[ph["layer"]]

    def all_slots(first, tiles):
        return [(first % 2, 16 * -(-tiles // 2)), (1 - first % 2, 16 * (tiles // 2))]

    table = {n: nc.dram_tensor(f"rows_{n}", [ROWS, D], F32).ap() for n in (1, 2, 3, 4)}
    x1_rows = nc.dram_tensor("x1_rows", [NP, D], F32).ap()

    ctx = ExitStack()
    with ctx:
        def sb(name, shape, dt=F32):
            return ctx.enter_context(nc.sbuf_tensor(name, shape, dt))

        def sem(name):
            return ctx.enter_context(nc.semaphore(name))

        w_hi = [sb(f"w_hi{s}", [P, KC, D], F16) for s in range(3)]
        w_lo = [sb(f"w_lo{s}", [P, KC, D], F16) for s in range(3)]
        w_raw = sb("w_raw", [P, KC * D])
        w_of = {1: 0, 2: 1, 3: 2, 4: 0}
        w_scale = sb("w_scale", [P, 4, 4])
        row_in = [sb(f"row_in{s}", [P, D]) for s in range(2)]
        row_in2 = [sb(f"row_in2{s}", [P, D]) for s in range(2)]
        pre = [sb(f"pre{s}", [P, D]) for s in range(2)]
        z = [sb(f"z{s}", [P, D]) for s in range(2)]
        z_hi = [sb(f"z_hi{s}", [P, KC, P], F16) for s in range(2)]
        z_lo = [sb(f"z_lo{s}", [P, KC, P], F16) for s in range(2)]
        row_out = [sb(f"row_out{s}", [P, D]) for s in range(2)]
        pre_out = [sb(f"pre_out{s}", [P, D]) for s in range(2)]
        bn = [sb(f"bn{s}", [P, 12]) for s in range(2)]
        mv = [sb(f"mv{s}", [P, 2]) for s in range(4)]
        veps = [sb(f"veps{s}", [P, 1]) for s in range(4)]
        rstd = [sb(f"rstd{s}", [P, 1]) for s in range(4)]
        nmr = [sb(f"nmr{s}", [P, 1]) for s in range(4)]
        top = [sb(f"top{s}", [P, 1]) for s in range(4)]
        topc = [sb(f"topc{s}", [P, 1]) for s in range(4)]
        shrink = [sb(f"shrink{s}", [P, 1]) for s in range(4)]
        grow = [sb(f"grow{s}", [P, 1]) for s in range(4)]
        idx_a = [sb(f"idx_a{s}", [P, 1], I32) for s in range(2)]
        idx_b = [sb(f"idx_b{s}", [P, 1], I32) for s in range(2)]
        idx_o = [sb(f"idx_o{s}", [P, 1], I32) for s in range(2)]
        bias_bc = {n: sb(f"bias_bc{n}", [P, D]) for n in (1, 2, 3, 4)}
        atts_bc = {n: sb(f"atts_bc{n}", [P, D]) for n in (1, 2)}
        attd_bc = {n: sb(f"attd_bc{n}", [P, D]) for n in (1, 2)}
        ident = sb("ident", [P, P])
        ones = sb("ones", [P, P])
        upper = sb("upper", [P, P])
        half_neg = sb("half_neg", [P, 1])
        iota_c = sb("iota_c", [P, P])
        iota_m1 = sb("iota_m1", [P, P])
        node_id = sb("node_id", [P, NT])
        node_id_pad = sb("node_id_pad", [P, COLS * (-(-NT // COLS))])
        cnt_pad = sb("cnt_pad", [P, COLS * (-(-NT // COLS))])
        edge_id = sb("edge_id", [P, EC])
        tile_ends = sb("tile_ends", [P, ET])
        rank_mem = sb("rank_mem", [P, 3, EP])
        row_dst, row_cmp, row_iota = (rank_mem[:, k, :] for k in range(3))
        masks = rank_mem[:, 0:2, :].rearrange("p a (t q) -> p a t q", q=P)
        far_mask, same_t = masks[:, 0], masks[:, 1]
        e_src = sb("e_src", [P, EC], I32)
        e_dst = sb("e_dst", [P, EC], I32)
        e_part = sb("e_part", [P, 2, EC], I32)
        e_f = sb("e_f", [P, 5, EC])
        e_rank = sb("e_rank", [P, 4, EC])
        onehot = w_raw[:, 0:COLS * 3 * P].rearrange("p (k c) -> p k c", k=COLS)
        sorts = sb("sorts", [P, 2, 2 * ET])
        diag2 = sb("diag2", [P, 2, P])
        sorted_src = sb("sorted_src", [P, ET], I32)
        sorted_dst_i = sb("sorted_dst_i", [P, ET], I32)
        dst_of = sb("dst_of", [P, ET])
        dst_in = sb("dst_in", [P, ET])
        flag_cnt = sb("flag_cnt", [P, 2, NT])
        scan = [sb(f"scan{s}", [P, 2, NT]) for s in range(3)]
        work = sb("work", [P, 4, NT])
        place = sb("place", [P, 3, COLS * (-(-NT // COLS))])
        place_i = sb("place_i", [P, 3, NT], I32)
        perm_f = sb("perm_f", [P, 3, NT])
        perm = sb("perm", [P, NT], I32)
        perm_x = sb("perm_x", [P, NT], I32)
        perm_agg = sb("perm_agg", [P, NT], I32)
        dinv = sb("dinv", [P, NT])
        dinv_grow = sb("dinv_grow", [P, 2, NT])
        eg = [sb(f"eg{s}", [P, D + 1]) for s in range(2)]
        eh = [sb(f"eh{s}", [P, D]) for s in range(2)]
        idx_s = [sb(f"idx_s{s}", [P, 1], I32) for s in range(2)]
        idx_d = [sb(f"idx_d{s}", [P, 1], I32) for s in range(2)]
        e_tmp = sb("e_tmp", [P, D])
        e_prod = sb("e_prod", [P, D])
        e_out = sb("e_out", [P, D])
        zeros = e_out[:, 0:512]
        dots = sb("dots", [P, 3])
        score = sb("score", [P, 2])
        lrelu = sb("lrelu", [P, 2])
        e_max = [sb(f"e_max{s}", [P, 1]) for s in range(2)]
        e_top = sb("e_top", [P, 1])
        e_negmax = sb("e_negmax", [P, 1])
        e_self = sb("e_self", [P, 1])
        e_den = sb("e_den", [P, 2])
        e_diag = sb("e_diag", [P, P])
        e_arg = sb("e_arg", [P, P])
        e_wt = sb("e_wt", [P, P])
        e_wt_t = sb("e_wt_t", [P, P])

        ps_z = ctx.enter_context(nc.psum_tensor("ps_z", [P, 2, 512], F32))
        ps_h = [ctx.enter_context(nc.psum_tensor(f"ps_h{s}", [P, 2, 512], F32)) for s in range(2)]
        ps_e = ctx.enter_context(nc.psum_tensor("ps_e", [P, 2, 512], F32))
        SPLIT = HALF + 1
        e_lo, e_hi = ps_e[:, 0, 0:SPLIT], ps_e[:, 1, 0:D + 1 - SPLIT]
        e_den_ps = ps_e[:, 1, D - SPLIT:D + 1 - SPLIT]
        e_small = ps_e[:, 1, HALF:HALF + P]
        sort_ps = ps_e[:, 0, 0:2 * ET]
        count_ps = ps_e[:, 1, 0:NT]
        perm_ps = ps_e[:, 0, 0:3 * NT]
        mask_ps = ps_e[:, 1, 0:2 * P]

        consts_ready = sem("consts_ready")
        params_loaded = sem("params_loaded")
        graph_loaded = sem("graph_loaded")
        graph_padded = sem("graph_padded")
        setup_step = sem("setup_step")
        w_loaded = sem("w_loaded")
        w_max = sem("w_max")
        w_max_all = sem("w_max_all")
        w_scaled = sem("w_scaled")
        w_hi_ready = sem("w_hi_ready")
        w_ready = sem("w_ready")
        x_loaded = [sem(f"x_loaded{s}") for s in range(2)]
        in_ready = [sem(f"in_ready{s}") for s in range(2)]
        in_used = sem("in_used")
        x_ready = [sem(f"x_ready{s}") for s in range(2)]
        x1_loaded = [sem(f"x1_loaded{s}") for s in range(2)]
        x1_ready = sem("x1_ready")
        x1_stored = [sem(f"x1_stored{s}") for s in range(2)]
        x1_used = sem("x1_used")
        stats_done = sem("stats_done")
        mean_var = sem("mean_var")
        var_eps = sem("var_eps")
        rstd_done = sem("rstd_done")
        norm_ready = sem("norm_ready")
        top_found = sem("top_found")
        top_kept = sem("top_kept")
        shrink_ready = sem("shrink_ready")
        grow_ready = sem("grow_ready")
        z_ready = sem("z_ready")
        z_turned = sem("z_turned")
        z_hi_ready = sem("z_hi_ready")
        z_lo_ready = sem("z_lo_ready")
        h_ready = sem("h_ready")
        row_ready = sem("row_ready")
        row1_stored = [sem(f"row1_stored{s}") for s in range(2)]
        row_stored = [sem(f"row_stored{s}") for s in range(2)]
        res_ready = sem("res_ready")
        res_stored = [sem(f"res_stored{s}") for s in range(2)]
        idx_in_ready = sem("idx_in_ready")
        idx_out_ready = sem("idx_out_ready")
        pool_gate = sem("pool_gate")
        dve_gate = sem("dve_gate")
        ranks_step = sem("ranks_step")
        onehot_ready = sem("onehot_ready")
        onehot_used = sem("onehot_used")
        mid_mm = sem("mid_mm")
        mid_in = sem("mid_in")
        place_ready = sem("place_ready")
        place_used = sem("place_used")
        dst_diag = sem("dst_diag")
        mask_mm = sem("mask_mm")
        mask_part = sem("mask_part")
        mask_ready = sem("mask_ready")
        perm_ready = sem("perm_ready")
        sqrt_in = sem("sqrt_in")
        sqrt_done = sem("sqrt_done")
        eidx_ready = sem("eidx_ready")
        e_rows = [sem(f"e_rows{s}") for s in range(2)]
        dots_done = sem("dots_done")
        score_done = sem("score_done")
        lrelu_done = sem("lrelu_done")
        score_fixed = sem("score_fixed")
        diag_ready = sem("diag_ready")
        score_rows = sem("score_rows")
        arg_done = sem("arg_done")
        top_done = sem("top_done")
        max_done = sem("max_done")
        negmax_ready = sem("negmax_ready")
        weights_done = sem("weights_done")
        weights_turned = sem("weights_turned")
        weights_ready = sem("weights_ready")
        carry_ready = sem("carry_ready")
        e_summed = sem("e_summed")
        den_done = sem("den_done")
        den_inv = sem("den_inv")
        edge_done = sem("edge_done")
        e_out_ready = sem("e_out_ready")
        e_stored = sem("e_stored")
        f_in = [sem(f"f_in{s}") for s in range(2)]
        f_x1 = [sem(f"f_x1{s}") for s in range(2)]
        f_idx = sem("f_idx")
        f_sum = sem("f_sum")
        f_ready = sem("f_ready")
        f_stored = [sem(f"f_stored{s}") for s in range(2)]

        block = ctx.enter_context(nc.Block())
        GATS = (1, 2)

        def w_view(t):
            return t[:, :].rearrange("p (c n) -> p c n", c=KC)

        def psum_pair(t):
            return t[:, :, 0:HALF]

        def pair(t):
            return t[:, :].rearrange("p (a n) -> p a n", a=2)

        def pair3(t):
            return t[:, :, :].rearrange("p (a c) n -> p a (c n)", a=2)

        def ln_count(t):
            return t.count(t.phase["g0"] if t.phase["layer"] == 1 else t.phase["g0"] - NT)

        def top_count(t):
            return t.count(t.phase["g0"] - NT if t.phase["layer"] == 2 else t.phase["g0"] - 2 * NT)

        @block.sync
        def _(sp):
            def load_w(layer):
                if layer > 1:
                    sp.wait_ge(w_ready, layer - 1)
                if layer == 2:
                    sp.wait_ge(onehot_used, 2 + EC)
                sp.dma_start(w_view(w_raw), w[layer].rearrange("(c p) n -> p c n", p=P)).then_inc(w_loaded, 16)

            def row_of(v):
                return bass.AP(v.tensor, v.offset, [[0, P], [1, v.shape[0]]])

            def load_x(t):
                if t.i is None and t.at == NT - 1:
                    wait(sp, z_ready, t.g - 1)
                    sp.dma_start(row_in[t.slot][0:LAST, :], x[(NT - 1) * P:N, :]).then_inc(x_loaded[t.slot], 16)
                    return
                wait(sp, z_ready, t.g - 1)
                at = t.count(0) * P
                sp.dma_start(row_in[t.slot][:, :], x[bass.ds(at, P), :]).then_inc(x_loaded[t.slot], 16)

            def window1(t, has, side, i, r):
                if has(-1):
                    b = t.plus(-1)
                    wait(sp, row_ready, b.g + 1)
                    sp.dma_start(table[1][bass.ds(b.count(0) * P, P), :], row_out[b.slot][:, :]).then_inc(row1_stored[b.slot], 16)
                if has(4):
                    load_x(t.plus(4))

            def edge_store(layer, h, j):
                if layer in GATS:
                    sp.wait_ge(e_out_ready, h + 1)
                else:
                    sp.wait_ge(edge_done, h + 3)
                sp.dma_start(table[layer][bass.ds(j * P + AGG, P), :], e_out[:, :]).then_inc(e_stored, 16)

            def window(t, has, side, i, r):
                layer = t.phase["layer"]
                if layer == 3 and has(2):
                    b = t.plus(2)
                    wait(sp, x1_ready, b.count(b.phase["first"]) + 1)
                    sp.dma_start(x1_rows[bass.ds(b.pos * P, P), :], pre[b.slot][:, :]).then_inc(x1_stored[b.slot], 16)
                if layer == 4 and not t.phase["mixed"] and has(1):
                    b = t.plus(1)
                    wait(sp, x1_used, b.pos - 1)
                    sp.dma_start(row_in2[b.slot][:, :], x1_rows[bass.ds(b.pos * P, P), :]).then_inc(x1_loaded[b.slot], 16)
                if side == "edges" and r % 2:
                    j = i * 2 + r // 2
                    edge_store(layer - 1, j + t.phase["edge0"], j)

            load_w(1)
            sp.wait_ge(graph_padded, 1)
            sp.dma_start(e_src[0:ER, :], src.rearrange("(p c) -> p c", c=EC)).then_inc(graph_loaded, 16)
            sp.dma_start(e_dst[0:ER, :], dst.rearrange("(p c) -> p c", c=EC)).then_inc(graph_loaded, 16)
            sp.dma_start(row_cmp[:, 0:E].bitcast(I32), row_of(dst)).then_inc(graph_loaded, 16)
            sp.sem_inc(e_stored, 16)
            run_windows(sp, phases["1"], window1, lambda: (load_w(2), load_w(3)))
            for n in (1, 2, 3, 4):
                sp.dma_start(bias_bc[n][:, :], row_of(bias[n])).then_inc(params_loaded, 16)
            for n in GATS:
                sp.dma_start(atts_bc[n][:, :], row_of(att_src[n])).then_inc(params_loaded, 16)
                sp.dma_start(attd_bc[n][:, :], row_of(att_dst[n])).then_inc(params_loaded, 16)
            run_windows(sp, phases["2f"], window)
            load_w(4)
            run_windows(sp, phases["2m"], window)
            run_windows(sp, phases["3f"], window)
            run_windows(sp, phases["3m"], window)
            for s, uses in ((0, -(-NT // 2)), (1, NT // 2)):
                sp.wait_ge(x1_stored[(s + phases["3f"]["g0"]) % 2], 16 * uses)
            run_windows(sp, phases["4f"], window)
            with sp.Fori(0, ET // 2) as i:
                for r in range(2):
                    edge_store(4, i * 2 + r + 3 * ET, i * 2 + r)
            def final_load(at, i=None):
                s = at % 2
                k = at // 2 if i is None else i + at // 2
                if i is None and at < 2:
                    pass
                else:
                    sp.wait_ge(f_ready, (at - 1) if i is None else i * 2 + at - 1)
                row = (FREE + at) * P if i is None else (i * 2 + (FREE + at)) * P
                sp.dma_start(row_in2[s][:, :], x1_rows[bass.ds(row, P), :]).then_inc(f_x1[s], 16)
            sp.wait_ge(row_ready, 4 * NT)
            sp.wait_ge(res_ready, FREE)
            final_load(0)
            final_load(1)
            with sp.Fori(0, (MIXED - 2) // 2) as i:
                final_load(2, i)
                final_load(3, i)
            for at in range(2 + (MIXED - 2) // 2 * 2, MIXED):
                final_load(at)
            for s in range(2):
                sp.wait_ge(res_stored[(s + phases["4f"]["g0"]) % 2], 16 * ((FREE + 1 - s) // 2))
                sp.wait_ge(f_stored[s], 16 * ((MIXED + 1 - s) // 2))

        @block.gpsimd
        def _(pool):
            def gate():
                pool.sem_inc(pool_gate, 1)

            def gather(to, idx, rows, done):
                pool.indirect_dma_start(out=to, out_offset=None, in_=rows,
                                        in_offset=bass.IndirectOffsetOnAxis(ap=idx[:, 0:1], axis=0)).then_inc(done, 16)

            def scatter(rows, idx, frm, done, limit=None):
                more = {} if limit is None else dict(bounds_check=limit, oob_is_err=False)
                pool.indirect_dma_start(out=rows, out_offset=bass.IndirectOffsetOnAxis(ap=idx[:, 0:1], axis=0),
                                        in_=frm, in_offset=None, **more).then_inc(done, 16)

            def norm_factors(t):
                s, k = t.slot4, ln_count(t)
                wait(pool, mean_var, k + 1)
                gate()
                nc.gpsimd.tensor_scalar(veps[s][:, :], mv[s][:, 1:2], EPS, None, ALU.add).then_inc(var_eps, 1)
                pool.wait_ge(var_eps, k + 1)
                nc.gpsimd.tensor_tensor(rstd[s][:, :], veps[s][:, :], half_neg[:, :], ALU.pow).then_inc(rstd_done, 1)
                pool.wait_ge(rstd_done, k + 1)
                gate()
                nc.gpsimd.tensor_scalar(nmr[s][:, :], mv[s][:, 0:1], rstd[s][:, 0:1], -1.0, ALU.mult, ALU.mult).then_inc(norm_ready, 1)

            def window1(t, has, side, i, r):
                if has(2):
                    norm_factors(t.plus(2))

            def load(t):
                layer, s, k = t.phase["layer"], t.slot, t.count(t.phase["g0"] - NT)
                wait(pool, in_used, k - 1)
                gate()
                rows_idx = perm_agg if t.phase["mixed"] else perm
                nc.gpsimd.tensor_copy(idx_a[s][:, :], rows_idx[:, bass.ds(t.pos, 1)])
                nc.gpsimd.tensor_copy(idx_b[s][:, :], perm_x[:, bass.ds(t.pos, 1)]).then_inc(idx_in_ready, 1)
                pool.wait_ge(idx_in_ready, k + 1)
                gate()
                gather(row_in[s][:, :], idx_a[s], table[layer - 1][0:ROWS if t.phase["mixed"] else NP, :], in_ready[s])
                if layer == 3:
                    gather(row_in2[s][:, :], idx_b[s], x, x_ready[s])

            def store(t):
                layer, s, k = t.phase["layer"], t.slot, t.count(t.phase["g0"] - NT)
                free4 = layer == 4 and not t.phase["mixed"]
                wait(pool, row_ready, t.g + 1)
                if free4:
                    wait(pool, res_ready, t.pos + 1)
                gate()
                nc.gpsimd.tensor_copy(idx_o[s][:, :], perm[:, bass.ds(t.pos, 1)]).then_inc(idx_out_ready, 1)
                pool.wait_ge(idx_out_ready, k + 1)
                gate()
                scatter(table[layer][0:NP, :], idx_o[s], row_out[s][:, :], row_stored[s])
                if free4:
                    scatter(out, idx_o[s], pre_out[s][:, :], res_stored[s], N - 1)

            def edge_rows(layer, h, slot, j):
                pool.wait_ge(edge_done, h + 1)
                gate()
                nc.gpsimd.tensor_copy(idx_s[slot][:, :], sorted_src[:, bass.ds(j, 1)])
                nc.gpsimd.tensor_copy(idx_d[slot][:, :], sorted_dst_i[:, bass.ds(j, 1)]).then_inc(eidx_ready, 1)
                pool.wait_ge(eidx_ready, h + 1)
                gate()
                gather(eg[slot][:, 0:D], idx_s[slot], table[layer][0:NP, :], e_rows[slot])
                gather(eh[slot][:, :], idx_d[slot], table[layer][0:NP, :], e_rows[slot])

            def window(t, has, side, i, r):
                layer = t.phase["layer"]
                if has(-1):
                    store(t.plus(-1))
                if side == "edges" and r % 2 == 0:
                    j = i * 2 + r // 2
                    edge_rows(layer - 1, j + t.phase["edge0"], (r // 2) % 2, j)
                if layer == 3 and has(2):
                    norm_factors(t.plus(2))
                if has(4):
                    load(t.plus(4))

            nc.gpsimd.iota(iota_c[:, :], [[1, P]], base=0, channel_multiplier=0, allow_small_or_imprecise_dtypes=True)
            nc.gpsimd.iota(iota_m1[:, :], [[1, P]], base=-1, channel_multiplier=0, allow_small_or_imprecise_dtypes=True)
            nc.gpsimd.iota(node_id[:, :], [[P, NT]], base=0, channel_multiplier=1, allow_small_or_imprecise_dtypes=True)
            nc.gpsimd.iota(edge_id[:, :], [[1, EC]], base=0, channel_multiplier=EC, allow_small_or_imprecise_dtypes=True)
            nc.gpsimd.iota(tile_ends[:, :], [[SLOTS, ET]], base=SLOTS, channel_multiplier=0, allow_small_or_imprecise_dtypes=True)
            nc.gpsimd.iota(row_iota, [[1, EP]], base=0, channel_multiplier=0, allow_small_or_imprecise_dtypes=True)
            nc.gpsimd.memset(zeros, 0.0)
            nc.gpsimd.memset(half_neg[:, :], -0.5)
            nc.gpsimd.memset(ident[:, :], 0.0)
            nc.gpsimd.memset(ones[:, :], 1.0).then_inc(consts_ready, 1)
            pool.wait_ge(consts_ready, 1)
            nc.gpsimd.affine_select(ident[:, :], ident[:, :], [[-1, P]], ALU.not_equal, 1.0, base=0, channel_multiplier=1)
            nc.gpsimd.affine_select(upper[:, :], ones[:, :], [[1, P]], ALU.is_gt, 0.0, base=0, channel_multiplier=-1).then_inc(consts_ready, 1)

            def all_max(layer):
                pool.wait_ge(w_max, layer)
                nc.gpsimd.partition_all_reduce(w_scale[:, layer - 1, 1:2], w_scale[:, layer - 1, 0:1], P, RMAX).then_inc(w_max_all, 1)

            all_max(1)
            run_windows(pool, phases["1"], window1, lambda: (all_max(2), all_max(3)))
            pool.wait_ge(perm_ready, 1)
            for s, v in all_slots(0, NT):
                pool.wait_ge(row1_stored[s], v)
            run_windows(pool, phases["2f"], window)
            all_max(4)
            pool.wait_ge(e_stored, 16 * (ET + 1))
            run_windows(pool, phases["2m"], window)
            for s, v in all_slots(NT, NT):
                pool.wait_ge(row_stored[s], v)
            run_windows(pool, phases["3f"], window)
            pool.wait_ge(e_stored, 16 * (2 * ET + 1))
            run_windows(pool, phases["3m"], window)
            for s, v in all_slots(NT, 2 * NT):
                pool.wait_ge(row_stored[s], v)
            run_windows(pool, phases["4f"], window)
            pool.wait_ge(e_stored, 16 * (3 * ET + 1))
            run_windows(pool, phases["4m"], window)
            for s, v in all_slots(NT, 3 * NT):
                pool.wait_ge(row_stored[s], v)
            with pool.Fori(0, ET // 2) as i:
                for r in range(2):
                    edge_rows(4, i * 2 + r + 3 * ET, r, i * 2 + r)
            pool.wait_ge(e_stored, 16 * (4 * ET + 1))

            def final_gather(at, i=None):
                s, n = at % 2, (at if i is None else i * 2 + at)
                if i is not None or at >= 2:
                    pool.wait_ge(f_ready, n - 1)
                gate()
                nc.gpsimd.tensor_copy(idx_a[s][:, :], perm_agg[:, bass.ds(n + FREE, 1)])
                nc.gpsimd.tensor_copy(idx_b[s][:, :], perm[:, bass.ds(n + FREE, 1)]).then_inc(f_idx, 1)
                pool.wait_ge(f_idx, n + 1)
                gate()
                gather(row_in[s][:, :], idx_a[s], table[4], f_in[s])

            def final_scatter(at, i=None):
                s, n = at % 2, (at if i is None else i * 2 + at)
                pool.wait_ge(f_ready, n + 1)
                gate()
                scatter(out, idx_b[s], pre_out[s][:, :], f_stored[s], N - 1)

            def final_turn(at, i=None):
                k = at // 2 if i is None else i + at // 2
                final_scatter(at - 2, i)
                pool.wait_ge(f_stored[at % 2], k * 16)
                gate()
                final_gather(at, i)

            final_gather(0)
            final_gather(1)
            with pool.Fori(0, (MIXED - 2) // 2) as i:
                final_turn(2, i)
                final_turn(3, i)
            done = 2 + (MIXED - 2) // 2 * 2
            for at in range(done, MIXED):
                final_turn(at)
            for at in range(MIXED - 2, MIXED):
                final_scatter(at)

        @block.scalar
        def _(act):
            def split_w(layer):
                act.wait_ge(w_scaled, layer)
                act.wait_ge(w_loaded, 16 * layer)
                if layer == 4:
                    act.wait_ge(h_ready, NT)
                nc.scalar.activation(w_hi[w_of[layer]][:, :, :], w_view(w_raw), ACT.Copy,
                                     scale=w_scale[:, layer - 1, 3:4]).then_inc(w_hi_ready, 1)

            def window(t, has, side, i, r):
                layer = t.phase["layer"]
                if has(-1):
                    b = t.plus(-1)
                    wait(act, h_ready, b.g + 1)
                    if layer == 1:
                        wait(act, row1_stored[b.slot], b.slot_uses * 16)
                    else:
                        wait(act, row_stored[b.slot], b.later_uses * 16)
                    if layer == 1:
                        scale = w_scale[:, 0, 2:3]
                    else:
                        act.wait_ge(grow_ready, b.count(b.phase["g0"] - NT) + 1)
                        scale = grow[b.slot4][:, 0:1]
                    nc.scalar.activation(pair(row_out[b.slot]), psum_pair(ps_h[b.slot]), ACT.Copy,
                                         scale=scale).then_inc(row_ready, 1)
                if has(1):
                    b = t.plus(1)
                    wait(act, z_turned, b.g + 1)
                    wait(act, h_ready, b.g - 1)
                    nc.scalar.activation(pair3(z_hi[b.slot]), psum_pair(ps_z), ACT.Copy).then_inc(z_hi_ready, 1)
                if side == "edges" and layer - 1 in GATS and r % 2 == 1:
                    weights(i * 2 + r // 2 + t.phase["edge0"])
                if has(2):
                    b = t.plus(2)
                    wait(act, z_turned, b.g - 1)
                    if layer in (1, 3):
                        act.wait_ge(norm_ready, ln_count(b) + 1)
                        if layer == 1:
                            wait(act, x_loaded[b.slot], (b.slot_uses + 1) * 16)
                        frm = row_in[b.slot] if layer == 1 else pre[b.slot]
                        nc.scalar.activation(z[b.slot][:, :], frm[:, :], ACT.Relu, bias=nmr[b.slot4][:, 0:1],
                                             scale=rstd[b.slot4][:, 0:1]).then_inc(z_ready, 1)
                    else:
                        act.wait_ge(shrink_ready, top_count(b) + 1)
                        nc.scalar.activation(z[b.slot][:, :], pre[b.slot][:, :], ACT.Relu,
                                             scale=shrink[b.slot4][:, 0:1]).then_inc(z_ready, 1)
                if side == "edges" and layer - 1 in GATS and r % 2 == 1:
                    weights_turn(i * 2 + r // 2 + t.phase["edge0"])
                    divide(i * 2 + r // 2 + t.phase["edge0"])

            def weights(h):
                act.wait_ge(negmax_ready, h + 1)
                nc.scalar.activation(e_wt[:, :], e_arg[:, :], ACT.Exp, bias=e_negmax[:, 0:1])
                nc.scalar.activation(e_self[:, :], lrelu[:, 1:2], ACT.Exp, bias=e_negmax[:, 0:1]).then_inc(weights_done, 1)

            def weights_turn(h):
                act.wait_ge(weights_turned, h + 1)
                nc.scalar.activation(e_wt_t[:, :], e_small, ACT.Copy).then_inc(weights_ready, 1)

            def divide(h):
                act.wait_ge(den_inv, h + 1)
                act.wait_ge(e_stored, (h + 1) * 16)
                nc.scalar.activation(e_out[:, :], e_tmp[:, :], ACT.Copy, scale=e_den[:, 1:2]).then_inc(e_out_ready, 1)

            split_w(1)
            run_windows(act, phases["1"], window, lambda: (split_w(2), split_w(3)))
            act.wait_ge(sqrt_in, 1)
            nc.scalar.activation(dinv[:, :], perm_f[:, 2, :], ACT.Sqrt).then_inc(sqrt_done, 1)
            run_windows(act, phases["2f"], window)
            split_w(4)
            for name in ("2m", "3f", "3m", "4f", "4m"):
                run_windows(act, phases[name], window)

        @block.tensor
        def _(pe):
            def turn(t):
                wait(pe, z_ready, t.g + 1)
                wait(pe, z_lo_ready, t.g)
                for c in range(KC):
                    last = nc.tensor.transpose(ps_z[:, c // 3, (c % 3) * P:(c % 3 + 1) * P],
                                               z[t.slot][:, c * P:(c + 1) * P], ident[:, :])
                last.then_inc(z_turned, 1)

            def products(t, side_step):
                layer, s = t.phase["layer"], t.slot
                wait(pe, z_lo_ready, t.g + 1)
                wait(pe, row_ready, t.g - 1)
                hi, lo = w_hi[w_of[layer]], w_lo[w_of[layer]]
                for c in range(KC):
                    for zp, wp in ((z_hi, hi), (z_hi, lo), (z_lo, hi)):
                        for a in range(2):
                            last = nc.tensor.matmul(ps_h[s][:, a, 0:HALF], zp[s][:, c, :], wp[:, c, a * HALF:(a + 1) * HALF],
                                                    start=(c == 0 and zp is z_hi and wp is hi),
                                                    stop=(c == KC - 1 and zp is z_lo))
                    if c == KC - 1:
                        last.then_inc(h_ready, 1)
                    elif c % 2 == 1:
                        side_step(c // 2)

            def rank_mm(c, slot):
                pe.wait_ge(onehot_ready, c + 1)
                o = onehot[:, slot, :]
                nc.tensor.matmul(sort_ps, o[:, 0:P], sorts[:, slot, :], start=False, stop=False, skip_group_check=True)
                nc.tensor.matmul(count_ps, o[:, P:2 * P], o[:, 2 * P:2 * P + NT], start=False, stop=False,
                                 skip_group_check=True).then_inc(onehot_used, 1)

            def order_mm(c, slot):
                pe.wait_ge(place_ready, c + 1)
                o = onehot[:, slot, :]
                nc.tensor.matmul(perm_ps, o[:, 0:P], o[:, P:P + 3 * NT], start=False, stop=False,
                                 skip_group_check=True).then_inc(place_used, 1)

            def window(t, has, side, i, r):
                layer = t.phase["layer"]
                if has(1):
                    turn(t.plus(1))

                def side_step(k):
                    if side == "order+mask" and k == 1:
                        j = i * 4 + r
                        pe.wait_ge(dst_diag, j + 1)
                        nc.tensor.matmul(mask_ps, ones[:, :], diag2[:, :, :].rearrange("p a q -> p (a q)"),
                                         start=True, stop=True, skip_group_check=True).then_inc(mask_mm, 1)
                    if side == "edges" and layer - 1 in GATS and r % 2 == 1:
                        h = i * 2 + r // 2 + t.phase["edge0"]
                        if k == 0:
                            pe.wait_ge(diag_ready, h + 1)
                            nc.tensor.matmul(e_small, ones[:, :], e_diag[:, :], start=True, stop=True,
                                             skip_group_check=True).then_inc(score_rows, 1)
                        if k == 1:
                            pe.wait_ge(weights_done, h + 1)
                            nc.tensor.transpose(e_small, e_wt[:, :], ident[:, :]).then_inc(weights_turned, 1)

                if has(0):
                    products(t, side_step)
                if side == "rank" and r % 2 == 1:
                    rank_mm(i * 2 + r // 2, r // 2)
                if side in ("order", "order+mask"):
                    base = 0 if side == "order+mask" else 5 * COLS
                    for c in SHARE[r]:
                        order_mm(i * COLS + (base + c), c)
                if side == "edges" and r % 2 == 1:
                    edge_mm(layer - 1, i * 2 + r // 2 + t.phase["edge0"], r // 2)

            def edge_mm(layer, h, slot):
                pe.wait_ge(carry_ready, h + 1)
                if layer in GATS:
                    pe.wait_ge(weights_ready, h + 1)
                nc.tensor.matmul(e_lo, e_wt_t[:, :], eg[slot][:, 0:SPLIT], start=True, stop=True, skip_group_check=True)
                nc.tensor.matmul(e_hi, e_wt_t[:, :], eg[slot][:, SPLIT:D + 1], start=True, stop=True,
                                 skip_group_check=True).then_inc(e_summed, 1)

            def clear():
                for a in range(2):
                    last = nc.tensor.matmul(ps_e[:, a, :], e_out[:, 0:P], zeros, start=True, stop=True, skip_group_check=True)
                return last

            def prefixes():
                pe.wait_ge(mid_in, 1)
                fc = flag_cnt[:, :, :].rearrange("p a n -> p (a n)")
                nc.tensor.matmul(ps_e[:, 0, 0:2 * NT], upper[:, :], fc, start=True, stop=True, skip_group_check=True)
                nc.tensor.matmul(ps_e[:, 1, 0:2 * NT], ones[:, :], fc, start=True, stop=True, skip_group_check=True).then_inc(mid_mm, 1)
                pe.wait_ge(mid_in, 2)
                clear().then_inc(mid_mm, 1)

            pe.wait_ge(consts_ready, 2)
            clear().then_inc(mid_mm, 1)
            pe.wait_ge(w_ready, 1)
            run_windows(pe, phases["1"], window, prefixes)
            pe.wait_ge(perm_ready, 1)
            clear().then_inc(e_summed, 1)
            pe.wait_ge(w_ready, 2)
            run_windows(pe, phases["2f"], window)
            run_windows(pe, phases["2m"], window)
            pe.wait_ge(w_ready, 3)
            run_windows(pe, phases["3f"], window)
            run_windows(pe, phases["3m"], window)
            pe.wait_ge(w_ready, 4)
            run_windows(pe, phases["4f"], window)
            run_windows(pe, phases["4m"], window)
            with pe.Fori(0, ET // 2) as i:
                for r in range(2):
                    edge_mm(4, i * 2 + r + 3 * ET, r)

        @block.vector
        def _(dve):
            steps = [0]

            def step(ins):
                steps[0] += 1
                ins.then_inc(setup_step, 1)
                dve.wait_ge(setup_step, steps[0])

            V = nc.vector

            def scale_w(layer):
                sc = w_scale[:, layer - 1, :]
                dve.wait_ge(w_loaded, 16 * layer)
                V.tensor_reduce(sc[:, 0:1], w_raw[:, :], AX_X, ALU.max, apply_absolute_value=True).then_inc(w_max, 1)
                dve.wait_ge(w_max_all, layer)
                step(V.tensor_scalar(sc[:, 1:2], sc[:, 1:2], TINY, None, ALU.max))
                step(V.tensor_scalar(sc[:, 2:3].bitcast(I32), sc[:, 1:2].bitcast(I32), EXPONENT, None, ALU.bitwise_and))
                V.reciprocal(sc[:, 3:4], sc[:, 2:3]).then_inc(w_scaled, 1)
                dve.wait_ge(w_hi_ready, layer)
                V.scalar_tensor_tensor(w_lo[w_of[layer]][:, :, :].rearrange("p c n -> p (c n)"), w_raw[:, :], sc[:, 3:4],
                                       w_hi[w_of[layer]][:, :, :].rearrange("p c n -> p (c n)"),
                                       ALU.mult, ALU.subtract).then_inc(w_ready, 1)

            def prepare(t):
                layer, s, s4 = t.phase["layer"], t.slot, t.slot4
                if layer == 1:
                    dve.wait_ge(x_loaded[s], (t.slot_uses + 1) * 16)
                else:
                    dve.wait_ge(in_ready[s], (t.later_uses + 1) * 16)
                if layer in (1, 3):
                    rows = row_in[s]
                    if layer == 3:
                        rows = pre[s]
                        dve.wait_ge(x_ready[s], (t.layer_uses + 1) * 16)
                        wait(dve, x1_stored[s], t.layer_uses * 16)
                        wait(dve, z_ready, t.g - 1)
                        k = t.count(t.phase["g0"] - NT)
                        V.tensor_tensor(pre[s][:, :], row_in[s][:, :], row_in2[s][:, :], ALU.add).then_inc(in_used, 1)
                        dve.wait_ge(in_used, k + 1)
                        V.tensor_tensor(pre[s][:, :], pre[s][:, :], bias_bc[2][:, :], ALU.add).then_inc(x1_ready, 1)
                        dve.wait_ge(x1_ready, t.pos + 1)
                    k = ln_count(t)
                    for a in range(2):
                        last = V.bn_stats(bn[s][:, 6 * a:6 * a + 6], rows[:, a * HALF:(a + 1) * HALF])
                    last.then_inc(stats_done, 1)
                    dve.wait_ge(stats_done, k + 1)
                    dve.sem_inc(dve_gate, 1)
                    V.bn_aggr(mv[s4][:, :], bn[s][:, :]).then_inc(mean_var, 1)
                    if layer == 3:
                        V.tensor_scalar(grow[s4][:, :], dinv_grow[:, 0, bass.ds(t.pos, 1)], 1.0, None, ALU.mult).then_inc(grow_ready, 1)
                    return
                k = t.count(t.phase["g0"] - NT)
                n = top_count(t)
                wait(dve, z_ready, t.g - 1)
                b = bias_bc[layer - 1]
                if layer == 4 and t.phase["mixed"]:
                    V.scalar_tensor_tensor(pre[s][:, :], row_in[s][:, :], dinv[:, bass.ds(t.pos, 1)], b[:, :],
                                           ALU.mult, ALU.add).then_inc(in_used, 1)
                    dve.wait_ge(in_used, k + 1)
                    V.tensor_reduce(top[s4][:, :], pre[s][:, :], AX_X, ALU.max).then_inc(top_found, 1)
                    dve.wait_ge(top_found, t.count(0) + 1)
                else:
                    dve.sem_inc(dve_gate, 1)
                    V.tensor_tensor_reduce(pre[s][:, :], row_in[s][:, :], b[:, :], 1.0, -FAR, ALU.add, ALU.max,
                                           top[s4][:, :]).then_inc(in_used, 1)
                    dve.wait_ge(in_used, k + 1)
                V.tensor_scalar(topc[s4][:, :], top[s4][:, :], TINY, None, ALU.max).then_inc(top_kept, 1)
                dve.wait_ge(top_kept, n + 1)
                V.reciprocal(shrink[s4][:, :], topc[s4][:, :]).then_inc(shrink_ready, 1)
                by = w_scale[:, 1, 2:3] if layer == 2 else dinv_grow[:, 1, bass.ds(t.pos, 1)]
                V.tensor_scalar(grow[s4][:, :], topc[s4][:, :], by, None, ALU.mult).then_inc(grow_ready, 1)

            def low_parts(t):
                wait(dve, z_hi_ready, t.g + 1)
                V.tensor_tensor(pair3(z_lo[t.slot]), psum_pair(ps_z), pair3(z_hi[t.slot]), ALU.subtract).then_inc(z_lo_ready, 1)

            def result(t):
                s = t.slot
                wait(dve, row_ready, t.g + 1)
                dve.wait_ge(x1_loaded[s], (t.layer_uses + 1) * 16)
                wait(dve, res_stored[s], t.layer_uses * 16)
                V.tensor_tensor(pre_out[s][:, :], row_out[s][:, :], row_in2[s][:, :], ALU.add).then_inc(x1_used, 1)
                dve.wait_ge(x1_used, t.pos + 1)
                V.tensor_tensor(pre_out[s][:, :], pre_out[s][:, :], bias_bc[4][:, :], ALU.add).then_inc(res_ready, 1)

            def carry(slot):
                V.tensor_copy(eg[slot][0:1, 0:SPLIT], ps_e[0:1, 0, 0:SPLIT])
                return V.tensor_copy(eg[slot][0:1, SPLIT:D + 1], ps_e[0:1, 1, 0:D + 1 - SPLIT])

            def edge_scores(layer, h, slot, per_slot):
                dve.wait_ge(e_rows[slot], (per_slot + 1) * 32)
                dve.wait_ge(e_summed, h + 1)
                carry(slot).then_inc(carry_ready, 1)
                dve.wait_ge(carry_ready, h + 1)
                for n, (rows, att) in enumerate(((eg[slot][:, 0:D], atts_bc), (eh[slot][:, :], atts_bc), (eh[slot][:, :], attd_bc))):
                    V.tensor_tensor_reduce(e_prod[:, :], rows, att[layer][:, :], 1.0, 0.0, ALU.mult, ALU.add,
                                           dots[:, n:n + 1]).then_inc(dots_done, 1)
                    dve.wait_ge(dots_done, h * 3 + (n + 1))
                V.tensor_scalar(score[:, :], dots[:, 0:2], dots[:, 2:3], None, ALU.add).then_inc(score_done, 1)
                dve.wait_ge(score_done, h + 1)
                V.scalar_tensor_tensor(lrelu[:, :], score[:, :], NEG_SLOPE, score[:, :], ALU.mult, ALU.max).then_inc(lrelu_done, 1)
                dve.wait_ge(lrelu_done, h + 1)
                V.tensor_copy(lrelu[0:1, 0:1], e_max[1 - slot][0:1, :]).then_inc(score_fixed, 1)
                dve.wait_ge(score_fixed, h + 1)
                V.tensor_scalar(e_diag[:, :], ident[:, :], lrelu[:, 0:1], None, ALU.mult).then_inc(diag_ready, 1)

            def edge_max(h, slot, j):
                dve.wait_ge(score_rows, h + 1)
                V.tensor_tensor(e_arg[:, :], e_small, far_mask[:, bass.ds(j, 1), :].rearrange("p a q -> p (a q)"), ALU.add).then_inc(arg_done, 1)
                dve.wait_ge(arg_done, h + 1)
                V.tensor_reduce(e_top[:, :], e_arg[:, :], AX_X, ALU.max).then_inc(top_done, 1)
                dve.wait_ge(top_done, h + 1)
                V.tensor_tensor(e_max[slot][:, :], e_top[:, :], lrelu[:, 1:2], ALU.max).then_inc(max_done, 1)
                dve.wait_ge(max_done, h + 1)
                V.tensor_scalar(e_negmax[:, :], e_max[slot][:, :], -1.0, None, ALU.mult).then_inc(negmax_ready, 1)

            def edge_sums(layer, h, slot):
                dve.wait_ge(e_summed, h + 2)
                if layer in GATS:
                    V.tensor_tensor(e_den[:, 0:1], e_den_ps, e_self[:, :], ALU.add).then_inc(den_done, 1)
                    dve.wait_ge(den_done, h + 1)
                    V.scalar_tensor_tensor(e_tmp[:, 0:SPLIT], eh[slot][:, 0:SPLIT], e_self[:, 0:1], e_lo, ALU.mult, ALU.add)
                    V.scalar_tensor_tensor(e_tmp[:, SPLIT:D], eh[slot][:, SPLIT:D], e_self[:, 0:1], ps_e[:, 1, 0:D - SPLIT],
                                           ALU.mult, ALU.add).then_inc(edge_done, 1)
                    V.reciprocal(e_den[:, 1:2], e_den[:, 0:1]).then_inc(den_inv, 1)
                else:
                    dve.wait_ge(e_stored, (h + 1) * 16)
                    V.tensor_tensor(e_out[:, 0:SPLIT], eh[slot][:, 0:SPLIT], e_lo, ALU.add)
                    V.tensor_tensor(e_out[:, SPLIT:D], eh[slot][:, SPLIT:D], ps_e[:, 1, 0:D - SPLIT], ALU.add).then_inc(edge_done, 1)

            def edge_plain(h, slot, per_slot, j):
                dve.wait_ge(e_rows[slot], (per_slot + 1) * 32)
                V.tensor_scalar(e_wt_t[:, :], same_t[:, bass.ds(j, 1), :].rearrange("p a q -> p (a q)"), 1.0, None, ALU.mult)
                carry(slot).then_inc(carry_ready, 1)

            def rank_column(c, slot):
                col = bass.ds(c, 1)
                dve.wait_ge(onehot_used, c + 1)
                k = c * 5
                V.scalar_tensor_tensor(row_cmp, row_iota, edge_id[:, col], row_dst, ALU.is_lt, ALU.subtract).then_inc(ranks_step, 1)
                dve.wait_ge(ranks_step, k + 1)
                V.tensor_scalar(row_cmp, row_cmp, e_f[:, 2, col], 0.0, ALU.is_gt, ALU.add, accum_out=e_rank[:, 0, 0:1]).then_inc(ranks_step, 1)
                dve.wait_ge(ranks_step, k + 2)
                V.tensor_scalar(e_rank[:, 3, :], tile_ends[:, :], e_rank[:, 0, 0:1], 0.0, ALU.is_le, ALU.add,
                                accum_out=e_rank[:, 1, 0:1]).then_inc(ranks_step, 1)
                dve.wait_ge(ranks_step, k + 3)
                V.tensor_scalar(e_rank[:, 2, 0:1], e_rank[:, 1, 0:1], -float(SLOTS), e_rank[:, 0, 0:1], ALU.mult, ALU.add).then_inc(ranks_step, 1)
                dve.wait_ge(ranks_step, k + 4)
                o = onehot[:, slot, :]
                V.tensor_scalar(o[:, 0:P], iota_m1[:, :], e_rank[:, 2, 0:1], None, ALU.is_equal).then_inc(ranks_step, 1)
                V.tensor_scalar(sorts[:, slot, 0:ET], iota_c[:, 0:ET], e_rank[:, 1, 0:1], e_f[:, 0, col], ALU.is_equal, ALU.mult)
                V.tensor_scalar(sorts[:, slot, ET:2 * ET], iota_c[:, 0:ET], e_rank[:, 1, 0:1], e_f[:, 1, col], ALU.is_equal, ALU.mult)
                V.tensor_scalar(o[:, P:2 * P], iota_c[:, :], e_f[:, 3, col], None, ALU.is_equal)
                V.tensor_scalar(o[:, 2 * P:2 * P + NT], iota_c[:, 0:NT], e_f[:, 4, col], None, ALU.is_equal)
                dve.wait_ge(ranks_step, k + 5)
                V.tensor_copy(o[:, 0:1], o[:, P - 1:P]).then_inc(onehot_ready, 1)

            def node_order():
                f, cnt = flag_cnt[:, 0, :], flag_cnt[:, 1, :]
                dve.wait_ge(onehot_used, 2 + EC)
                V.tensor_copy(sorted_src[:, :], sort_ps[:, 0:ET])
                V.tensor_copy(sorted_dst_i[:, :], sort_ps[:, ET:2 * ET])
                V.tensor_copy(dst_in[:, :], sort_ps[:, ET:2 * ET])
                step(V.tensor_copy(dst_of[:, :], sort_ps[:, ET:2 * ET]))
                V.tensor_copy(dst_in[0:1, 1:ET], dst_of[0:1, 0:ET - 1])
                V.memset(dst_in[0:1, 0:1], -1.0)
                step(V.tensor_copy(cnt, count_ps))
                step(V.tensor_scalar(f, cnt, 0.0, None, ALU.is_gt))
                dve.sem_inc(mid_in, 1)
                dve.wait_ge(mid_mm, 2)
                below, total = (ps_e[:, a, 0:2 * NT].rearrange("p (a n) -> p a n", a=2) for a in range(2))
                V.tensor_copy(scan[2][:, :, :], total)
                step(V.tensor_copy(scan[0][:, :, :], total))
                at, d = 0, 1
                while d < NT:
                    V.tensor_copy(scan[1 - at][:, :, 0:d], scan[at][:, :, 0:d])
                    step(V.tensor_tensor(scan[1 - at][:, :, d:NT], scan[at][:, :, d:NT], scan[at][:, :, 0:NT - d], ALU.add))
                    at, d = 1 - at, 2 * d
                incl, before = scan[at], scan[1 - at]
                step(V.tensor_tensor(before[:, :, :], incl[:, :, :], scan[2][:, :, :], ALU.subtract))
                step(V.tensor_tensor(before[:, :, :], before[:, :, :], below, ALU.add))
                dve.sem_inc(mid_in, 1)
                A, C = before[:, 0, :], before[:, 1, :]
                w0, w1, w2, w3 = (work[:, k, :] for k in range(4))
                step(V.tensor_scalar(w3[:, 0:1], incl[:, 0, NT - 1:NT], -1.0, float(NP), ALU.mult, ALU.add))
                step(V.scalar_tensor_tensor(w0, A, 2.0, node_id[:, :], ALU.mult, ALU.subtract))
                step(V.tensor_scalar(w0, w0, w3[:, 0:1], None, ALU.add))
                step(V.tensor_tensor(w0, w0, f, ALU.mult))
                step(V.tensor_tensor(w1, node_id[:, :], A, ALU.subtract))
                step(V.tensor_tensor(w0, w0, w1, ALU.add))
                step(V.tensor_copy(place_i[:, 0, :], w0))
                V.tensor_scalar(place_i[:, 1, :], place_i[:, 0, :], P - 1, None, ALU.bitwise_and)
                step(V.tensor_scalar(place_i[:, 2, :], place_i[:, 0, :], 7, None, ALU.arith_shift_right))
                step(V.memset(place[:, :, :], -1.0))
                V.tensor_copy(place[:, 0, 0:NT], place_i[:, 1, :])
                V.tensor_copy(place[:, 1, 0:NT], place_i[:, 2, :])
                step(V.scalar_tensor_tensor(w1, C, -1.0, cnt, ALU.add, ALU.add))
                step(V.tensor_copy(w2, w1))
                for j in range(ET):
                    step(V.scalar_tensor_tensor(w2, w1, float(SLOTS * (j + 1)), w2, ALU.is_ge, ALU.add))
                step(V.tensor_scalar(w2, w2, float(AGG + 1), float(ROWS - 1), ALU.add, ALU.min))
                step(V.tensor_tensor(w2, w2, node_id[:, :], ALU.subtract))
                step(V.tensor_tensor(w2, w2, f, ALU.mult))
                step(V.tensor_tensor(place[:, 2, 0:NT], w2, node_id[:, :], ALU.add))
                dve.wait_ge(mid_mm, 3)

            def order_column(c, slot, at):
                dve.wait_ge(place_used, c + 1)
                o, col = onehot[:, slot, :], bass.ds(c, 1)
                V.tensor_scalar(o[:, 0:P], iota_c[:, :], place[:, 0, col], None, ALU.is_equal)
                V.tensor_scalar(o[:, P:P + NT], iota_c[:, 0:NT], place[:, 1, col], node_id_pad[:, col], ALU.is_equal, ALU.mult)
                V.tensor_scalar(o[:, P + NT:P + 2 * NT], iota_c[:, 0:NT], place[:, 1, col], place[:, 2, col], ALU.is_equal, ALU.mult)
                V.tensor_scalar(o[:, P + 2 * NT:P + 3 * NT], iota_c[:, 0:NT], place[:, 1, col], cnt_pad[:, col],
                                ALU.is_equal, ALU.mult).then_inc(place_ready, 1)

            def mask_diag(j):
                col = bass.ds(j, 1)
                V.tensor_scalar(diag2[:, 0, :], ident[:, :], dst_in[:, col], None, ALU.mult)
                V.tensor_scalar(diag2[:, 1, :], ident[:, :], dst_of[:, col], None, ALU.mult).then_inc(dst_diag, 1)

            def mask_make(j):
                col = bass.ds(j, 1)
                far = far_mask[:, col, :].rearrange("p a q -> p (a q)")
                dve.wait_ge(mask_mm, j + 1)
                V.tensor_scalar(e_arg[:, :], mask_ps[:, 0:P], dst_of[:, col], FAR, ALU.is_equal, ALU.mult).then_inc(mask_part, 1)
                V.tensor_scalar(same_t[:, col, :].rearrange("p a q -> p (a q)"), mask_ps[:, P:2 * P], dst_in[:, col], None, ALU.is_equal)
                dve.wait_ge(mask_part, j + 1)
                V.tensor_scalar(far, e_arg[:, :], -FAR, None, ALU.add).then_inc(mask_ready, 1)

            def window(t, has, side, i, r):
                layer = t.phase["layer"]
                edges = side == "edges"
                gat = edges and layer - 1 in GATS
                h = i * 2 + r // 2 + t.phase["edge0"] if edges else None
                if layer == 4 and not t.phase["mixed"] and has(-1):
                    result(t.plus(-1))
                if has(1):
                    low_parts(t.plus(1))
                if gat and r % 2 == 1:
                    edge_max(h, r // 2, i * 2 + r // 2)
                if side == "order+mask":
                    mask_diag(i * 4 + r)
                if has(2):
                    prepare(t.plus(2))
                if gat and r % 2 == 0:
                    edge_scores(layer - 1, h, r // 2, i + t.phase["edge0"] // 2)
                if edges and not gat and r % 2 == 0:
                    edge_plain(h, r // 2, i + t.phase["edge0"] // 2, i * 2 + r // 2)
                if side == "rank" and r % 2 == 0:
                    rank_column(i * 2 + r // 2, r // 2)
                if side in ("order", "order+mask"):
                    base = 0 if side == "order+mask" else 5 * COLS
                    for c in SHARE[r]:
                        order_column(i * COLS + (base + c), c, c)
                if side == "order+mask":
                    mask_make(i * 4 + r)
                if edges and r % 2 == 1:
                    edge_sums(layer - 1, h, r // 2)

            def mid():
                node_order()
                step(V.tensor_copy(node_id_pad[:, 0:NT], node_id[:, :]))
                step(V.tensor_copy(cnt_pad[:, 0:NT], flag_cnt[:, 1, :]))
                scale_w(2)
                scale_w(3)

            V.memset(e_src[:, :], PAD)
            V.memset(e_dst[:, :], PAD)
            V.memset(node_id_pad[:, :], 0.0)
            V.memset(cnt_pad[:, :], 0.0)
            for s in range(2):
                V.memset(e_max[s][:, :], 0.0)
                V.memset(eg[s][:, D:D + 1], 1.0)
            V.memset(row_cmp[:, E:EP].bitcast(I32), PAD).then_inc(graph_padded, 1)
            dve.sem_inc(edge_done, 2)
            dve.sem_inc(onehot_used, 2)
            dve.sem_inc(place_used, COLS)
            dve.wait_ge(consts_ready, 2)
            scale_w(1)
            dve.wait_ge(graph_loaded, 48)
            V.tensor_scalar(row_dst, row_cmp.bitcast(I32), 2.0, None, ALU.mult)
            V.tensor_copy(e_f[:, 0, :], e_src[:, :])
            V.tensor_copy(e_f[:, 1, :], e_dst[:, :])
            V.tensor_scalar(e_f[:, 2, :], e_dst[:, :], -2.0, None, ALU.mult)
            V.tensor_scalar(e_part[:, 0, :], e_dst[:, :], P - 1, None, ALU.bitwise_and)
            step(V.tensor_scalar(e_part[:, 1, :], e_dst[:, :], 7, None, ALU.arith_shift_right))
            V.tensor_copy(e_f[:, 3, :], e_part[:, 0, :])
            step(V.tensor_copy(e_f[:, 4, :], e_part[:, 1, :]))
            dve.wait_ge(mid_mm, 1)
            run_windows(dve, phases["1"], window, mid)
            dve.wait_ge(place_used, COLS + COLS * (-(-NT // COLS)))
            step(V.tensor_copy(perm_f[:, :, :], perm_ps.rearrange("p (a n) -> p a n", a=3)))
            V.tensor_copy(perm_agg[:, :], perm_f[:, 1, :])
            step(V.tensor_copy(perm[:, :], perm_f[:, 0, :]))
            step(V.tensor_scalar(perm_f[:, 0, :], perm_f[:, 0, :], float(N - 1), None, ALU.min))
            step(V.tensor_copy(perm_x[:, :], perm_f[:, 0, :]))
            V.tensor_scalar(perm_f[:, 2, :], perm_f[:, 2, :], 1.0, None, ALU.add).then_inc(sqrt_in, 1)
            dve.sem_inc(perm_ready, 1)
            dve.wait_ge(sqrt_done, 1)
            step(V.reciprocal(dinv[:, :], dinv[:, :]))
            step(V.tensor_scalar(dinv_grow[:, 0, :], dinv[:, :], w_scale[:, 2, 2:3], None, ALU.mult))
            dve.wait_ge(params_loaded, 16 * 8)
            run_windows(dve, phases["2f"], window)
            scale_w(4)
            step(V.tensor_scalar(dinv_grow[:, 1, :], dinv[:, :], w_scale[:, 3, 2:3], None, ALU.mult))
            for name in ("2m", "3f", "3m"):
                run_windows(dve, phases[name], window)
            for s, uses in ((0, -(-NT // 2)), (1, NT // 2)):
                dve.wait_ge(x1_stored[(s + phases["3f"]["g0"]) % 2], 16 * uses)
            for name in ("4f", "4m"):
                run_windows(dve, phases[name], window)
            with dve.Fori(0, ET // 2) as i:
                for r in range(2):
                    edge_plain(i * 2 + r + 3 * ET, r, i + 3 * ET // 2, i * 2 + r)
                    edge_sums(4, i * 2 + r + 3 * ET, r)

            def final(at, i=None):
                s, n, k = at % 2, (at if i is None else i * 2 + at), (at // 2 if i is None else i + at // 2)
                dve.wait_ge(f_in[s], k * 16 + 16)
                dve.wait_ge(f_x1[s], k * 16 + 16)
                if i is not None or at >= 2:
                    dve.wait_ge(f_stored[s], k * 16)
                V.scalar_tensor_tensor(pre_out[s][:, :], row_in[s][:, :], dinv[:, bass.ds(n + FREE, 1)], row_in2[s][:, :],
                                       ALU.mult, ALU.add).then_inc(f_sum, 1)
                dve.wait_ge(f_sum, n + 1)
                V.tensor_tensor(pre_out[s][:, :], pre_out[s][:, :], bias_bc[4][:, :], ALU.add).then_inc(f_ready, 1)

            for s in range(2):
                dve.wait_ge(res_stored[(s + phases["4f"]["g0"]) % 2], 16 * ((FREE + 1 - s) // 2))
            final(0)
            final(1)
            with dve.Fori(0, (MIXED - 2) // 2) as i:
                final(2, i)
                final(3, i)
            for at in range(2 + (MIXED - 2) // 2 * 2, MIXED):
                final(at)


_INS = ["x", "src", "dst", "L0_gnn_W1", "L0_gnn_att_src1", "L0_gnn_att_dst1", "L0_gnn_b1", "L0_gnn_W2", "L0_gnn_att_src2",
        "L0_gnn_att_dst2", "L0_gnn_b2", "L1_gnn_W1", "L1_gnn_b1", "L1_gnn_W2", "L1_gnn_b2"]


def kernel(**inputs):
    import numpy as _np
    import concourse.bacc as _bacc
    from concourse import mybir as _mybir
    from concourse.bass_utils import run_bass_kernel_spmd as _run

    nc = _bacc.Bacc("TRN2", target_bir_lowering=False, num_devices=1)
    arrays, a = {}, {}
    for name in _INS:
        v = _np.ascontiguousarray(inputs[name])
        arrays[f"in_{name}"] = v
        a[name] = nc.dram_tensor(f"in_{name}", v.shape, _mybir.dt.from_np(v.dtype), kind="ExternalInput").ap()
    out = nc.dram_tensor("out", inputs["x"].shape, _mybir.dt.float32, kind="ExternalOutput").ap()
    build(nc, a["x"], a["src"], a["dst"],
          {1: a["L0_gnn_W1"], 2: a["L0_gnn_W2"], 3: a["L1_gnn_W1"], 4: a["L1_gnn_W2"]},
          {1: a["L0_gnn_att_src1"], 2: a["L0_gnn_att_src2"]}, {1: a["L0_gnn_att_dst1"], 2: a["L0_gnn_att_dst2"]},
          {1: a["L0_gnn_b1"], 2: a["L0_gnn_b2"], 3: a["L1_gnn_b1"], 4: a["L1_gnn_b2"]}, out)
    r = _run(nc, [arrays], core_ids=[0])
    return r.results[0]["out"]
```

```python
from contextlib import ExitStack

import concourse.bass as bass
from concourse import mybir

P = 128
F32 = mybir.dt.float32
F16 = mybir.dt.float16
I32 = mybir.dt.int32
ALU = mybir.AluOpType
ACT = mybir.ActivationFunctionType
AX_X = mybir.AxisListType.X
RMAX = bass.bass_isa.ReduceOp.max

NEG_SLOPE = 0.2
EPS = 1e-5
TINY = 1e-30
FAR = 1e30
EXPONENT = 0x7F800000
UP = 2.0 ** 12
UP_LN = 2.0 ** 10


class Tile:

    def __init__(self, phase, at, i=None, step=4):
        self.phase, self.at, self.i, self.step = phase, at, i, step

    def plus(self, k):
        phase, at = self.phase, self.at + k
        if self.i is None and at >= phase["n"] and phase["next"]:
            phase, at = phase["next"], at - phase["n"]
        elif self.i is None and at < 0 and phase["before"]:
            phase, at = phase["before"], at + phase["before"]["n"]
        return Tile(phase, at, self.i, self.step)

    def exists(self, k):
        return self.i is not None or 0 <= self.plus(k).at < self.plus(k).phase["n"]

    def count(self, before, every=1):
        c = (before + self.at) // every
        return c if self.i is None else self.i * (self.step // every) + c

    @property
    def g(self):
        return self.count(self.phase["g0"])

    @property
    def slot(self):
        return (self.phase["g0"] + self.at) % 2

    @property
    def slot4(self):
        return (self.phase["g0"] + self.at) % 4

    @property
    def slot_uses(self):
        return self.count(self.phase["g0"], 2)

    @property
    def phase_uses(self):
        return self.count(0, 2)

    @property
    def pos(self):
        return self.count(self.phase["first"])

    @property
    def layer_uses(self):
        return (self.phase["first"] + self.at) // 2 if self.i is None else self.i * (self.step // 2) + (self.phase["first"] + self.at) // 2


def wait(e, sem, value):
    if not isinstance(value, int) or value > 0:
        e.wait_ge(sem, value)


def run_windows(e, phase, window, hooks=None):
    n = phase["n"]
    t = 0 if phase["before"] else -4
    starts = {start: (turns, side) for start, turns, side in phase["loops"]}
    while t < n + (0 if phase["next"] else 1):
        if hooks and t in hooks:
            hooks[t]()
        if t in starts:
            turns, side = starts[t]
            peel = 1 if side == "edges" else 0
            for i in range(peel):
                for r in range(4):
                    window(Tile(phase, t + r), side, i, r)
            with e.Fori(peel, turns - peel) as i:
                for r in range(4):
                    window(Tile(phase, t + r, i), side, i, r)
            for i in range(turns - peel, turns):
                for r in range(4):
                    window(Tile(phase, t + 4 * i + r), side, i, r)
            t += 4 * turns
            if peel:
                window(Tile(phase, t), side, turns, 0)
                t += 1
            continue
        window(Tile(phase, t), None, None, 0)
        t += 1


def edge_tile(i, c, tiles):
    j = i * 2 + c
    return j, c % 2, not isinstance(i, int) or 0 <= j < tiles


def build(nc, x, src, dst, w, att_src, att_dst, bias, out):
    N, D = x.shape
    E = src.shape[0]
    KC = D // P
    HALF = D // 2
    NT = -(-N // P)
    NP = NT * P
    LAST = N - (NT - 1) * P
    EC = -(-E // P)
    ER = -(-E // EC)
    assert ER * EC == E and EC * P == -(-E // P) * P
    EP = EC * P
    SLOTS = P - 1
    ET = EC
    assert ET * SLOTS >= E and (ET - 1) * SLOTS < E
    PAD = NP - 1
    assert PAD >= N
    FREE = (NP - E - 1) // P
    MIXED = NT - FREE
    AGG = NP
    ROWS = NP + ET * P
    COLS = 10
    SHARE = [(0, 1, 2), (3, 4, 5), (6, 7), (8, 9)]

    phases = {}
    g = 0
    for layer in (1, 2, 3, 4):
        if layer == 1:
            phases["1"] = dict(layer=1, n=NT, g0=0, first=0, mixed=False,
                               loops=[(2, ET // 2, "rank"), (42, 5, "order+mask"), (62, 3, "order")])
            g = NT
            continue
        phases[f"{layer}f"] = dict(layer=layer, n=FREE, g0=g, first=0, mixed=False,
                                   loops=[(2, ET // 2, "edges"), (3 + 2 * ET, (FREE - 7 - 2 * ET) // 4, None)])
        phases[f"{layer}m"] = dict(layer=layer, n=MIXED, g0=g + FREE, first=FREE, mixed=True,
                                   loops=[(1, (MIXED - 5) // 4, None)])
        g += NT
    for name, ph in phases.items():
        ph["name"] = name
        ph["before"] = ph["next"] = None
        ph["edge0"] = {1: 0, 2: 0, 3: ET, 4: 2 * ET}[ph["layer"]]

    chain = [phases[k] for k in ("2f", "2m", "3f", "3m", "4f", "4m")]
    for one, two in zip(chain, chain[1:]):
        one["next"], two["before"] = two, one

    def all_slots(first, tiles):
        return [(first % 2, 16 * -(-tiles // 2)), (1 - first % 2, 16 * (tiles // 2))]

    table = {n: nc.dram_tensor(f"rows_{n}", [ROWS, D], F32).ap() for n in (1, 2, 3, 4)}
    pos_of = nc.dram_tensor("pos_of", [NP, 1], I32).ap()
    x1_rows = nc.dram_tensor("x1_rows", [NP, D + 1], F32).ap()

    ctx = ExitStack()
    with ctx:
        def sb(name, shape, dt=F32):
            return ctx.enter_context(nc.sbuf_tensor(name, shape, dt))

        def sem(name):
            return ctx.enter_context(nc.semaphore(name))

        w_hi = [sb(f"w_hi{s}", [P, KC, D], F16) for s in range(3)]
        w_lo = [sb(f"w_lo{s}", [P, KC, D], F16) for s in range(3)]
        w_raw = sb("w_raw", [P, KC * D])
        w_of = {1: 0, 2: 1, 3: 2, 4: 0}
        w_scale = sb("w_scale", [P, 4, 4])
        row_in = [sb(f"row_in{s}", [P, D]) for s in range(2)]
        row_in2_x1 = [sb(f"row_in2_x1{s}", [P, D + 1]) for s in range(2)]
        pre_x1 = [sb(f"pre_x1{s}", [P, D + 1]) for s in range(2)]
        row_in2, pre = ([b[:, 0:D] for b in bufs] for bufs in (row_in2_x1, pre_x1))
        z = [sb(f"z{s}", [P, D]) for s in range(2)]
        z_hi = [sb(f"z_hi{s}", [P, KC, P], F16) for s in range(2)]
        z_lo = [sb(f"z_lo{s}", [P, KC, P], F16) for s in range(2)]
        row_out = [sb(f"row_out{s}", [P, D]) for s in range(2)]
        pre_out = [sb(f"pre_out{s}", [P, D]) for s in range(2)]
        bn = [sb(f"bn{s}", [P, 12]) for s in range(2)]
        mv = [sb(f"mv{s}", [P, 2]) for s in range(4)]
        veps = [sb(f"veps{s}", [P, 1]) for s in range(4)]
        rstd = [sb(f"rstd{s}", [P, 1]) for s in range(4)]
        nmr = [sb(f"nmr{s}", [P, 1]) for s in range(4)]
        top = [sb(f"top{s}", [P, 1]) for s in range(4)]
        topc = [sb(f"topc{s}", [P, 1]) for s in range(4)]
        shrink = [sb(f"shrink{s}", [P, 1]) for s in range(4)]
        grow = [sb(f"grow{s}", [P, 1]) for s in range(4)]
        idx_a = [sb(f"idx_a{s}", [P, 1], I32) for s in range(2)]
        idx_b = [sb(f"idx_b{s}", [P, 1], I32) for s in range(2)]
        idx_o = [sb(f"idx_o{s}", [P, 1], I32) for s in range(2)]
        bias_bc = {n: sb(f"bias_bc{n}", [P, D]) for n in (1, 2, 3, 4)}
        atts_bc = {n: sb(f"atts_bc{n}", [P, D]) for n in (1, 2)}
        attd_bc = {n: sb(f"attd_bc{n}", [P, D]) for n in (1, 2)}
        ident = sb("ident", [P, P])
        ones = sb("ones", [P, P])
        upper = sb("upper", [P, P])
        half_neg = sb("half_neg", [P, 1])
        iota_c = sb("iota_c", [P, P])
        iota_m1 = sb("iota_m1", [P, P])
        node_id = sb("node_id", [P, NT])
        node_id_pad = sb("node_id_pad", [P, COLS * (-(-NT // COLS))])
        cnt_pad = sb("cnt_pad", [P, COLS * (-(-NT // COLS))])
        edge_id = sb("edge_id", [P, EC])
        tile_ends = sb("tile_ends", [P, ET])
        rank_mem = sb("rank_mem", [P, 3, EP])
        row_dst, row_cmp, row_iota = (rank_mem[:, k, :] for k in range(3))
        masks = rank_mem[:, 0:2, :].rearrange("p a (t q) -> p a t q", q=P)
        far_mask, same_t = masks[:, 0], masks[:, 1]
        e_src = sb("e_src", [P, EC], I32)
        e_dst = sb("e_dst", [P, EC], I32)
        e_part = sb("e_part", [P, 2, EC], I32)
        e_f = sb("e_f", [P, 5, EC])
        e_rank = sb("e_rank", [P, 4, EC])
        edge_mem = sb("edge_mem", [P, 6 * D + 2])
        onehot = edge_mem[:, 0:COLS * 3 * P].rearrange("p (k c) -> p k c", k=COLS)
        sorts = sb("sorts", [P, 2, 2 * ET])
        diag2 = sb("diag2", [P, 2, P])
        sorted_src = sb("sorted_src", [P, ET], I32)
        sorted_dst_i = sb("sorted_dst_i", [P, ET], I32)
        dst_of = sb("dst_of", [P, ET])
        dst_in = sb("dst_in", [P, ET])
        flag_cnt = sb("flag_cnt", [P, 2, NT])
        scan = [sb(f"scan{s}", [P, 2, NT]) for s in range(3)]
        work = sb("work", [P, 4, NT])
        place = sb("place", [P, 3, COLS * (-(-NT // COLS))])
        place_i = sb("place_i", [P, 3, NT], I32)
        perm_f = sb("perm_f", [P, 3, NT])
        perm = sb("perm", [P, NT], I32)
        perm_out = sb("perm_out", [P, NT], I32)
        perm_x = sb("perm_x", [P, NT], I32)
        perm_agg = sb("perm_agg", [P, NT], I32)
        pos_agg = sb("pos_agg", [P, NT], I32)
        dinv = sb("dinv", [P, NT])
        dinv_grow = sb("dinv_grow", [P, 2, NT])
        eg = [edge_mem[:, s * (D + 1):(s + 1) * (D + 1)] for s in range(2)]
        eh = [edge_mem[:, 2 + (2 + s) * D:2 + (3 + s) * D] for s in range(2)]
        pos_src = sb("pos_src", [P, ET], I32)
        pos_dst = sb("pos_dst", [P, ET], I32)
        pos_got = sb("pos_got", [P, 2], I32)
        idx_s = [sb(f"idx_s{s}", [P, 1], I32) for s in range(2)]
        idx_d = [sb(f"idx_d{s}", [P, 1], I32) for s in range(2)]
        e_tmp = edge_mem[:, 2 + 4 * D:2 + 5 * D]
        e_prod = edge_mem[:, 2 + 5 * D:2 + 6 * D]
        e_out = sb("e_out", [P, D])
        zeros = e_out[:, 0:512]
        dots = sb("dots", [P, 3])
        score = sb("score", [P, 2])
        lrelu = sb("lrelu", [P, 2])
        e_max = [sb(f"e_max{s}", [P, 1]) for s in range(2)]
        e_top = sb("e_top", [P, 1])
        e_negmax = sb("e_negmax", [P, 1])
        e_self = sb("e_self", [P, 1])
        e_den = sb("e_den", [P, 2])
        pos_t = row_iota[:, 0:P].bitcast(I32)
        e_diag, e_arg, e_wt, e_wt_t = (row_iota[:, (k + 1) * P:(k + 2) * P] for k in range(4))

        ps_z = ctx.enter_context(nc.psum_tensor("ps_z", [P, 2, 512], F32))
        ps_h = [ctx.enter_context(nc.psum_tensor(f"ps_h{s}", [P, 2, 512], F32)) for s in range(2)]
        ps_e = ctx.enter_context(nc.psum_tensor("ps_e", [P, 2, 512], F32))
        SPLIT = HALF + 1
        e_lo, e_hi = ps_e[:, 0, 0:SPLIT], ps_e[:, 1, 0:D + 1 - SPLIT]
        e_den_ps = ps_e[:, 1, D - SPLIT:D + 1 - SPLIT]
        e_small = ps_e[:, 1, HALF:HALF + P]
        sort_ps = ps_e[:, 0, 0:2 * ET]
        count_ps = ps_e[:, 1, 0:NT]
        perm_ps = ps_e[:, 0, 0:3 * NT]
        mask_ps = ps_e[:, 1, 0:2 * P]

        consts_ready = sem("consts_ready")
        params_loaded = sem("params_loaded")
        graph_loaded = sem("graph_loaded")
        graph_padded = sem("graph_padded")
        setup_step = sem("setup_step")
        w_loaded = sem("w_loaded")
        w_max = sem("w_max")
        w_max_all = sem("w_max_all")
        w_scaled = sem("w_scaled")
        w_hi_ready = sem("w_hi_ready")
        w_ready = sem("w_ready")
        x_loaded = [sem(f"x_loaded{s}") for s in range(2)]
        in_ready = {name: [sem(f"in_ready{name}_{s}") for s in range(2)] for name in phases if name != "1"}
        in_used = sem("in_used")
        x_ready = [sem(f"x_ready{s}") for s in range(2)]
        x1_loaded = [sem(f"x1_loaded{s}") for s in range(2)]
        x1_ready = sem("x1_ready")
        x1_stored = [sem(f"x1_stored{s}") for s in range(2)]
        x1_used = sem("x1_used")
        stats_done = sem("stats_done")
        mean_var = sem("mean_var")
        var_eps = sem("var_eps")
        rstd_done = sem("rstd_done")
        norm_ready = sem("norm_ready")
        top_found = sem("top_found")
        top_kept = sem("top_kept")
        shrink_ready = sem("shrink_ready")
        grow_ready = sem("grow_ready")
        z_ready = sem("z_ready")
        z_turned = sem("z_turned")
        z_hi_ready = sem("z_hi_ready")
        z_lo_ready = sem("z_lo_ready")
        h_ready = sem("h_ready")
        row_ready = sem("row_ready")
        row_stored = [sem(f"row_stored{s}") for s in range(2)]
        res_ready = sem("res_ready")
        res_stored = [sem(f"res_stored{s}") for s in range(2)]
        idx_in_ready = sem("idx_in_ready")
        idx_out_ready = sem("idx_out_ready")
        pool_gate = sem("pool_gate")
        dve_gate = sem("dve_gate")
        ranks_step = sem("ranks_step")
        onehot_ready = sem("onehot_ready")
        onehot_used = sem("onehot_used")
        mid_mm = sem("mid_mm")
        pos_ready = sem("pos_ready")
        pos_stored = sem("pos_stored")
        pos_idx = sem("pos_idx")
        pos_kept = sem("pos_kept")
        pos_found = [sem(f"pos_found{k}") for k in range(2)]
        mid_in = sem("mid_in")
        place_ready = sem("place_ready")
        place_used = sem("place_used")
        dst_diag = sem("dst_diag")
        mask_mm = sem("mask_mm")
        mask_part = sem("mask_part")
        mask_ready = sem("mask_ready")
        perm_ready = sem("perm_ready")
        sqrt_in = sem("sqrt_in")
        sqrt_done = sem("sqrt_done")
        eidx_ready = sem("eidx_ready")
        e_rows = [sem(f"e_rows{s}") for s in range(2)]
        dots_done = sem("dots_done")
        score_done = sem("score_done")
        lrelu_done = sem("lrelu_done")
        score_fixed = sem("score_fixed")
        diag_ready = sem("diag_ready")
        score_rows = sem("score_rows")
        arg_done = sem("arg_done")
        top_done = sem("top_done")
        max_done = sem("max_done")
        negmax_ready = sem("negmax_ready")
        weights_done = sem("weights_done")
        weights_turned = sem("weights_turned")
        weights_ready = sem("weights_ready")
        plain_ready = sem("plain_ready")
        carry_ready = sem("carry_ready")
        e_summed = sem("e_summed")
        den_done = sem("den_done")
        den_inv = sem("den_inv")
        edge_done = sem("edge_done")
        e_out_ready = sem("e_out_ready")
        e_stored = sem("e_stored")
        last_x1 = [sem(f"last_x1{s}") for s in range(2)]
        x1_idx = sem("x1_idx")
        f_idx = sem("f_idx")
        f_sum = sem("f_sum")
        f_ready = sem("f_ready")
        f_stored = [sem(f"f_stored{s}") for s in range(2)]

        block = ctx.enter_context(nc.Block())
        GATS = (1, 2)

        def w_view(t):
            return t[:, :].rearrange("p (c n) -> p c n", c=KC)

        def psum_pair(t):
            return t[:, :, 0:HALF]

        def pair(t):
            return t[:, :].rearrange("p (a n) -> p a n", a=2)

        def pair3(t):
            return t[:, :, :].rearrange("p (a c) n -> p a (c n)", a=2)

        def ln_count(t):
            return t.count(t.phase["g0"] if t.phase["layer"] == 1 else t.phase["g0"] - NT)

        def top_count(t):
            return t.count(t.phase["g0"] - NT if t.phase["layer"] == 2 else t.phase["g0"] - 2 * NT)

        @block.sync
        def _(sp):
            def load_w(layer):
                if layer > 1:
                    sp.wait_ge(w_ready, layer - 1)
                sp.dma_start(w_view(w_raw), w[layer].rearrange("(c p) n -> p c n", p=P)).then_inc(w_loaded, 16)

            def row_of(v):
                return bass.AP(v.tensor, v.offset, [[0, P], [1, v.shape[0]]])

            def load_x(t):
                if t.i is None and t.at == NT - 1:
                    wait(sp, z_ready, t.g - 1)
                    sp.dma_start(row_in[t.slot][0:LAST, :], x[(NT - 1) * P:N, :]).then_inc(x_loaded[t.slot], 16)
                    return
                wait(sp, z_ready, t.g - 1)
                at = t.count(0) * P
                sp.dma_start(row_in[t.slot][:, :], x[bass.ds(at, P), :]).then_inc(x_loaded[t.slot], 16)

            def store(t):
                wait(sp, row_ready, t.g + 1)
                sp.dma_start(table[t.phase["layer"]][bass.ds(t.pos * P, P), :], row_out[t.slot][:, :]).then_inc(row_stored[t.slot], 16)

            def window1(t, side, i, r):
                if t.exists(-1):
                    store(t.plus(-1))
                if t.exists(4):
                    load_x(t.plus(4))

            def load(t):
                s, ago = t.slot, t.count(t.phase["g0"] - NT)
                sp.wait_ge(in_used, ago - 1)
                sp.wait_ge(row_stored[1 - s], (t.count(t.phase["g0"] - NT, 2) + 1) * 16)
                sp.dma_start(row_in[s][:, :], table[t.phase["layer"] - 1][bass.ds(t.pos * P, P), :]).then_inc(
                    in_ready[t.phase["name"]][s], 16)

            def edge_store(layer, h, j):
                if layer in GATS:
                    sp.wait_ge(e_out_ready, h + 1)
                else:
                    sp.wait_ge(edge_done, h + 3)
                sp.dma_start(table[layer][bass.ds(j * P + AGG, P), :], e_out[:, :]).then_inc(e_stored, 16)

            def window(t, side, i, r):
                if t.exists(4) and t.plus(4).phase["name"] in ("3f", "4f"):
                    load(t.plus(4))
                if t.exists(-1):
                    store(t.plus(-1))
                b = t.plus(1)
                if t.exists(1) and b.phase["layer"] == 4:
                    if b.i is None and b.pos < 2:
                        sp.wait_ge(in_used, b.g - NT - 1)
                    else:
                        wait(sp, x1_used, b.pos - 1)
                    sp.wait_ge(x1_stored[1 - b.slot], (b.layer_uses + 1) * 16)
                    sp.dma_start(row_in2[b.slot][:, :], x1_rows[bass.ds(b.pos * P, P), 0:D]).then_inc(x1_loaded[b.slot], 16)
                b = t.plus(3)
                if t.exists(3) and b.phase["layer"] == 3:
                    wait(sp, x1_ready, b.pos + 1)
                    sp.dma_start(x1_rows[bass.ds(b.pos * P, P), :], pre_x1[b.slot][:, :]).then_inc(x1_stored[b.slot], 16)
                if side == "edges":
                    gat = t.phase["layer"] - 1 in GATS
                    j, _, there = edge_tile(i, r // 2 - (1 if gat else 0), ET)
                    if there and r % 2 == (0 if gat else 1):
                        edge_store(t.phase["layer"] - 1, j + t.phase["edge0"], j)

            load_w(1)
            sp.wait_ge(graph_padded, 1)
            sp.dma_start(e_src[0:ER, :], src.rearrange("(p c) -> p c", c=EC)).then_inc(graph_loaded, 16)
            sp.dma_start(e_dst[0:ER, :], dst.rearrange("(p c) -> p c", c=EC)).then_inc(graph_loaded, 16)
            sp.dma_start(row_cmp[:, 0:E].bitcast(I32), row_of(dst)).then_inc(graph_loaded, 16)
            sp.sem_inc(e_stored, 16)
            def load_params():
                for n in (1, 2, 3, 4):
                    sp.dma_start(bias_bc[n][:, :], row_of(bias[n])).then_inc(params_loaded, 16)
                for n in GATS:
                    sp.dma_start(atts_bc[n][:, :], row_of(att_src[n])).then_inc(params_loaded, 16)
                    sp.dma_start(attd_bc[n][:, :], row_of(att_dst[n])).then_inc(params_loaded, 16)

            def store_positions():
                sp.wait_ge(pos_ready, 1)
                sp.dma_start(pos_of.rearrange("(h l) a -> h (l a)", l=P), pos_t[0:NT, :]).then_inc(pos_stored, 16)

            run_windows(sp, phases["1"], window1, {-2: lambda: load_w(2), 42: store_positions, 74: load_params, 76: lambda: load_w(3)})
            for phase in chain:
                run_windows(sp, phase, window, {56: lambda: load_w(4)} if phase["name"] == "2f" else None)
            for s, v in all_slots(phases["4f"]["g0"], NT):
                sp.wait_ge(res_stored[s], v)
            for s, v in all_slots(0, ET):
                sp.wait_ge(f_stored[s], v)

        @block.gpsimd
        def _(pool):
            def gate():
                pool.sem_inc(pool_gate, 1)

            def gather(to, idx, rows, done):
                pool.indirect_dma_start(out=to, out_offset=None, in_=rows,
                                        in_offset=bass.IndirectOffsetOnAxis(ap=idx[:, 0:1], axis=0)).then_inc(done, 16)

            def scatter(rows, idx, frm, done, limit=None):
                more = {} if limit is None else dict(bounds_check=limit, oob_is_err=False)
                pool.indirect_dma_start(out=rows, out_offset=bass.IndirectOffsetOnAxis(ap=idx[:, 0:1], axis=0),
                                        in_=frm, in_offset=None, **more).then_inc(done, 16)

            def norm_factors(t):
                s, k = t.slot4, ln_count(t)
                wait(pool, mean_var, k + 1)
                gate()
                nc.gpsimd.tensor_scalar(veps[s][:, :], mv[s][:, 1:2], EPS, UP_LN ** -2, ALU.add, ALU.mult).then_inc(var_eps, 1)
                pool.wait_ge(var_eps, k + 1)
                nc.gpsimd.tensor_tensor(rstd[s][:, :], veps[s][:, :], half_neg[:, :], ALU.pow).then_inc(rstd_done, 1)
                pool.wait_ge(rstd_done, k + 1)
                gate()
                nc.gpsimd.tensor_scalar(nmr[s][:, :], mv[s][:, 0:1], rstd[s][:, 0:1], -1.0, ALU.mult, ALU.mult).then_inc(norm_ready, 1)

            def window1(t, side, i, r):
                if side == "order+mask":
                    find_positions(i * 4 + r)
                if t.exists(3):
                    norm_factors(t.plus(3))
                if side == "order+mask":
                    keep_positions(i * 4 + r)

            def find_positions(j):
                nc.gpsimd.tensor_copy(idx_s[0][:, :], sorted_src[:, bass.ds(j, 1)])
                nc.gpsimd.tensor_copy(idx_d[0][:, :], sorted_dst_i[:, bass.ds(j, 1)]).then_inc(pos_idx, 1)
                pool.wait_ge(pos_idx, j + 1)
                gate()
                gather(pos_got[:, 0:1], idx_s[0], pos_of, pos_found[0])
                gather(pos_got[:, 1:2], idx_d[0], pos_of, pos_found[1])

            def keep_positions(j):
                for k, to in enumerate((pos_src, pos_dst)):
                    pool.wait_ge(pos_found[k], j * 16 + 16)
                    gate()
                    nc.gpsimd.tensor_copy(to[:, bass.ds(j, 1)], pos_got[:, k:k + 1]).then_inc(pos_kept, 1)

            def load(t):
                phase, s, k = t.phase, t.slot, t.count(t.phase["g0"] - NT)
                if t.i is None and t.at == 0 and phase["mixed"]:
                    pool.wait_ge(e_stored, 16 * (phase["edge0"] + ET + 1))
                wait(pool, in_used, k - 1)
                gate()
                rows_idx = (perm_agg if phase["layer"] == 2 else pos_agg) if phase["mixed"] else perm
                if phase["name"] != "3f":
                    last = nc.gpsimd.tensor_copy(idx_a[s][:, :], rows_idx[:, bass.ds(t.pos, 1)])
                if phase["layer"] == 3:
                    last = nc.gpsimd.tensor_copy(idx_b[s][:, :], perm_x[:, bass.ds(t.pos, 1)])
                last.then_inc(idx_in_ready, 1)
                pool.wait_ge(idx_in_ready, (k if phase["layer"] < 4 else t.count(t.phase["g0"] - NT - FREE)) + 1)
                gate()
                if phase["name"] != "3f":
                    gather(row_in[s][:, :], idx_a[s], table[phase["layer"] - 1][0:ROWS if phase["mixed"] else NP, :],
                           in_ready[phase["name"]][s])
                if phase["layer"] == 3:
                    gather(row_in2[s][:, :], idx_b[s], x, x_ready[s])

            def store_result(t):
                s = t.slot
                pool.wait_ge(res_ready, t.pos + 1)
                gate()
                nc.gpsimd.tensor_copy(idx_o[s][:, :], perm_out[:, bass.ds(t.pos, 1)]).then_inc(idx_out_ready, 1)
                pool.wait_ge(idx_out_ready, t.pos + 1)
                gate()
                scatter(out, idx_o[s], pre_out[s][:, :], res_stored[s], N - 1)

            def edge_rows(layer, h, slot, j):
                of_src, of_dst = (sorted_src, sorted_dst_i) if layer == 1 else (pos_src, pos_dst)
                pool.wait_ge(edge_done, h + 1)
                gate()
                nc.gpsimd.tensor_copy(idx_s[slot][:, :], of_src[:, bass.ds(j, 1)])
                nc.gpsimd.tensor_copy(idx_d[slot][:, :], of_dst[:, bass.ds(j, 1)]).then_inc(eidx_ready, 1)
                pool.wait_ge(eidx_ready, h + 1)
                gate()
                gather(eg[slot][:, 0:D], idx_s[slot], table[layer][0:NP, :], e_rows[slot])
                gather(eh[slot][:, :], idx_d[slot], table[layer][0:NP, :], e_rows[slot])

            def window(t, side, i, r):
                if t.exists(4) and t.plus(4).phase["name"] != "4f":
                    load(t.plus(4))
                b = t.plus(-1)
                if t.exists(-1) and b.phase["layer"] == 4:
                    store_result(b)
                if side == "edges" and r % 2 == 1:
                    j, slot, there = edge_tile(i, r // 2 + 1, ET)
                    if there:
                        edge_rows(t.phase["layer"] - 1, j + t.phase["edge0"], slot, j)
                if t.exists(3) and t.plus(3).phase["layer"] == 3:
                    norm_factors(t.plus(3))

            nc.gpsimd.iota(iota_c[:, :], [[1, P]], base=0, channel_multiplier=0, allow_small_or_imprecise_dtypes=True)
            nc.gpsimd.iota(iota_m1[:, :], [[1, P]], base=-1, channel_multiplier=0, allow_small_or_imprecise_dtypes=True)
            nc.gpsimd.iota(node_id[:, :], [[P, NT]], base=0, channel_multiplier=1, allow_small_or_imprecise_dtypes=True)
            nc.gpsimd.iota(edge_id[:, :], [[1, EC]], base=0, channel_multiplier=EC, allow_small_or_imprecise_dtypes=True)
            nc.gpsimd.iota(tile_ends[:, :], [[SLOTS, ET]], base=SLOTS, channel_multiplier=0, allow_small_or_imprecise_dtypes=True)
            nc.gpsimd.iota(row_iota, [[1, EP]], base=0, channel_multiplier=0, allow_small_or_imprecise_dtypes=True)
            nc.gpsimd.memset(zeros, 0.0)
            nc.gpsimd.memset(half_neg[:, :], -0.5)
            nc.gpsimd.memset(ident[:, :], 0.0)
            nc.gpsimd.memset(ones[:, :], 1.0).then_inc(consts_ready, 1)
            pool.wait_ge(consts_ready, 1)
            nc.gpsimd.affine_select(ident[:, :], ident[:, :], [[-1, P]], ALU.not_equal, 1.0, base=0, channel_multiplier=1)
            nc.gpsimd.affine_select(upper[:, :], ones[:, :], [[1, P]], ALU.is_gt, 0.0, base=0, channel_multiplier=-1).then_inc(consts_ready, 1)

            def all_max(layer):
                pool.wait_ge(w_max, layer)
                nc.gpsimd.partition_all_reduce(w_scale[:, layer - 1, 1:2], w_scale[:, layer - 1, 0:1], P, RMAX).then_inc(w_max_all, 1)

            all_max(1)
            run_windows(pool, phases["1"], window1,
                        {2: lambda: all_max(2), 42: lambda: pool.wait_ge(pos_stored, 16)})
            pool.wait_ge(sqrt_in, 1)
            nc.gpsimd.tensor_tensor(dinv[:, :], perm_f[:, 2, :], work[:, 2, :], ALU.pow).then_inc(sqrt_done, 1)
            pool.wait_ge(perm_ready, 1)
            pool.wait_ge(pos_kept, 2 * ET)
            for phase in chain:
                def rows_complete(layer=phase["layer"] - 1):
                    for s, v in all_slots(0, layer * NT):
                        pool.wait_ge(row_stored[s], v)

                def first_edges(phase=phase, rows_complete=rows_complete):
                    rows_complete()
                    edge_rows(phase["layer"] - 1, phase["edge0"], 0, 0)

                if phase["name"] == "2f":
                    rows_complete()
                hooks = {} if phase["mixed"] else {1: first_edges}
                if phase["name"] == "2f":
                    hooks[0] = lambda: all_max(3)
                if phase["name"] == "2m":
                    hooks[0] = lambda: all_max(4)
                run_windows(pool, phase, window, hooks)
            for s, v in all_slots(0, 4 * NT):
                pool.wait_ge(row_stored[s], v)
            for s, v in all_slots(phases["3f"]["g0"], NT):
                pool.wait_ge(x1_stored[s], v)

            def last_rows(at, i=None):
                j = at if i is None else i * 2 + at
                edge_rows(4, j + 3 * ET, at % 2, j)

            def last_x1_rows(at, i=None):
                s, j = at % 2, at if i is None else i * 2 + at
                if i is not None or at >= 2:
                    pool.wait_ge(f_sum, j - 1)
                gate()
                nc.gpsimd.tensor_copy(idx_a[s][:, :], pos_dst[:, bass.ds(j, 1)]).then_inc(x1_idx, 1)
                pool.wait_ge(x1_idx, j + 1)
                gate()
                gather(row_in2_x1[s][:, :], idx_a[s], x1_rows, last_x1[s])

            def last_store(at, i=None):
                s, j = at % 2, at if i is None else i * 2 + at
                pool.wait_ge(f_ready, j + 1)
                if i is None and at == 0:
                    for slot, v in all_slots(phases["4f"]["g0"], NT):
                        pool.wait_ge(res_stored[slot], v)
                else:
                    pool.wait_ge(f_stored[1 - s], ((at + 1) // 2 if i is None else i + (at + 1) // 2) * 16)
                gate()
                nc.gpsimd.tensor_copy(idx_o[s][:, :], sorted_dst_i[:, bass.ds(j, 1)]).then_inc(f_idx, 1)
                pool.wait_ge(f_idx, j + 1)
                gate()
                scatter(out, idx_o[s], pre_out[s][:, :], f_stored[s], N - 1)

            for at in range(2):
                last_rows(at)
                last_x1_rows(at)

            def last_turn(at, i=None):
                last_rows(at + 2, i)
                last_store(at, i)
                last_x1_rows(at + 2, i)

            last_turn(0)
            with pool.Fori(0, (ET - 4) // 2) as i:
                last_turn(1, i)
                last_turn(2, i)
            last_turn(ET - 3)
            last_store(ET - 2)
            last_store(ET - 1)

        @block.scalar
        def _(act):
            def split_w(layer):
                act.wait_ge(w_scaled, layer)
                act.wait_ge(w_loaded, 16 * layer)
                if layer == 4:
                    act.wait_ge(h_ready, NT)
                nc.scalar.activation(w_hi[w_of[layer]][:, :, :], w_view(w_raw), ACT.Copy,
                                     scale=w_scale[:, layer - 1, 3:4]).then_inc(w_hi_ready, 1)

            def window(t, side, i, r):
                edges, gat, e0 = side == "edges", t.phase["layer"] - 1 in GATS, t.phase["edge0"]
                if edges:
                    j, slot, there = edge_tile(i, r // 2, ET)
                    before, _, was_there = edge_tile(i, r // 2 - 1, ET)
                if edges and gat and r % 2 == 0 and was_there:
                    weights_turn(before + e0)
                if t.exists(-1):
                    b = t.plus(-1)
                    wait(act, h_ready, b.g + 1)
                    wait(act, row_stored[b.slot], b.slot_uses * 16)
                    if b.phase["layer"] == 1:
                        scale = w_scale[:, 0, 0:1]
                    else:
                        act.wait_ge(grow_ready, b.count(b.phase["g0"] - NT) + 1)
                        scale = grow[b.slot4][:, 0:1]
                    if b.phase["layer"] == 4:
                        wait(act, x1_used, b.pos - 1)
                    nc.scalar.activation(pair(row_out[b.slot]), psum_pair(ps_h[b.slot]), ACT.Copy,
                                         scale=scale).then_inc(row_ready, 1)
                if t.exists(1):
                    b = t.plus(1)
                    wait(act, z_turned, b.g + 1)
                    wait(act, h_ready, b.g - 1)
                    nc.scalar.activation(pair3(z_hi[b.slot]), psum_pair(ps_z), ACT.Copy).then_inc(z_hi_ready, 1)
                if t.exists(2):
                    b = t.plus(2)
                    layer = b.phase["layer"]
                    wait(act, z_turned, b.g - 1)
                    if layer in (1, 3):
                        act.wait_ge(norm_ready, ln_count(b) + 1)
                        if layer == 1:
                            wait(act, x_loaded[b.slot], (b.slot_uses + 1) * 16)
                        frm = row_in[b.slot] if layer == 1 else pre[b.slot]
                        nc.scalar.activation(z[b.slot][:, :], frm[:, :], ACT.Relu, bias=nmr[b.slot4][:, 0:1],
                                             scale=rstd[b.slot4][:, 0:1]).then_inc(z_ready, 1)
                    else:
                        act.wait_ge(shrink_ready, top_count(b) + 1)
                        nc.scalar.activation(z[b.slot][:, :], pre[b.slot][:, :], ACT.Relu,
                                             scale=shrink[b.slot4][:, 0:1]).then_inc(z_ready, 1)
                if edges and r % 2 == 0 and there:
                    carry(t.phase["layer"] - 1, j + e0, slot, i + e0 // 2)
                if edges and gat and r % 2 == 0 and was_there:
                    divide(before + e0)
                if edges and gat and r % 2 == 1 and there:
                    weights(j + e0)

            def carry(layer, h, slot, per_slot):
                act.wait_ge(e_rows[slot], (per_slot + 1) * 32)
                act.wait_ge(edge_done, h + 2)
                if layer in GATS:
                    act.wait_ge(dots_done, h * 3 + 1)
                nc.scalar.activation(eg[slot][0:1, 0:SPLIT], ps_e[0:1, 0, 0:SPLIT], ACT.Copy)
                nc.scalar.activation(eg[slot][0:1, SPLIT:D + 1], ps_e[0:1, 1, 0:D + 1 - SPLIT], ACT.Copy).then_inc(carry_ready, 1)

            def weights(h):
                act.wait_ge(negmax_ready, h + 1)
                nc.scalar.activation(e_wt[:, :], e_arg[:, :], ACT.Exp, bias=e_negmax[:, 0:1])
                nc.scalar.activation(e_self[:, :], lrelu[:, 1:2], ACT.Exp, bias=e_negmax[:, 0:1]).then_inc(weights_done, 1)

            def weights_turn(h):
                act.wait_ge(weights_turned, h + 1)
                nc.scalar.activation(e_wt_t[:, :], e_small, ACT.Copy).then_inc(weights_ready, 1)

            def divide(h):
                act.wait_ge(den_inv, h + 1)
                act.wait_ge(e_stored, (h + 1) * 16)
                nc.scalar.activation(e_out[:, :], e_tmp[:, :], ACT.Copy, scale=e_den[:, 1:2]).then_inc(e_out_ready, 1)

            split_w(1)
            run_windows(act, phases["1"], window, {62: lambda: split_w(2)})
            for phase in chain:
                run_windows(act, phase, window, {"2f": {43: lambda: split_w(3)}, "2m": {13: lambda: split_w(4)}}.get(phase["name"]))
            with act.Fori(0, ET // 2) as i:
                for r in range(2):
                    carry(4, i * 2 + r + 3 * ET, r, i + 3 * ET // 2)

        @block.tensor
        def _(pe):
            def turn(t):
                wait(pe, z_ready, t.g + 1)
                wait(pe, z_lo_ready, t.g)
                for c in range(KC):
                    last = nc.tensor.transpose(ps_z[:, c // 3, (c % 3) * P:(c % 3 + 1) * P],
                                               z[t.slot][:, c * P:(c + 1) * P], ident[:, :])
                last.then_inc(z_turned, 1)

            def products(t, side_step):
                layer, s = t.phase["layer"], t.slot
                wait(pe, z_lo_ready, t.g + 1)
                wait(pe, row_ready, t.g - 1)
                hi, lo = w_hi[w_of[layer]], w_lo[w_of[layer]]
                for c in range(KC):
                    for zp, wp in ((z_hi, hi), (z_hi, lo), (z_lo, hi)):
                        for a in range(2):
                            last = nc.tensor.matmul(ps_h[s][:, a, 0:HALF], zp[s][:, c, :], wp[:, c, a * HALF:(a + 1) * HALF],
                                                    start=(c == 0 and zp is z_hi and wp is hi),
                                                    stop=(c == KC - 1 and zp is z_lo))
                    if c == KC - 1:
                        last.then_inc(h_ready, 1)
                    elif c % 2 == 1:
                        side_step(c // 2)

            def rank_mm(c, slot):
                pe.wait_ge(onehot_ready, c + 1)
                o = onehot[:, slot, :]
                nc.tensor.matmul(sort_ps, o[:, 0:P], sorts[:, slot, :], start=False, stop=False, skip_group_check=True)
                nc.tensor.matmul(count_ps, o[:, P:2 * P], o[:, 2 * P:2 * P + NT], start=False, stop=False,
                                 skip_group_check=True).then_inc(onehot_used, 1)

            def order_mm(c, slot):
                pe.wait_ge(place_ready, c + 1)
                o = onehot[:, slot, :]
                nc.tensor.matmul(perm_ps, o[:, 0:P], o[:, P:P + 3 * NT], start=False, stop=False,
                                 skip_group_check=True).then_inc(place_used, 1)

            def window(t, side, i, r):
                layer = t.phase["layer"]
                if t.exists(1):
                    turn(t.plus(1))
                if t.i is None and t.at == 0 and layer > 1:
                    pe.wait_ge(w_ready, layer)

                def side_step(k):
                    if side == "order+mask" and k == 1:
                        j = i * 4 + r
                        pe.wait_ge(dst_diag, j + 1)
                        nc.tensor.matmul(mask_ps, ones[:, :], diag2[:, :, :].rearrange("p a q -> p (a q)"),
                                         start=True, stop=True, skip_group_check=True).then_inc(mask_mm, 1)
                    if side == "edges" and k == 0:
                        e0 = t.phase["edge0"]
                        j, slot, there = edge_tile(i, r // 2, ET)
                        before, slot_before, was_there = edge_tile(i, r // 2 - 1, ET)
                        if layer - 1 not in GATS:
                            if r % 2 == 1 and there:
                                edge_mm(layer - 1, j + e0, slot)
                        elif r % 2 == 0 and was_there:
                            edge_mm(layer - 1, before + e0, slot_before)
                        elif r % 2 == 1 and there:
                            h = j + e0
                            pe.wait_ge(diag_ready, h + 1)
                            pe.wait_ge(carry_ready, h + 1)
                            wait(pe, edge_done, h + 2)
                            nc.tensor.matmul(e_small, ones[:, :], e_diag[:, :], start=True, stop=True,
                                             skip_group_check=True).then_inc(score_rows, 1)

                if t.exists(0):
                    products(t, side_step)
                if side == "rank" and r % 2 == 1:
                    rank_mm(i * 2 + r // 2, r // 2)
                if side in ("order", "order+mask"):
                    base = 0 if side == "order+mask" else 5 * COLS
                    for c in SHARE[r]:
                        order_mm(i * COLS + (base + c), c)
                if side == "edges" and layer - 1 in GATS and r % 2 == 1:
                    pe.wait_ge(weights_done, i * 2 + (r // 2 + t.phase["edge0"] + 1))
                    nc.tensor.transpose(e_small, e_wt[:, :], ident[:, :]).then_inc(weights_turned, 1)

            def edge_mm(layer, h, slot):
                pe.wait_ge(carry_ready, h + 1)
                if layer in GATS:
                    pe.wait_ge(weights_ready, h + 1)
                else:
                    pe.wait_ge(plain_ready, h - (2 * ET - 1))
                    pe.wait_ge(edge_done, h + 2)
                nc.tensor.matmul(e_lo, e_wt_t[:, :], eg[slot][:, 0:SPLIT], start=True, stop=True, skip_group_check=True)
                nc.tensor.matmul(e_hi, e_wt_t[:, :], eg[slot][:, SPLIT:D + 1], start=True, stop=True,
                                 skip_group_check=True).then_inc(e_summed, 1)

            def clear():
                for a in range(2):
                    last = nc.tensor.matmul(ps_e[:, a, :], e_out[:, 0:P], zeros, start=True, stop=True, skip_group_check=True)
                return last

            def prefixes():
                pe.wait_ge(mid_in, 1)
                fc = flag_cnt[:, :, :].rearrange("p a n -> p (a n)")
                nc.tensor.matmul(ps_e[:, 0, 0:2 * NT], upper[:, :], fc, start=True, stop=True, skip_group_check=True)
                nc.tensor.matmul(ps_e[:, 1, 0:2 * NT], ones[:, :], fc, start=True, stop=True, skip_group_check=True).then_inc(mid_mm, 1)
                pe.wait_ge(mid_in, 2)
                nc.tensor.transpose(ps_e[0:NT, 0, 0:P], work[:, 0, :], ident[:, :]).then_inc(mid_mm, 1)
                pe.wait_ge(mid_in, 3)
                clear().then_inc(mid_mm, 1)

            pe.wait_ge(consts_ready, 2)
            clear().then_inc(mid_mm, 1)
            pe.wait_ge(w_ready, 1)
            run_windows(pe, phases["1"], window, {42: prefixes})
            pe.wait_ge(perm_ready, 1)
            clear().then_inc(e_summed, 1)
            for phase in chain:
                run_windows(pe, phase, window)
            with pe.Fori(0, ET // 2) as i:
                for r in range(2):
                    edge_mm(4, i * 2 + r + 3 * ET, r)

        @block.vector
        def _(dve):
            steps = [0]

            def step(ins):
                steps[0] += 1
                ins.then_inc(setup_step, 1)
                dve.wait_ge(setup_step, steps[0])

            V = nc.vector

            def max_w(layer):
                dve.wait_ge(w_loaded, 16 * layer)
                V.tensor_reduce(w_scale[:, layer - 1, 0:1], w_raw[:, :], AX_X, ALU.max, apply_absolute_value=True).then_inc(w_max, 1)

            def scale_w(layer):
                sc = w_scale[:, layer - 1, :]
                dve.wait_ge(w_max_all, layer)
                step(V.tensor_scalar(sc[:, 1:2], sc[:, 1:2], TINY, None, ALU.max))
                step(V.tensor_scalar(sc[:, 2:3].bitcast(I32), sc[:, 1:2].bitcast(I32), EXPONENT, None, ALU.bitwise_and))
                step(V.tensor_scalar(sc[:, 2:3], sc[:, 2:3], 1.0 / UP, None, ALU.mult))
                if layer == 1:
                    V.tensor_scalar(sc[:, 0:1], sc[:, 2:3], 1.0 / UP_LN, None, ALU.mult)
                V.reciprocal(sc[:, 3:4], sc[:, 2:3]).then_inc(w_scaled, 1)

            def low_w(layer):
                dve.wait_ge(w_hi_ready, layer)
                V.scalar_tensor_tensor(w_lo[w_of[layer]][:, :, :].rearrange("p c n -> p (c n)"), w_raw[:, :],
                                       w_scale[:, layer - 1, 3:4],
                                       w_hi[w_of[layer]][:, :, :].rearrange("p c n -> p (c n)"),
                                       ALU.mult, ALU.subtract).then_inc(w_ready, 1)

            def prepare(t):
                layer, s, s4 = t.phase["layer"], t.slot, t.slot4
                if layer == 1:
                    dve.wait_ge(x_loaded[s], (t.slot_uses + 1) * 16)
                else:
                    dve.wait_ge(in_ready[t.phase["name"]][s], (t.phase_uses + 1) * 16)
                if layer in (1, 3):
                    rows = row_in[s]
                    if layer == 3:
                        rows = pre[s]
                        dve.wait_ge(x_ready[s], (t.layer_uses + 1) * 16)
                        wait(dve, x1_stored[s], t.layer_uses * 16)
                        wait(dve, z_ready, t.g - 1)
                        k = t.count(t.phase["g0"] - NT)
                        V.tensor_scalar(pre_x1[s][:, D:D + 1], dinv[:, bass.ds(t.pos, 1)], 1.0, None, ALU.mult)
                        V.tensor_tensor(pre[s][:, :], row_in[s][:, :], row_in2[s][:, :], ALU.add).then_inc(in_used, 1)
                        dve.wait_ge(in_used, k + 1)
                        V.tensor_tensor(pre[s][:, :], pre[s][:, :], bias_bc[2][:, :], ALU.add).then_inc(x1_ready, 1)
                        dve.wait_ge(x1_ready, t.pos + 1)
                    k = ln_count(t)
                    for a in range(2):
                        last = V.bn_stats(bn[s][:, 6 * a:6 * a + 6], rows[:, a * HALF:(a + 1) * HALF])
                    last.then_inc(stats_done, 1)
                    dve.wait_ge(stats_done, k + 1)
                    dve.sem_inc(dve_gate, 1)
                    V.bn_aggr(mv[s4][:, :], bn[s][:, :]).then_inc(mean_var, 1)
                    if layer == 3:
                        V.tensor_scalar(grow[s4][:, :], dinv_grow[:, 0, bass.ds(t.pos, 1)], 1.0, None, ALU.mult).then_inc(grow_ready, 1)
                    return
                k = t.count(t.phase["g0"] - NT)
                n = top_count(t)
                wait(dve, z_ready, t.g - 1)
                if layer == 4 and t.i is None and t.pos < 2:
                    dve.wait_ge(x1_stored[s], 16 * (NT // 2 + 1 - s))
                b = bias_bc[layer - 1]
                if layer == 4 and t.phase["mixed"]:
                    V.scalar_tensor_tensor(pre[s][:, :], row_in[s][:, :], dinv[:, bass.ds(t.pos, 1)], b[:, :],
                                           ALU.mult, ALU.add).then_inc(in_used, 1)
                    dve.wait_ge(in_used, k + 1)
                    V.tensor_reduce(top[s4][:, :], pre[s][:, :], AX_X, ALU.max).then_inc(top_found, 1)
                    dve.wait_ge(top_found, t.count(0) + 1)
                else:
                    dve.sem_inc(dve_gate, 1)
                    V.tensor_tensor_reduce(pre[s][:, :], row_in[s][:, :], b[:, :], 1.0, -FAR, ALU.add, ALU.max,
                                           top[s4][:, :]).then_inc(in_used, 1)
                    dve.wait_ge(in_used, k + 1)
                V.tensor_scalar(topc[s4][:, :], top[s4][:, :], TINY, 1.0 / UP, ALU.max, ALU.mult).then_inc(top_kept, 1)
                dve.wait_ge(top_kept, n + 1)
                V.reciprocal(shrink[s4][:, :], topc[s4][:, :]).then_inc(shrink_ready, 1)
                by = w_scale[:, 1, 2:3] if layer == 2 else dinv_grow[:, 1, bass.ds(t.pos, 1)]
                V.tensor_scalar(grow[s4][:, :], topc[s4][:, :], by, None, ALU.mult).then_inc(grow_ready, 1)

            def low_parts(t):
                wait(dve, z_hi_ready, t.g + 1)
                V.tensor_tensor(pair3(z_lo[t.slot]), psum_pair(ps_z), pair3(z_hi[t.slot]), ALU.subtract).then_inc(z_lo_ready, 1)

            def result(t):
                s = t.slot
                wait(dve, row_ready, t.g + 1)
                dve.wait_ge(x1_loaded[s], (t.layer_uses + 1) * 16)
                wait(dve, res_stored[s], t.layer_uses * 16)
                V.tensor_tensor(pre_out[s][:, :], row_out[s][:, :], row_in2[s][:, :], ALU.add).then_inc(x1_used, 1)
                dve.wait_ge(x1_used, t.pos + 1)
                V.tensor_tensor(pre_out[s][:, :], pre_out[s][:, :], bias_bc[4][:, :], ALU.add).then_inc(res_ready, 1)

            def edge_dots(layer, h, slot, per_slot, which):
                if 0 in which:
                    dve.wait_ge(e_rows[slot], (per_slot + 1) * 32)
                for n in which:
                    rows, att = ((eg[slot][:, 0:D], atts_bc), (eh[slot][:, :], atts_bc), (eh[slot][:, :], attd_bc))[n]
                    V.tensor_tensor_reduce(e_prod[:, :], rows, att[layer][:, :], 1.0, 0.0, ALU.mult, ALU.add,
                                           dots[:, n:n + 1]).then_inc(dots_done, 1)
                    dve.wait_ge(dots_done, h * 3 + (n + 1))

            def edge_scores(h, slot):
                wait(dve, weights_done, h)
                V.tensor_scalar(score[:, :], dots[:, 0:2], dots[:, 2:3], None, ALU.add).then_inc(score_done, 1)
                dve.wait_ge(score_done, h + 1)
                V.scalar_tensor_tensor(lrelu[:, :], score[:, :], NEG_SLOPE, score[:, :], ALU.mult, ALU.max).then_inc(lrelu_done, 1)
                dve.wait_ge(lrelu_done, h + 1)
                V.tensor_copy(lrelu[0:1, 0:1], e_max[1 - slot][0:1, :]).then_inc(score_fixed, 1)
                dve.wait_ge(score_fixed, h + 1)
                V.tensor_scalar(e_diag[:, :], ident[:, :], lrelu[:, 0:1], None, ALU.mult).then_inc(diag_ready, 1)

            def edge_max(h, slot, j):
                dve.wait_ge(score_rows, h + 1)
                V.tensor_tensor(e_arg[:, :], e_small, far_mask[:, bass.ds(j, 1), :].rearrange("p a q -> p (a q)"), ALU.add).then_inc(arg_done, 1)
                dve.wait_ge(arg_done, h + 1)
                V.tensor_reduce(e_top[:, :], e_arg[:, :], AX_X, ALU.max).then_inc(top_done, 1)
                dve.wait_ge(top_done, h + 1)
                V.tensor_tensor(e_max[slot][:, :], e_top[:, :], lrelu[:, 1:2], ALU.max).then_inc(max_done, 1)
                dve.wait_ge(max_done, h + 1)
                V.tensor_scalar(e_negmax[:, :], e_max[slot][:, :], -1.0, None, ALU.mult).then_inc(negmax_ready, 1)

            def edge_sums(layer, h, slot):
                dve.wait_ge(e_summed, h + 2)
                if layer in GATS:
                    V.tensor_tensor(e_den[:, 0:1], e_den_ps, e_self[:, :], ALU.add).then_inc(den_done, 1)
                    dve.wait_ge(den_done, h + 1)
                    V.scalar_tensor_tensor(e_tmp[:, 0:SPLIT], eh[slot][:, 0:SPLIT], e_self[:, 0:1], e_lo, ALU.mult, ALU.add)
                    V.scalar_tensor_tensor(e_tmp[:, SPLIT:D], eh[slot][:, SPLIT:D], e_self[:, 0:1], ps_e[:, 1, 0:D - SPLIT],
                                           ALU.mult, ALU.add).then_inc(edge_done, 1)
                    V.reciprocal(e_den[:, 1:2], e_den[:, 0:1]).then_inc(den_inv, 1)
                else:
                    dve.wait_ge(e_stored, (h + 1) * 16)
                    V.tensor_tensor(e_out[:, 0:SPLIT], eh[slot][:, 0:SPLIT], e_lo, ALU.add)
                    V.tensor_tensor(e_out[:, SPLIT:D], eh[slot][:, SPLIT:D], ps_e[:, 1, 0:D - SPLIT], ALU.add).then_inc(edge_done, 1)

            def edge_plain(h, j):
                dve.wait_ge(e_summed, h + 1)
                V.tensor_scalar(e_wt_t[:, :], same_t[:, bass.ds(j, 1), :].rearrange("p a q -> p (a q)"), 1.0, None,
                                ALU.mult).then_inc(plain_ready, 1)

            def rank_column(c, slot):
                col = bass.ds(c, 1)
                dve.wait_ge(onehot_used, c + 1)
                k = c * 5
                V.scalar_tensor_tensor(row_cmp, row_iota, edge_id[:, col], row_dst, ALU.is_lt, ALU.subtract).then_inc(ranks_step, 1)
                dve.wait_ge(ranks_step, k + 1)
                V.tensor_scalar(row_cmp, row_cmp, e_f[:, 2, col], 0.0, ALU.is_gt, ALU.add, accum_out=e_rank[:, 0, 0:1]).then_inc(ranks_step, 1)
                dve.wait_ge(ranks_step, k + 2)
                V.tensor_scalar(e_rank[:, 3, :], tile_ends[:, :], e_rank[:, 0, 0:1], 0.0, ALU.is_le, ALU.add,
                                accum_out=e_rank[:, 1, 0:1]).then_inc(ranks_step, 1)
                dve.wait_ge(ranks_step, k + 3)
                V.tensor_scalar(e_rank[:, 2, 0:1], e_rank[:, 1, 0:1], -float(SLOTS), e_rank[:, 0, 0:1], ALU.mult, ALU.add).then_inc(ranks_step, 1)
                dve.wait_ge(ranks_step, k + 4)
                o = onehot[:, slot, :]
                V.tensor_scalar(o[:, 0:P], iota_m1[:, :], e_rank[:, 2, 0:1], None, ALU.is_equal).then_inc(ranks_step, 1)
                V.tensor_scalar(sorts[:, slot, 0:ET], iota_c[:, 0:ET], e_rank[:, 1, 0:1], e_f[:, 0, col], ALU.is_equal, ALU.mult)
                V.tensor_scalar(sorts[:, slot, ET:2 * ET], iota_c[:, 0:ET], e_rank[:, 1, 0:1], e_f[:, 1, col], ALU.is_equal, ALU.mult)
                V.tensor_scalar(o[:, P:2 * P], iota_c[:, :], e_f[:, 3, col], None, ALU.is_equal)
                V.tensor_scalar(o[:, 2 * P:2 * P + NT], iota_c[:, 0:NT], e_f[:, 4, col], None, ALU.is_equal)
                dve.wait_ge(ranks_step, k + 5)
                V.tensor_copy(o[:, 0:1], o[:, P - 1:P]).then_inc(onehot_ready, 1)

            def node_order():
                f, cnt = flag_cnt[:, 0, :], flag_cnt[:, 1, :]
                dve.wait_ge(onehot_used, 2 + EC)
                V.tensor_copy(sorted_src[:, :], sort_ps[:, 0:ET])
                V.tensor_copy(sorted_dst_i[:, :], sort_ps[:, ET:2 * ET])
                V.tensor_copy(dst_in[:, :], sort_ps[:, ET:2 * ET])
                step(V.tensor_copy(dst_of[:, :], sort_ps[:, ET:2 * ET]))
                V.tensor_copy(dst_in[0:1, 1:ET], dst_of[0:1, 0:ET - 1])
                V.memset(dst_in[0:1, 0:1], -1.0)
                step(V.tensor_copy(cnt, count_ps))
                step(V.tensor_scalar(f, cnt, 0.0, None, ALU.is_gt))
                dve.sem_inc(mid_in, 1)
                dve.wait_ge(mid_mm, 2)
                below, total = (ps_e[:, a, 0:2 * NT].rearrange("p (a n) -> p a n", a=2) for a in range(2))
                V.tensor_copy(scan[2][:, :, :], total)
                step(V.tensor_copy(scan[0][:, :, :], total))
                at, d = 0, 1
                while d < NT:
                    V.tensor_copy(scan[1 - at][:, :, 0:d], scan[at][:, :, 0:d])
                    step(V.tensor_tensor(scan[1 - at][:, :, d:NT], scan[at][:, :, d:NT], scan[at][:, :, 0:NT - d], ALU.add))
                    at, d = 1 - at, 2 * d
                incl, before = scan[at], scan[1 - at]
                step(V.tensor_tensor(before[:, :, :], incl[:, :, :], scan[2][:, :, :], ALU.subtract))
                step(V.tensor_tensor(before[:, :, :], before[:, :, :], below, ALU.add))
                A, C = before[:, 0, :], before[:, 1, :]
                w0, w1, w2, w3 = (work[:, k, :] for k in range(4))
                step(V.tensor_scalar(w3[:, 0:1], incl[:, 0, NT - 1:NT], -1.0, float(NP), ALU.mult, ALU.add))
                step(V.scalar_tensor_tensor(w0, A, 2.0, node_id[:, :], ALU.mult, ALU.subtract))
                step(V.tensor_scalar(w0, w0, w3[:, 0:1], None, ALU.add))
                step(V.tensor_tensor(w0, w0, f, ALU.mult))
                step(V.tensor_tensor(w1, node_id[:, :], A, ALU.subtract))
                step(V.tensor_tensor(w0, w0, w1, ALU.add))
                dve.sem_inc(mid_in, 1)
                step(V.tensor_copy(place_i[:, 0, :], w0))
                dve.wait_ge(mid_mm, 3)
                step(V.tensor_copy(pos_t[0:NT, :], ps_e[0:NT, 0, 0:P]))
                dve.sem_inc(mid_in, 1)
                dve.sem_inc(pos_ready, 1)
                V.tensor_scalar(place_i[:, 1, :], place_i[:, 0, :], P - 1, None, ALU.bitwise_and)
                step(V.tensor_scalar(place_i[:, 2, :], place_i[:, 0, :], 7, None, ALU.arith_shift_right))
                step(V.memset(place[:, :, :], -1.0))
                V.tensor_copy(place[:, 0, 0:NT], place_i[:, 1, :])
                V.tensor_copy(place[:, 1, 0:NT], place_i[:, 2, :])
                step(V.scalar_tensor_tensor(w1, C, -1.0, cnt, ALU.add, ALU.add))
                step(V.tensor_copy(w2, w1))
                for j in range(ET):
                    step(V.scalar_tensor_tensor(w2, w1, float(SLOTS * (j + 1)), w2, ALU.is_ge, ALU.add))
                step(V.tensor_scalar(w2, w2, float(AGG + 1), float(ROWS - 1), ALU.add, ALU.min))
                step(V.tensor_tensor(w2, w2, node_id[:, :], ALU.subtract))
                step(V.tensor_tensor(w2, w2, f, ALU.mult))
                step(V.tensor_tensor(place[:, 2, 0:NT], w2, node_id[:, :], ALU.add))
                dve.wait_ge(mid_mm, 4)

            def order_column(c, slot, at):
                dve.wait_ge(place_used, c + 1)
                o, col = onehot[:, slot, :], bass.ds(c, 1)
                V.tensor_scalar(o[:, 0:P], iota_c[:, :], place[:, 0, col], None, ALU.is_equal)
                V.tensor_scalar(o[:, P:P + NT], iota_c[:, 0:NT], place[:, 1, col], node_id_pad[:, col], ALU.is_equal, ALU.mult)
                V.tensor_scalar(o[:, P + NT:P + 2 * NT], iota_c[:, 0:NT], place[:, 1, col], place[:, 2, col], ALU.is_equal, ALU.mult)
                V.tensor_scalar(o[:, P + 2 * NT:P + 3 * NT], iota_c[:, 0:NT], place[:, 1, col], cnt_pad[:, col],
                                ALU.is_equal, ALU.mult).then_inc(place_ready, 1)

            def mask_diag(j):
                col = bass.ds(j, 1)
                V.tensor_scalar(diag2[:, 0, :], ident[:, :], dst_in[:, col], None, ALU.mult)
                V.tensor_scalar(diag2[:, 1, :], ident[:, :], dst_of[:, col], None, ALU.mult).then_inc(dst_diag, 1)

            def mask_make(j):
                col = bass.ds(j, 1)
                far = far_mask[:, col, :].rearrange("p a q -> p (a q)")
                dve.wait_ge(mask_mm, j + 1)
                V.tensor_scalar(e_arg[:, :], mask_ps[:, 0:P], dst_of[:, col], FAR, ALU.is_equal, ALU.mult).then_inc(mask_part, 1)
                V.tensor_scalar(same_t[:, col, :].rearrange("p a q -> p (a q)"), mask_ps[:, P:2 * P], dst_in[:, col], None, ALU.is_equal)
                dve.wait_ge(mask_part, j + 1)
                V.tensor_scalar(far, e_arg[:, :], -FAR, None, ALU.add).then_inc(mask_ready, 1)

            def window(t, side, i, r):
                layer = t.phase["layer"]
                edges, gat, e0 = side == "edges", layer - 1 in GATS, t.phase["edge0"]
                if edges:
                    j, slot, there = edge_tile(i, r // 2, ET)
                    before, slot_before, was_there = edge_tile(i, r // 2 - 1, ET)
                if t.exists(-1) and t.plus(-1).phase["layer"] == 4:
                    result(t.plus(-1))
                if t.exists(1):
                    low_parts(t.plus(1))
                if edges and r % 2 == 0:
                    if gat:
                        if there:
                            edge_dots(layer - 1, j + e0, slot, i + e0 // 2, (0, 1))
                        if was_there:
                            edge_sums(layer - 1, before + e0, slot_before)
                        if there:
                            edge_dots(layer - 1, j + e0, slot, i + e0 // 2, (2,))
                            edge_scores(j + e0, slot)
                    elif there:
                        edge_plain(j + e0, j)
                if edges and gat and r % 2 == 1:
                    edge_max(j + e0, slot, j)
                if side == "order+mask":
                    mask_diag(i * 4 + r)
                if t.exists(3):
                    prepare(t.plus(3))
                if side == "rank" and r % 2 == 0:
                    rank_column(i * 2 + r // 2, r // 2)
                if side in ("order", "order+mask"):
                    base = 0 if side == "order+mask" else 5 * COLS
                    for c in SHARE[r]:
                        order_column(i * COLS + (base + c), c, c)
                if side == "order+mask":
                    mask_make(i * 4 + r)
                if edges and not gat and r % 2 == 1:
                    edge_sums(layer - 1, j + e0, slot)

            def mid():
                node_order()
                step(V.tensor_copy(node_id_pad[:, 0:NT], node_id[:, :]))
                step(V.tensor_copy(cnt_pad[:, 0:NT], flag_cnt[:, 1, :]))

            V.memset(e_src[:, :], PAD)
            V.memset(e_dst[:, :], PAD)
            V.memset(node_id_pad[:, :], 0.0)
            V.memset(cnt_pad[:, :], 0.0)
            for s in range(2):
                V.memset(e_max[s][:, :], 0.0)
            V.memset(row_cmp[:, E:EP].bitcast(I32), PAD).then_inc(graph_padded, 1)
            dve.sem_inc(edge_done, 2)
            dve.sem_inc(onehot_used, 2)
            dve.sem_inc(place_used, COLS)
            dve.wait_ge(consts_ready, 2)
            max_w(1)
            scale_w(1)
            low_w(1)
            dve.wait_ge(graph_loaded, 48)
            V.tensor_scalar(row_dst, row_cmp.bitcast(I32), 2.0, None, ALU.mult)
            V.tensor_copy(e_f[:, 0, :], e_src[:, :])
            V.tensor_copy(e_f[:, 1, :], e_dst[:, :])
            V.tensor_scalar(e_f[:, 2, :], e_dst[:, :], -2.0, None, ALU.mult)
            V.tensor_scalar(e_part[:, 0, :], e_dst[:, :], P - 1, None, ALU.bitwise_and)
            step(V.tensor_scalar(e_part[:, 1, :], e_dst[:, :], 7, None, ALU.arith_shift_right))
            V.tensor_copy(e_f[:, 3, :], e_part[:, 0, :])
            step(V.tensor_copy(e_f[:, 4, :], e_part[:, 1, :]))
            dve.wait_ge(mid_mm, 1)
            run_windows(dve, phases["1"], window, {2: lambda: max_w(2), 42: mid, 62: lambda: scale_w(2), 74: lambda: low_w(2)})
            dve.wait_ge(place_used, COLS + COLS * (-(-NT // COLS)))
            step(V.tensor_copy(perm_f[:, :, :], perm_ps.rearrange("p (a n) -> p a n", a=3)))
            V.tensor_copy(perm_agg[:, :], perm_f[:, 1, :])
            V.tensor_copy(perm[:, :], perm_f[:, 0, :])
            V.scalar_tensor_tensor(perm_out[:, :], perm_f[:, 2, :], float(NP), perm_f[:, 0, :], ALU.mult, ALU.add)
            V.tensor_scalar(perm_x[:, :], perm_f[:, 0, :], float(N - 1), None, ALU.min)
            step(V.tensor_scalar(work[:, 0, :], perm_f[:, 2, :], 0.0, None, ALU.is_gt))
            step(V.tensor_tensor(work[:, 1, :], perm_f[:, 1, :], node_id[:, :], ALU.subtract))
            step(V.tensor_tensor(work[:, 1, :], work[:, 1, :], work[:, 0, :], ALU.mult))
            step(V.tensor_tensor(pos_agg[:, :], work[:, 1, :], node_id[:, :], ALU.add))
            for s in range(2):
                V.memset(eg[s][:, D:D + 1], 1.0)
            step(V.tensor_scalar(perm_f[:, 2, :], perm_f[:, 2, :], 1.0, None, ALU.add))
            step(V.memset(work[:, 2, :], -0.5))
            dve.sem_inc(sqrt_in, 1)
            dve.wait_ge(sqrt_done, 1)
            step(V.tensor_tensor(work[:, 0, :], dinv[:, :], dinv[:, :], ALU.mult))
            step(V.tensor_tensor(work[:, 0, :], work[:, 0, :], perm_f[:, 2, :], ALU.mult))
            step(V.tensor_scalar(work[:, 0, :], work[:, 0, :], -0.5, 1.5, ALU.mult, ALU.add))
            step(V.tensor_tensor(dinv[:, :], dinv[:, :], work[:, 0, :], ALU.mult))
            dve.sem_inc(perm_ready, 1)
            dve.wait_ge(params_loaded, 16 * 8)

            def grow3():
                scale_w(3)
                step(V.tensor_scalar(dinv_grow[:, 0, :], dinv[:, :], w_scale[:, 2, 2:3], 1.0 / UP_LN, ALU.mult, ALU.mult))

            def grow4():
                scale_w(4)
                step(V.tensor_scalar(dinv_grow[:, 1, :], dinv[:, :], w_scale[:, 3, 2:3], None, ALU.mult))

            for phase in chain:
                run_windows(dve, phase, window, {"2f": {0: lambda: max_w(3), 43: grow3, 55: lambda: low_w(3)},
                                                 "2m": {0: lambda: max_w(4), 13: grow4, 15: lambda: low_w(4)}}.get(phase["name"]))

            def last_result(j, s, per_slot):
                h = j + 3 * ET
                dve.wait_ge(e_summed, h + 2)
                V.tensor_tensor(e_tmp[:, 0:SPLIT], eh[s][:, 0:SPLIT], e_lo, ALU.add)
                V.tensor_tensor(e_tmp[:, SPLIT:D], eh[s][:, SPLIT:D], ps_e[:, 1, 0:D - SPLIT], ALU.add).then_inc(edge_done, 1)
                dve.wait_ge(edge_done, h + 3)
                dve.wait_ge(last_x1[s], (per_slot + 1) * 16)
                wait(dve, f_stored[s], per_slot * 16)
                V.scalar_tensor_tensor(pre_out[s][:, :], e_tmp, row_in2_x1[s][:, D:D + 1], row_in2[s], ALU.mult, ALU.add).then_inc(f_sum, 1)
                dve.wait_ge(f_sum, j + 1)
                V.tensor_tensor(pre_out[s][:, :], pre_out[s][:, :], bias_bc[4][:, :], ALU.add).then_inc(f_ready, 1)

            for s, v in all_slots(phases["4f"]["g0"], NT):
                dve.wait_ge(res_stored[s], v)
            for j in range(2):
                edge_plain(j + 3 * ET, j)
                last_result(j, j, 0)
            with dve.Fori(1, ET // 2) as i:
                for r in range(2):
                    edge_plain(i * 2 + r + 3 * ET, i * 2 + r)
                    last_result(i * 2 + r, r, i)


_INS = ["x", "src", "dst", "L0_gnn_W1", "L0_gnn_att_src1", "L0_gnn_att_dst1", "L0_gnn_b1", "L0_gnn_W2", "L0_gnn_att_src2",
        "L0_gnn_att_dst2", "L0_gnn_b2", "L1_gnn_W1", "L1_gnn_b1", "L1_gnn_W2", "L1_gnn_b2"]


def kernel(**inputs):
    import numpy as _np
    import concourse.bacc as _bacc
    from concourse import mybir as _mybir
    from concourse.bass_utils import run_bass_kernel_spmd as _run

    nc = _bacc.Bacc("TRN2", target_bir_lowering=False, num_devices=1)
    arrays, a = {}, {}
    for name in _INS:
        v = _np.ascontiguousarray(inputs[name])
        arrays[f"in_{name}"] = v
        a[name] = nc.dram_tensor(f"in_{name}", v.shape, _mybir.dt.from_np(v.dtype), kind="ExternalInput").ap()
    out = nc.dram_tensor("out", inputs["x"].shape, _mybir.dt.float32, kind="ExternalOutput").ap()
    build(nc, a["x"], a["src"], a["dst"],
          {1: a["L0_gnn_W1"], 2: a["L0_gnn_W2"], 3: a["L1_gnn_W1"], 4: a["L1_gnn_W2"]},
          {1: a["L0_gnn_att_src1"], 2: a["L0_gnn_att_src2"]}, {1: a["L0_gnn_att_dst1"], 2: a["L0_gnn_att_dst2"]},
          {1: a["L0_gnn_b1"], 2: a["L0_gnn_b2"], 3: a["L1_gnn_b1"], 4: a["L1_gnn_b2"]}, out)
    r = _run(nc, [arrays], core_ids=[0])
    return r.results[0]["out"]
```

```python
from contextlib import ExitStack

import concourse.bass as bass
from concourse import mybir

P = 128
F32 = mybir.dt.float32
F16 = mybir.dt.float16
I32 = mybir.dt.int32
ALU = mybir.AluOpType
ACT = mybir.ActivationFunctionType
AX_X = mybir.AxisListType.X
RMAX = bass.bass_isa.ReduceOp.max

NEG_SLOPE = 0.2
EPS = 1e-5
TINY = 1e-30
FAR = 1e30
EXPONENT = 0x7F800000
UP = 2.0 ** 12
UP_LN = 2.0 ** 10


class Tile:

    def __init__(self, phase, at, i=None, step=4):
        self.phase, self.at, self.i, self.step = phase, at, i, step

    def plus(self, k):
        phase, at = self.phase, self.at + k
        if self.i is None and at >= phase["n"] and phase["next"]:
            phase, at = phase["next"], at - phase["n"]
        elif self.i is None and at < 0 and phase["before"]:
            phase, at = phase["before"], at + phase["before"]["n"]
        return Tile(phase, at, self.i, self.step)

    def exists(self, k):
        return self.i is not None or 0 <= self.plus(k).at < self.plus(k).phase["n"]

    def count(self, before, every=1):
        c = (before + self.at) // every
        return c if self.i is None else self.i * (self.step // every) + c

    @property
    def g(self):
        return self.count(self.phase["g0"])

    @property
    def slot(self):
        return (self.phase["g0"] + self.at) % 2

    @property
    def slot4(self):
        return (self.phase["g0"] + self.at) % 4

    @property
    def slot_uses(self):
        return self.count(self.phase["g0"], 2)

    @property
    def phase_uses(self):
        return self.count(0, 2)

    @property
    def pos(self):
        return self.count(self.phase["first"])

    @property
    def layer_uses(self):
        return (self.phase["first"] + self.at) // 2 if self.i is None else self.i * (self.step // 2) + (self.phase["first"] + self.at) // 2


def wait(e, sem, value):
    if not isinstance(value, int) or value > 0:
        e.wait_ge(sem, value)


def run_windows(e, phase, window, hooks=None):
    n = phase["n"]
    t = 0 if phase["before"] else -4
    starts = {start: (turns, side) for start, turns, side in phase["loops"]}
    while t < n + (0 if phase["next"] else 1):
        if hooks and t in hooks:
            hooks[t]()
        if t in starts:
            turns, side = starts[t]
            first, peel = (1 if side in ("edges", "rank") else 0), (1 if side == "edges" else 0)
            for i in range(first):
                for r in range(4):
                    window(Tile(phase, t + r), side, i, r)
            with e.Fori(first, turns - peel) as i:
                for r in range(4):
                    window(Tile(phase, t + r, i), side, i, r)
            for i in range(turns - peel, turns):
                for r in range(4):
                    window(Tile(phase, t + 4 * i + r), side, i, r)
            t += 4 * turns
            if peel:
                window(Tile(phase, t), side, turns, 0)
                t += 1
            continue
        window(Tile(phase, t), None, None, 0)
        t += 1


def edge_tile(i, c, tiles):
    j = i * 2 + c
    return j, c % 2, not isinstance(i, int) or 0 <= j < tiles


def build(nc, x, src, dst, w, att_src, att_dst, bias, out):
    N, D = x.shape
    E = src.shape[0]
    KC = D // P
    HALF = D // 2
    NT = -(-N // P)
    NP = NT * P
    LAST = N - (NT - 1) * P
    EC = -(-E // P)
    ER = -(-E // EC)
    assert ER * EC == E and EC * P == -(-E // P) * P
    EP = EC * P
    SLOTS = P - 1
    ET = EC
    assert ET * SLOTS >= E and (ET - 1) * SLOTS < E
    PAD = NP - 1
    assert PAD >= N
    FREE = (NP - E - 1) // P
    MIXED = NT - FREE
    AGG = NP
    ROWS = NP + ET * P
    COLS = 12
    SHARE = [tuple(range(3 * r, 3 * r + 3)) for r in range(4)]
    RANKED = 2 + 2 * ET
    ORDER = RANKED + 4
    ORDERED = ORDER + 4 * (-(-NT // COLS))
    assert ORDERED + 4 <= NT

    phases = {}
    g = 0
    for layer in (1, 2, 3, 4):
        if layer == 1:
            phases["1"] = dict(layer=1, n=NT, g0=0, first=0, mixed=False,
                               loops=[(2, ET // 2, "rank"), (ORDER, ET // 4, "order+mask"),
                                      (ORDER + ET, -(-NT // COLS) - ET // 4, "order")])
            g = NT
            continue
        phases[f"{layer}f"] = dict(layer=layer, n=FREE, g0=g, first=0, mixed=False,
                                   loops=[(2, ET // 2, "edges"), (3 + 2 * ET, (FREE - 7 - 2 * ET) // 4, None)])
        phases[f"{layer}m"] = dict(layer=layer, n=MIXED, g0=g + FREE, first=FREE, mixed=True,
                                   loops=[(3, (MIXED - 7) // 4, None)])
        g += NT
    for name, ph in phases.items():
        ph["name"] = name
        ph["before"] = ph["next"] = None
        ph["edge0"] = {1: 0, 2: 0, 3: ET, 4: 2 * ET}[ph["layer"]]

    chain = [phases[k] for k in ("2f", "2m", "3f", "3m", "4f", "4m")]
    for one, two in zip([phases["1"]] + chain, chain):
        one["next"], two["before"] = two, one

    def all_slots(first, tiles):
        return [(first % 2, 16 * -(-tiles // 2)), (1 - first % 2, 16 * (tiles // 2))]

    table = {n: nc.dram_tensor(f"rows_{n}", [ROWS, D], F32).ap() for n in (1, 2, 3, 4)}
    pos_of = nc.dram_tensor("pos_of", [NP, 1], I32).ap()
    x1_rows = nc.dram_tensor("x1_rows", [NP, D], F32).ap()
    base_rows = nc.dram_tensor("base_rows", [MIXED * P, D + 1], F32).ap()

    ctx = ExitStack()
    with ctx:
        def sb(name, shape, dt=F32):
            return ctx.enter_context(nc.sbuf_tensor(name, shape, dt))

        def sem(name):
            return ctx.enter_context(nc.semaphore(name))

        w_hi = [sb(f"w_hi{s}", [P, KC, D], F16) for s in range(3)]
        w_lo = [sb(f"w_lo{s}", [P, KC, D], F16) for s in range(3)]
        w_raw = sb("w_raw", [P, KC * D])
        w_of = {1: 0, 2: 1, 3: 2, 4: 0}
        w_scale = sb("w_scale", [P, 4, 4])
        row_in = [sb(f"row_in{s}", [P, D]) for s in range(2)]
        row_in2 = [sb(f"row_in2{s}", [P, D]) for s in range(2)]
        pre = [sb(f"pre{s}", [P, D]) for s in range(2)]
        z = [sb(f"z{s}", [P, D]) for s in range(2)]
        z_hi = [sb(f"z_hi{s}", [P, KC, P], F16) for s in range(2)]
        z_lo = [sb(f"z_lo{s}", [P, KC, P], F16) for s in range(2)]
        row_out = [sb(f"row_out{s}", [P, D]) for s in range(2)]
        base_out = [sb(f"base_out{s}", [P, D + 1]) for s in range(2)]
        pre_out = [b[:, 0:D] for b in base_out]
        bn = [sb(f"bn{s}", [P, 12]) for s in range(2)]
        mv = [sb(f"mv{s}", [P, 2]) for s in range(4)]
        veps = [sb(f"veps{s}", [P, 1]) for s in range(4)]
        rstd = [sb(f"rstd{s}", [P, 1]) for s in range(4)]
        nmr = [sb(f"nmr{s}", [P, 1]) for s in range(4)]
        top = [sb(f"top{s}", [P, 1]) for s in range(4)]
        topc = [sb(f"topc{s}", [P, 1]) for s in range(4)]
        shrink = [sb(f"shrink{s}", [P, 1]) for s in range(4)]
        grow = [sb(f"grow{s}", [P, 1]) for s in range(4)]
        idx_a = [sb(f"idx_a{s}", [P, 1], I32) for s in range(2)]
        idx_b = [sb(f"idx_b{s}", [P, 1], I32) for s in range(2)]
        idx_o = [sb(f"idx_o{s}", [P, 1], I32) for s in range(2)]
        bias_bc = {n: sb(f"bias_bc{n}", [P, D]) for n in (1, 2, 3, 4)}
        atts_bc = {n: sb(f"atts_bc{n}", [P, D]) for n in (1, 2)}
        attd_bc = {n: sb(f"attd_bc{n}", [P, D]) for n in (1, 2)}
        ident = sb("ident", [P, P])
        ones = sb("ones", [P, P])
        upper = sb("upper", [P, P])
        half_neg = sb("half_neg", [P, 1])
        iota_c = sb("iota_c", [P, P])
        iota_m1 = sb("iota_m1", [P, P])
        node_id = sb("node_id", [P, NT])
        node_id_pad = sb("node_id_pad", [P, COLS * (-(-NT // COLS))])
        cnt_pad = sb("cnt_pad", [P, COLS * (-(-NT // COLS))])
        edge_id = sb("edge_id", [P, EC])
        tile_ends = sb("tile_ends", [P, ET])
        rank_mem = sb("rank_mem", [P, 3, EP])
        row_dst, row_cmp, row_iota = (rank_mem[:, k, :] for k in range(3))
        masks = rank_mem[:, 0:2, :].rearrange("p a (t q) -> p a t q", q=P)
        far_mask, same_t = masks[:, 0], masks[:, 1]
        e_src = sb("e_src", [P, EC], I32)
        e_dst = sb("e_dst", [P, EC], I32)
        e_part = sb("e_part", [P, 2, EC], I32)
        e_f = sb("e_f", [P, 5, EC])
        e_rank = sb("e_rank", [P, 4, EC])
        edge_mem = sb("edge_mem", [P, 6 * D + 2])
        onehot = edge_mem[:, 0:COLS * 3 * P].rearrange("p (k c) -> p k c", k=COLS)
        sorts = sb("sorts", [P, 2, 2 * ET])
        diag2 = sb("diag2", [P, 2, P])
        sorted_src = sb("sorted_src", [P, ET], I32)
        sorted_dst_i = sb("sorted_dst_i", [P, ET], I32)
        dst_of = sb("dst_of", [P, ET])
        dst_in = sb("dst_in", [P, ET])
        flag_cnt = sb("flag_cnt", [P, 2, NT])
        scan = [sb(f"scan{s}", [P, 2, NT]) for s in range(3)]
        work = sb("work", [P, 4, NT])
        place = sb("place", [P, 3, COLS * (-(-NT // COLS))])
        place_i = sb("place_i", [P, 3, NT], I32)
        perm_f = sb("perm_f", [P, 3, NT])
        perm = sb("perm", [P, NT], I32)
        perm_out = sb("perm_out", [P, NT], I32)
        perm_x = sb("perm_x", [P, NT], I32)
        perm_agg = sb("perm_agg", [P, NT], I32)
        pos_agg = sb("pos_agg", [P, NT], I32)
        dinv = sb("dinv", [P, NT])
        dinv_grow = sb("dinv_grow", [P, 2, NT])
        eg = [edge_mem[:, s * (D + 1):(s + 1) * (D + 1)] for s in range(2)]
        eh = [edge_mem[:, 2 + (2 + s) * D:2 + (3 + s) * D] for s in range(2)]
        pos_src = sb("pos_src", [P, ET], I32)
        pos_dst = sb("pos_dst", [P, ET], I32)
        pos_base = sb("pos_base", [P, ET], I32)
        pos_got = sb("pos_got", [P, 2], I32)
        idx_s = [sb(f"idx_s{s}", [P, 1], I32) for s in range(2)]
        idx_d = [sb(f"idx_d{s}", [P, 1], I32) for s in range(2)]
        e_tmp = edge_mem[:, 2 + 4 * D:2 + 5 * D]
        e_prod = edge_mem[:, 2 + 5 * D:2 + 6 * D]
        e_out = sb("e_out", [P, D])
        zeros = e_out[:, 0:512]
        last_src = [b[:, 0:D] for b in (eg[0], eg[1], eh[0], eh[1])]
        last_base = [w_raw[:, s * (D + 1):(s + 1) * (D + 1)] for s in range(4)]
        last_idx = [sb(f"last_idx{s}", [P, 2], I32) for s in range(4)]
        dots = sb("dots", [P, 3])
        score = sb("score", [P, 2])
        lrelu = sb("lrelu", [P, 2])
        e_max = [sb(f"e_max{s}", [P, 1]) for s in range(2)]
        e_top = sb("e_top", [P, 1])
        e_negmax = sb("e_negmax", [P, 1])
        e_self = sb("e_self", [P, 1])
        e_den = sb("e_den", [P, 2])
        pos_t = row_iota[:, 0:P].bitcast(I32)
        e_diag, e_arg, e_wt, e_wt_t = (row_iota[:, (k + 1) * P:(k + 2) * P] for k in range(4))

        ps_z = ctx.enter_context(nc.psum_tensor("ps_z", [P, 2, 512], F32))
        ps_h = [ctx.enter_context(nc.psum_tensor(f"ps_h{s}", [P, 2, 512], F32)) for s in range(2)]
        ps_e = ctx.enter_context(nc.psum_tensor("ps_e", [P, 2, 512], F32))
        SPLIT = HALF + 1
        e_lo, e_hi = ps_e[:, 0, 0:SPLIT], ps_e[:, 1, 0:D + 1 - SPLIT]
        e_den_ps = ps_e[:, 1, D - SPLIT:D + 1 - SPLIT]
        e_small = ps_e[:, 1, HALF:HALF + P]
        sort_ps = ps_e[:, 0, 0:2 * ET]
        count_ps = ps_e[:, 1, 0:NT]
        perm_ps = ps_e[:, 0, 0:3 * NT]
        mask_ps = ps_e[:, 1, 0:2 * P]

        consts_ready = sem("consts_ready")
        params_loaded = sem("params_loaded")
        graph_loaded = sem("graph_loaded")
        graph_padded = sem("graph_padded")
        setup_step = sem("setup_step")
        w_loaded = sem("w_loaded")
        w_max = sem("w_max")
        w_max_all = sem("w_max_all")
        w_scaled = sem("w_scaled")
        w_hi_ready = sem("w_hi_ready")
        w_ready = sem("w_ready")
        x_loaded = [sem(f"x_loaded{s}") for s in range(2)]
        in_ready = {name: [sem(f"in_ready{name}_{s}") for s in range(2)] for name in phases if name != "1"}
        in_used = sem("in_used")
        x_ready = [sem(f"x_ready{s}") for s in range(2)]
        x1_loaded = [sem(f"x1_loaded{s}") for s in range(2)]
        x1_ready = sem("x1_ready")
        x1_stored = [sem(f"x1_stored{s}") for s in range(2)]
        x1_used = sem("x1_used")
        stats_done = sem("stats_done")
        mean_var = sem("mean_var")
        var_eps = sem("var_eps")
        rstd_done = sem("rstd_done")
        norm_ready = sem("norm_ready")
        top_found = sem("top_found")
        top_kept = sem("top_kept")
        shrink_ready = sem("shrink_ready")
        grow_ready = sem("grow_ready")
        z_ready = sem("z_ready")
        z_turned = sem("z_turned")
        z_hi_ready = sem("z_hi_ready")
        z_lo_ready = sem("z_lo_ready")
        h_ready = sem("h_ready")
        row_ready = sem("row_ready")
        row_stored = [sem(f"row_stored{s}") for s in range(2)]
        res_ready = sem("res_ready")
        res_stored = [sem(f"res_stored{s}") for s in range(2)]
        idx_in_ready = sem("idx_in_ready")
        idx_out_ready = sem("idx_out_ready")
        pool_gate = sem("pool_gate")
        dve_gate = sem("dve_gate")
        ranks_step = sem("ranks_step")
        onehot_ready = sem("onehot_ready")
        onehot_used = sem("onehot_used")
        mid_mm = sem("mid_mm")
        pos_ready = sem("pos_ready")
        pos_stored = sem("pos_stored")
        pos_idx = sem("pos_idx")
        pos_kept = sem("pos_kept")
        pos_found = [sem(f"pos_found{k}") for k in range(2)]
        mid_in = sem("mid_in")
        place_ready = sem("place_ready")
        place_used = sem("place_used")
        dst_diag = sem("dst_diag")
        mask_mm = sem("mask_mm")
        mask_part = sem("mask_part")
        mask_ready = sem("mask_ready")
        perm_ready = sem("perm_ready")
        sqrt_in = sem("sqrt_in")
        sqrt_done = sem("sqrt_done")
        eidx_ready = sem("eidx_ready")
        e_rows = [sem(f"e_rows{s}") for s in range(2)]
        dots_done = sem("dots_done")
        score_done = sem("score_done")
        lrelu_done = sem("lrelu_done")
        score_fixed = sem("score_fixed")
        diag_ready = sem("diag_ready")
        score_rows = sem("score_rows")
        arg_done = sem("arg_done")
        top_done = sem("top_done")
        max_done = sem("max_done")
        negmax_ready = sem("negmax_ready")
        weights_done = sem("weights_done")
        weights_turned = sem("weights_turned")
        weights_ready = sem("weights_ready")
        plain_ready = sem("plain_ready")
        carry_ready = sem("carry_ready")
        e_summed = sem("e_summed")
        den_done = sem("den_done")
        den_inv = sem("den_inv")
        edge_done = sem("edge_done")
        e_out_ready = sem("e_out_ready")
        e_stored = sem("e_stored")
        base_stored = [sem(f"base_stored{s}") for s in range(2)]
        base_idx_ready = sem("base_idx_ready")
        last_idx_ready = sem("last_idx_ready")
        last_in = [sem(f"last_in{s}") for s in range(4)]
        last_stored = [sem(f"last_stored{s}") for s in range(2)]

        block = ctx.enter_context(nc.Block())
        GATS = (1, 2)

        def w_view(t):
            return t[:, :].rearrange("p (c n) -> p c n", c=KC)

        def psum_pair(t):
            return t[:, :, 0:HALF]

        def pair(t):
            return t[:, :].rearrange("p (a n) -> p a n", a=2)

        def pair3(t):
            return t[:, :, :].rearrange("p (a c) n -> p a (c n)", a=2)

        def ln_count(t):
            return t.count(t.phase["g0"] if t.phase["layer"] == 1 else t.phase["g0"] - NT)

        def top_count(t):
            return t.count(t.phase["g0"] - NT if t.phase["layer"] == 2 else t.phase["g0"] - 2 * NT)

        @block.sync
        def _(sp):
            def load_w(layer):
                if layer > 1:
                    sp.wait_ge(w_ready, layer - 1)
                sp.dma_start(w_view(w_raw), w[layer].rearrange("(c p) n -> p c n", p=P)).then_inc(w_loaded, 16)

            def row_of(v):
                return bass.AP(v.tensor, v.offset, [[0, P], [1, v.shape[0]]])

            def load_x(t):
                if t.i is None and t.at == NT - 1:
                    wait(sp, z_ready, t.g - 1)
                    sp.dma_start(row_in[t.slot][0:LAST, :], x[(NT - 1) * P:N, :]).then_inc(x_loaded[t.slot], 16)
                    return
                wait(sp, z_ready, t.g - 1)
                at = t.count(0) * P
                sp.dma_start(row_in[t.slot][:, :], x[bass.ds(at, P), :]).then_inc(x_loaded[t.slot], 16)

            def store(t):
                wait(sp, row_ready, t.g + 1)
                sp.dma_start(table[t.phase["layer"]][bass.ds(t.pos * P, P), :], row_out[t.slot][:, :]).then_inc(row_stored[t.slot], 16)

            def window1(t, side, i, r):
                if t.exists(-1):
                    store(t.plus(-1))
                if t.exists(4) and t.plus(4).phase["layer"] == 1:
                    load_x(t.plus(4))

            def load(t):
                s, ago = t.slot, t.count(t.phase["g0"] - NT)
                sp.wait_ge(in_used, ago - 1)
                sp.wait_ge(row_stored[1 - s], (t.count(t.phase["g0"] - NT, 2) + 1) * 16)
                sp.dma_start(row_in[s][:, :], table[t.phase["layer"] - 1][bass.ds(t.pos * P, P), :]).then_inc(
                    in_ready[t.phase["name"]][s], 16)

            def edge_store(layer, h, j):
                if layer in GATS:
                    sp.wait_ge(e_out_ready, h + 1)
                else:
                    sp.wait_ge(edge_done, h + 3)
                sp.dma_start(table[layer][bass.ds(j * P + AGG, P), :], e_out[:, :]).then_inc(e_stored, 16)

            def window(t, side, i, r):
                if t.exists(4) and t.plus(4).phase["name"] in ("3f", "4f"):
                    load(t.plus(4))
                if t.exists(-1):
                    store(t.plus(-1))
                b = t.plus(1)
                if t.exists(1) and b.phase["layer"] == 4:
                    if b.i is None and b.pos < 2:
                        sp.wait_ge(in_used, b.g - NT - 1)
                    else:
                        wait(sp, x1_used, b.pos - 1)
                    sp.wait_ge(x1_stored[1 - b.slot], (b.layer_uses + 1) * 16)
                    sp.dma_start(row_in2[b.slot][:, :], x1_rows[bass.ds(b.pos * P, P), :]).then_inc(x1_loaded[b.slot], 16)
                b = t.plus(3)
                if t.exists(3) and b.phase["layer"] == 3:
                    wait(sp, x1_ready, b.pos + 1)
                    sp.dma_start(x1_rows[bass.ds(b.pos * P, P), :], pre[b.slot][:, :]).then_inc(x1_stored[b.slot], 16)
                b = t.plus(-1)
                if t.exists(-1) and b.phase["name"] == "4m":
                    sp.wait_ge(res_ready, b.pos + 1)
                    sp.dma_start(base_rows[bass.ds(b.count(0) * P, P), :], base_out[b.slot][:, :]).then_inc(base_stored[b.slot], 16)
                if side == "edges":
                    gat = t.phase["layer"] - 1 in GATS
                    j, _, there = edge_tile(i, r // 2 - (1 if gat else 0), ET)
                    if there and r % 2 == (0 if gat else 1):
                        edge_store(t.phase["layer"] - 1, j + t.phase["edge0"], j)

            load_w(1)
            sp.wait_ge(graph_padded, 1)
            sp.dma_start(e_src[0:ER, :], src.rearrange("(p c) -> p c", c=EC)).then_inc(graph_loaded, 16)
            sp.dma_start(e_dst[0:ER, :], dst.rearrange("(p c) -> p c", c=EC)).then_inc(graph_loaded, 16)
            sp.dma_start(row_cmp[:, 0:E].bitcast(I32), row_of(dst)).then_inc(graph_loaded, 16)
            sp.sem_inc(e_stored, 16)

            def load_params():
                for n in (1, 2, 3, 4):
                    sp.dma_start(bias_bc[n][:, :], row_of(bias[n])).then_inc(params_loaded, 16)
                for n in GATS:
                    sp.dma_start(atts_bc[n][:, :], row_of(att_src[n])).then_inc(params_loaded, 16)
                    sp.dma_start(attd_bc[n][:, :], row_of(att_dst[n])).then_inc(params_loaded, 16)

            def store_positions():
                sp.wait_ge(pos_ready, 1)
                sp.dma_start(pos_of.rearrange("(h l) a -> h (l a)", l=P), pos_t[0:NT, :]).then_inc(pos_stored, 16)

            run_windows(sp, phases["1"], window1, {0: lambda: load_w(2), RANKED + 3: store_positions,
                                                   ORDERED: load_params, ORDERED + 2: lambda: load_w(3)})
            for phase in chain:
                run_windows(sp, phase, window, {56: lambda: load_w(4)} if phase["name"] == "2f" else None)
            for s, v in all_slots(phases["4f"]["g0"], NT):
                sp.wait_ge(res_stored[s], v)
            for s, v in all_slots(0, ET):
                sp.wait_ge(last_stored[s], v)

        @block.gpsimd
        def _(pool):
            def gate():
                pool.sem_inc(pool_gate, 1)

            def gather(to, idx, rows, done):
                pool.indirect_dma_start(out=to, out_offset=None, in_=rows,
                                        in_offset=bass.IndirectOffsetOnAxis(ap=idx[:, 0:1], axis=0)).then_inc(done, 16)

            def scatter(rows, idx, frm, done, limit=None):
                more = {} if limit is None else dict(bounds_check=limit, oob_is_err=False)
                pool.indirect_dma_start(out=rows, out_offset=bass.IndirectOffsetOnAxis(ap=idx[:, 0:1], axis=0),
                                        in_=frm, in_offset=None, **more).then_inc(done, 16)

            def norm_factors(t):
                s, k = t.slot4, ln_count(t)
                wait(pool, mean_var, k + 1)
                gate()
                nc.gpsimd.tensor_scalar(veps[s][:, :], mv[s][:, 1:2], EPS, UP_LN ** -2, ALU.add, ALU.mult).then_inc(var_eps, 1)
                pool.wait_ge(var_eps, k + 1)
                nc.gpsimd.tensor_tensor(rstd[s][:, :], veps[s][:, :], half_neg[:, :], ALU.pow).then_inc(rstd_done, 1)
                pool.wait_ge(rstd_done, k + 1)
                gate()
                nc.gpsimd.tensor_scalar(nmr[s][:, :], mv[s][:, 0:1], rstd[s][:, 0:1], -1.0, ALU.mult, ALU.mult).then_inc(norm_ready, 1)

            def window1(t, side, i, r):
                if side == "order+mask":
                    find_positions(i * 4 + r)
                if t.exists(3) and t.plus(3).phase["layer"] == 1:
                    norm_factors(t.plus(3))
                if t.exists(4) and t.plus(4).phase["layer"] == 2:
                    load(t.plus(4))
                if side == "order+mask":
                    keep_positions(i * 4 + r)

            def find_positions(j):
                nc.gpsimd.tensor_copy(idx_s[0][:, :], sorted_src[:, bass.ds(j, 1)])
                nc.gpsimd.tensor_copy(idx_d[0][:, :], sorted_dst_i[:, bass.ds(j, 1)]).then_inc(pos_idx, 1)
                pool.wait_ge(pos_idx, j + 1)
                gate()
                gather(pos_got[:, 0:1], idx_s[0], pos_of, pos_found[0])
                gather(pos_got[:, 1:2], idx_d[0], pos_of, pos_found[1])

            def keep_positions(j):
                for k, to in enumerate((pos_src, pos_dst)):
                    pool.wait_ge(pos_found[k], j * 16 + 16)
                    gate()
                    nc.gpsimd.tensor_copy(to[:, bass.ds(j, 1)], pos_got[:, k:k + 1]).then_inc(pos_kept, 1)

            def load(t):
                phase, s, k = t.phase, t.slot, t.count(t.phase["g0"] - NT)
                if t.i is None and t.at == 0 and phase["mixed"]:
                    pool.wait_ge(e_stored, 16 * (phase["edge0"] + ET + 1))
                if t.i is None and k < 2:
                    pool.wait_ge(z_ready, t.g - 1)
                wait(pool, in_used, k - 1)
                rows = ROWS if phase["mixed"] else NP
                if phase["name"] == "2f" and t.i is None and t.at < 6:
                    ahead = t.at + 2 + -(-E // P)
                    rows = ahead * P
                    for slot, v in all_slots(0, ahead):
                        pool.wait_ge(row_stored[slot], v)
                gate()
                rows_idx = (perm_agg if phase["layer"] == 2 else pos_agg) if phase["mixed"] else perm
                if phase["name"] != "3f":
                    last = nc.gpsimd.tensor_copy(idx_a[s][:, :], rows_idx[:, bass.ds(t.pos, 1)])
                if phase["layer"] == 3:
                    last = nc.gpsimd.tensor_copy(idx_b[s][:, :], perm_x[:, bass.ds(t.pos, 1)])
                last.then_inc(idx_in_ready, 1)
                pool.wait_ge(idx_in_ready, (k if phase["layer"] < 4 else t.count(t.phase["g0"] - NT - FREE)) + 1)
                gate()
                if phase["name"] != "3f":
                    gather(row_in[s][:, :], idx_a[s], table[phase["layer"] - 1][0:rows, :],
                           in_ready[phase["name"]][s])
                if phase["layer"] == 3:
                    gather(row_in2[s][:, :], idx_b[s], x, x_ready[s])

            def store_result(t):
                s = t.slot
                pool.wait_ge(res_ready, t.pos + 1)
                gate()
                nc.gpsimd.tensor_copy(idx_o[s][:, :], perm_out[:, bass.ds(t.pos, 1)]).then_inc(idx_out_ready, 1)
                pool.wait_ge(idx_out_ready, t.pos + 1)
                gate()
                scatter(out, idx_o[s], pre_out[s][:, :], res_stored[s], N - 1)

            def edge_rows(layer, h, slot, j):
                of_src, of_dst = (sorted_src, sorted_dst_i) if layer == 1 else (pos_src, pos_dst)
                pool.wait_ge(edge_done, h + 1)
                gate()
                nc.gpsimd.tensor_copy(idx_s[slot][:, :], of_src[:, bass.ds(j, 1)])
                nc.gpsimd.tensor_copy(idx_d[slot][:, :], of_dst[:, bass.ds(j, 1)]).then_inc(eidx_ready, 1)
                pool.wait_ge(eidx_ready, h + 1)
                gate()
                gather(eg[slot][:, 0:D], idx_s[slot], table[layer][0:NP, :], e_rows[slot])
                gather(eh[slot][:, :], idx_d[slot], table[layer][0:NP, :], e_rows[slot])

            def window(t, side, i, r):
                if t.exists(4) and t.plus(4).phase["name"] != "4f":
                    load(t.plus(4))
                b = t.plus(-1)
                if t.exists(-1) and b.phase["layer"] == 4:
                    store_result(b)
                if side == "edges" and r % 2 == 0:
                    j, slot, there = edge_tile(i, r // 2 + 1, ET)
                    if there:
                        edge_rows(t.phase["layer"] - 1, j + t.phase["edge0"], slot, j)
                if t.exists(3) and t.plus(3).phase["layer"] == 3:
                    norm_factors(t.plus(3))

            nc.gpsimd.iota(iota_c[:, :], [[1, P]], base=0, channel_multiplier=0, allow_small_or_imprecise_dtypes=True)
            nc.gpsimd.iota(iota_m1[:, :], [[1, P]], base=-1, channel_multiplier=0, allow_small_or_imprecise_dtypes=True)
            nc.gpsimd.iota(node_id[:, :], [[P, NT]], base=0, channel_multiplier=1, allow_small_or_imprecise_dtypes=True)
            nc.gpsimd.iota(edge_id[:, :], [[1, EC]], base=0, channel_multiplier=EC, allow_small_or_imprecise_dtypes=True)
            nc.gpsimd.iota(tile_ends[:, :], [[SLOTS, ET]], base=SLOTS, channel_multiplier=0, allow_small_or_imprecise_dtypes=True)
            nc.gpsimd.iota(row_iota, [[1, EP]], base=0, channel_multiplier=0, allow_small_or_imprecise_dtypes=True)
            nc.gpsimd.memset(zeros, 0.0)
            nc.gpsimd.memset(half_neg[:, :], -0.5)
            nc.gpsimd.memset(ident[:, :], 0.0)
            nc.gpsimd.memset(ones[:, :], 1.0).then_inc(consts_ready, 1)
            pool.wait_ge(consts_ready, 1)
            nc.gpsimd.affine_select(ident[:, :], ident[:, :], [[-1, P]], ALU.not_equal, 1.0, base=0, channel_multiplier=1)
            nc.gpsimd.affine_select(upper[:, :], ones[:, :], [[1, P]], ALU.is_gt, 0.0, base=0, channel_multiplier=-1).then_inc(consts_ready, 1)

            def all_max(layer):
                pool.wait_ge(w_max, layer)
                nc.gpsimd.partition_all_reduce(w_scale[:, layer - 1, 1:2], w_scale[:, layer - 1, 0:1], P, RMAX).then_inc(w_max_all, 1)

            def sqrt_degree():
                pool.wait_ge(sqrt_in, 1)
                nc.gpsimd.tensor_tensor(dinv[:, :], perm_f[:, 2, :], work[:, 2, :], ALU.pow).then_inc(sqrt_done, 1)

            all_max(1)
            run_windows(pool, phases["1"], window1,
                        {2: lambda: all_max(2), ORDER: lambda: pool.wait_ge(pos_stored, 16),
                         ORDERED + 1: lambda: pool.wait_ge(perm_ready, 1),
                         ORDERED + 3: sqrt_degree})
            pool.wait_ge(pos_kept, 2 * ET)
            for phase in chain:
                def rows_complete(layer=phase["layer"] - 1):
                    for s, v in all_slots(0, layer * NT):
                        pool.wait_ge(row_stored[s], v)

                def first_edges(phase=phase, rows_complete=rows_complete):
                    rows_complete()
                    edge_rows(phase["layer"] - 1, phase["edge0"], 0, 0)

                hooks = {} if phase["mixed"] else {1: first_edges}
                if phase["name"] == "2f":
                    hooks[0] = lambda: all_max(3)
                if phase["name"] == "2m":
                    hooks[0] = lambda: all_max(4)
                run_windows(pool, phase, window, hooks)
            for s, v in all_slots(0, 4 * NT):
                pool.wait_ge(row_stored[s], v)
            for s, v in all_slots(phases["4m"]["g0"], MIXED):
                pool.wait_ge(base_stored[s], v)

            def last_rows(at, i=None):
                slot, j = at % 4, at if i is None else i * 4 + at
                pool.wait_ge(last_idx_ready, j + 1)
                gate()
                gather(last_src[slot], last_idx[slot][:, 0:1], table[4][0:NP, :], last_in[slot])
                gather(last_base[slot], last_idx[slot][:, 1:2], base_rows, last_in[slot])

            def last_store(at, i=None):
                s, j = at % 2, at if i is None else i * 4 + at
                pool.wait_ge(edge_done, j + (3 * ET + 3))
                if i is not None or at > 0:
                    pool.wait_ge(last_stored[1 - s], ((at + 1) // 2 if i is None else i * 2 + (at + 1) // 2) * 16)
                gate()
                scatter(out, idx_o[s], pre_out[s][:, :], last_stored[s], N - 1)

            for at in range(4):
                last_rows(at)
            last_store(0)
            with pool.Fori(0, ET // 4 - 1) as i:
                for at in range(4):
                    last_rows(at + 4, i)
                    last_store(at + 1, i)
            for at in range(ET - 3, ET):
                last_store(at)

        @block.scalar
        def _(act):
            def split_w(layer):
                act.wait_ge(w_scaled, layer)
                act.wait_ge(w_loaded, 16 * layer)
                if layer == 4:
                    act.wait_ge(h_ready, NT)
                nc.scalar.activation(w_hi[w_of[layer]][:, :, :], w_view(w_raw), ACT.Copy,
                                     scale=w_scale[:, layer - 1, 3:4]).then_inc(w_hi_ready, 1)

            def window(t, side, i, r):
                edges, gat, e0 = side == "edges", t.phase["layer"] - 1 in GATS, t.phase["edge0"]
                if edges:
                    j, slot, there = edge_tile(i, r // 2, ET)
                    before, _, was_there = edge_tile(i, r // 2 - 1, ET)
                if edges and gat and r % 2 == 0 and was_there:
                    weights_turn(before + e0)
                if t.exists(-1):
                    b = t.plus(-1)
                    wait(act, h_ready, b.g + 1)
                    wait(act, row_stored[b.slot], b.slot_uses * 16)
                    if b.phase["layer"] == 1:
                        scale = w_scale[:, 0, 0:1]
                    else:
                        act.wait_ge(grow_ready, b.count(b.phase["g0"] - NT) + 1)
                        scale = grow[b.slot4][:, 0:1]
                    if b.phase["layer"] == 4:
                        wait(act, x1_used, b.pos - 1)
                    nc.scalar.activation(pair(row_out[b.slot]), psum_pair(ps_h[b.slot]), ACT.Copy,
                                         scale=scale).then_inc(row_ready, 1)
                if t.exists(1):
                    b = t.plus(1)
                    wait(act, z_turned, b.g + 1)
                    wait(act, h_ready, b.g - 1)
                    nc.scalar.activation(pair3(z_hi[b.slot]), psum_pair(ps_z), ACT.Copy).then_inc(z_hi_ready, 1)
                if t.exists(2):
                    b = t.plus(2)
                    layer = b.phase["layer"]
                    wait(act, z_turned, b.g - 1)
                    if layer in (1, 3):
                        act.wait_ge(norm_ready, ln_count(b) + 1)
                        if layer == 1:
                            wait(act, x_loaded[b.slot], (b.slot_uses + 1) * 16)
                        frm = row_in[b.slot] if layer == 1 else pre[b.slot]
                        nc.scalar.activation(z[b.slot][:, :], frm[:, :], ACT.Relu, bias=nmr[b.slot4][:, 0:1],
                                             scale=rstd[b.slot4][:, 0:1]).then_inc(z_ready, 1)
                    else:
                        act.wait_ge(shrink_ready, top_count(b) + 1)
                        nc.scalar.activation(z[b.slot][:, :], pre[b.slot][:, :], ACT.Relu,
                                             scale=shrink[b.slot4][:, 0:1]).then_inc(z_ready, 1)
                if edges and r % 2 == 0 and there:
                    carry(t.phase["layer"] - 1, j + e0, slot, i + e0 // 2)
                if edges and gat and r % 2 == 0 and was_there:
                    divide(before + e0)
                if edges and gat and r % 2 == 1 and there:
                    weights(j + e0)

            def carry(layer, h, slot, per_slot):
                act.wait_ge(e_rows[slot], (per_slot + 1) * 32)
                act.wait_ge(edge_done, h + 2)
                if layer in GATS:
                    act.wait_ge(dots_done, h * 3 + 1)
                nc.scalar.activation(eg[slot][0:1, 0:SPLIT], ps_e[0:1, 0, 0:SPLIT], ACT.Copy)
                nc.scalar.activation(eg[slot][0:1, SPLIT:D + 1], ps_e[0:1, 1, 0:D + 1 - SPLIT], ACT.Copy).then_inc(carry_ready, 1)

            def weights(h):
                act.wait_ge(negmax_ready, h + 1)
                nc.scalar.activation(e_wt[:, :], e_arg[:, :], ACT.Exp, bias=e_negmax[:, 0:1])
                nc.scalar.activation(e_self[:, :], lrelu[:, 1:2], ACT.Exp, bias=e_negmax[:, 0:1]).then_inc(weights_done, 1)

            def weights_turn(h):
                act.wait_ge(weights_turned, h + 1)
                nc.scalar.activation(e_wt_t[:, :], e_small, ACT.Copy).then_inc(weights_ready, 1)

            def divide(h):
                act.wait_ge(den_inv, h + 1)
                act.wait_ge(e_stored, (h + 1) * 16)
                nc.scalar.activation(e_out[:, :], e_tmp[:, :], ACT.Copy, scale=e_den[:, 1:2]).then_inc(e_out_ready, 1)

            split_w(1)
            run_windows(act, phases["1"], window, {RANKED + 1: lambda: split_w(2)})
            for phase in chain:
                run_windows(act, phase, window, {"2f": {43: lambda: split_w(3)}, "2m": {15: lambda: split_w(4)}}.get(phase["name"]))

            def last_carry(j, at, per_slot):
                to, slot = last_src[at % 4], at % 2
                act.wait_ge(last_in[at % 4], (per_slot + 1) * 32)
                if not isinstance(j, int) or j > 0:
                    act.wait_ge(e_summed, j + (3 * ET + 1))
                    sums = ps_h[1 - slot]
                    nc.scalar.activation(to[0:1, 0:SPLIT], sums[0:1, 0, 0:SPLIT], ACT.Copy)
                    nc.scalar.activation(to[0:1, SPLIT:D], sums[0:1, 1, 0:D - SPLIT], ACT.Copy).then_inc(carry_ready, 1)
                else:
                    act.sem_inc(carry_ready, 1)

            last_carry(0, 0, 0)
            for at in range(1, 4):
                last_carry(at, at, 0)
            with act.Fori(1, ET // 4) as i:
                for at in range(4):
                    last_carry(i * 4 + at, at, i)

        @block.tensor
        def _(pe):
            def turn(t):
                wait(pe, z_ready, t.g + 1)
                wait(pe, z_lo_ready, t.g)
                for c in range(KC):
                    last = nc.tensor.transpose(ps_z[:, c // 3, (c % 3) * P:(c % 3 + 1) * P],
                                               z[t.slot][:, c * P:(c + 1) * P], ident[:, :])
                last.then_inc(z_turned, 1)

            def products(t, side_step):
                layer, s = t.phase["layer"], t.slot
                wait(pe, z_lo_ready, t.g + 1)
                wait(pe, row_ready, t.g - 1)
                hi, lo = w_hi[w_of[layer]], w_lo[w_of[layer]]
                for c in range(KC):
                    for zp, wp in ((z_hi, hi), (z_hi, lo), (z_lo, hi)):
                        for a in range(2):
                            last = nc.tensor.matmul(ps_h[s][:, a, 0:HALF], zp[s][:, c, :], wp[:, c, a * HALF:(a + 1) * HALF],
                                                    start=(c == 0 and zp is z_hi and wp is hi),
                                                    stop=(c == KC - 1 and zp is z_lo))
                    if c == KC - 1:
                        last.then_inc(h_ready, 1)
                    elif c % 2 == 1:
                        side_step(c // 2)

            def rank_mm(c, slot):
                pe.wait_ge(onehot_ready, c + 1)
                o = onehot[:, slot, :]
                nc.tensor.matmul(sort_ps, o[:, 0:P], sorts[:, slot, :], start=False, stop=False, skip_group_check=True)
                nc.tensor.matmul(count_ps, o[:, P:2 * P], o[:, 2 * P:2 * P + NT], start=False, stop=False,
                                 skip_group_check=True).then_inc(onehot_used, 1)

            def order_mm(c, slot):
                pe.wait_ge(place_ready, c + 1)
                o = onehot[:, slot, :]
                nc.tensor.matmul(perm_ps, o[:, 0:P], o[:, P:P + 3 * NT], start=False, stop=False,
                                 skip_group_check=True).then_inc(place_used, 1)

            def window(t, side, i, r):
                layer = t.phase["layer"]
                if t.exists(1):
                    turn(t.plus(1))
                if t.i is None and t.at == 0 and layer > 1:
                    pe.wait_ge(w_ready, layer)

                def side_step(k):
                    if side == "order+mask" and k == 1:
                        j = i * 4 + r
                        pe.wait_ge(dst_diag, j + 1)
                        nc.tensor.matmul(mask_ps, ones[:, :], diag2[:, :, :].rearrange("p a q -> p (a q)"),
                                         start=True, stop=True, skip_group_check=True).then_inc(mask_mm, 1)
                    if side == "edges" and k == 0:
                        e0 = t.phase["edge0"]
                        j, slot, there = edge_tile(i, r // 2, ET)
                        before, slot_before, was_there = edge_tile(i, r // 2 - 1, ET)
                        if layer - 1 not in GATS:
                            if r % 2 == 1 and there:
                                edge_mm(layer - 1, j + e0, slot)
                        elif r % 2 == 0 and was_there:
                            edge_mm(layer - 1, before + e0, slot_before)
                        elif r % 2 == 1 and there:
                            h = j + e0
                            pe.wait_ge(diag_ready, h + 1)
                            pe.wait_ge(carry_ready, h + 1)
                            wait(pe, edge_done, h + 2)
                            nc.tensor.matmul(e_small, ones[:, :], e_diag[:, :], start=True, stop=True,
                                             skip_group_check=True).then_inc(score_rows, 1)

                if t.exists(0):
                    products(t, side_step)
                if side == "rank" and r % 2 == 1:
                    rank_mm(i * 2 + r // 2, r // 2)
                if side in ("order", "order+mask"):
                    base = 0 if side == "order+mask" else ET // 4 * COLS
                    for c in SHARE[r]:
                        order_mm(i * COLS + (base + c), c)
                if side == "edges" and layer - 1 in GATS and r % 2 == 1:
                    pe.wait_ge(weights_done, i * 2 + (r // 2 + t.phase["edge0"] + 1))
                    nc.tensor.transpose(e_small, e_wt[:, :], ident[:, :]).then_inc(weights_turned, 1)

            def edge_mm(layer, h, slot):
                pe.wait_ge(carry_ready, h + 1)
                if layer in GATS:
                    pe.wait_ge(weights_ready, h + 1)
                else:
                    pe.wait_ge(plain_ready, h - (2 * ET - 1))
                    pe.wait_ge(edge_done, h + 2)
                nc.tensor.matmul(e_lo, e_wt_t[:, :], eg[slot][:, 0:SPLIT], start=True, stop=True, skip_group_check=True)
                nc.tensor.matmul(e_hi, e_wt_t[:, :], eg[slot][:, SPLIT:D + 1], start=True, stop=True,
                                 skip_group_check=True).then_inc(e_summed, 1)

            def clear():
                for a in range(2):
                    last = nc.tensor.matmul(ps_e[:, a, :], e_out[:, 0:P], zeros, start=True, stop=True, skip_group_check=True)
                return last

            def prefixes():
                pe.wait_ge(mid_in, 1)
                fc = flag_cnt[:, :, :].rearrange("p a n -> p (a n)")
                nc.tensor.matmul(ps_e[:, 0, 0:2 * NT], upper[:, :], fc, start=True, stop=True, skip_group_check=True)
                nc.tensor.matmul(ps_e[:, 1, 0:2 * NT], ones[:, :], fc, start=True, stop=True, skip_group_check=True).then_inc(mid_mm, 1)

            def turn_positions():
                pe.wait_ge(mid_in, 2)
                nc.tensor.transpose(ps_e[0:NT, 0, 0:P], work[:, 0, :], ident[:, :]).then_inc(mid_mm, 1)

            def clear_for_order():
                pe.wait_ge(mid_in, 3)
                clear().then_inc(mid_mm, 1)

            def clear_for_edges():
                pe.wait_ge(perm_ready, 1)
                clear().then_inc(e_summed, 1)

            pe.wait_ge(consts_ready, 2)
            clear().then_inc(mid_mm, 1)
            run_windows(pe, phases["1"], window, {0: lambda: pe.wait_ge(w_ready, 1), RANKED: prefixes,
                                                  RANKED + 2: turn_positions, RANKED + 3: clear_for_order})
            for phase in chain:
                run_windows(pe, phase, window, {0: clear_for_edges} if phase["name"] == "2f" else None)

            def last_mm(h, slot, rows):
                pe.wait_ge(carry_ready, h + 1)
                pe.wait_ge(plain_ready, h - (2 * ET - 1))
                pe.wait_ge(edge_done, h + 1)
                nc.tensor.matmul(ps_h[slot][:, 0, 0:SPLIT], e_wt_t[:, :], rows[:, 0:SPLIT], start=True, stop=True)
                nc.tensor.matmul(ps_h[slot][:, 1, 0:D - SPLIT], e_wt_t[:, :], rows[:, SPLIT:D], start=True,
                                 stop=True).then_inc(e_summed, 1)

            pe.wait_ge(row_ready, 4 * NT)
            with pe.Fori(0, ET // 4) as i:
                for at in range(4):
                    last_mm(i * 4 + at + 3 * ET, at % 2, last_src[at])

        @block.vector
        def _(dve):
            steps = [0]

            def step(ins):
                steps[0] += 1
                ins.then_inc(setup_step, 1)
                dve.wait_ge(setup_step, steps[0])

            V = nc.vector

            def max_w(layer):
                dve.wait_ge(w_loaded, 16 * layer)
                V.tensor_reduce(w_scale[:, layer - 1, 0:1], w_raw[:, :], AX_X, ALU.max, apply_absolute_value=True).then_inc(w_max, 1)

            def scale_w(layer):
                sc = w_scale[:, layer - 1, :]
                dve.wait_ge(w_max_all, layer)
                step(V.tensor_scalar(sc[:, 1:2], sc[:, 1:2], TINY, None, ALU.max))
                step(V.tensor_scalar(sc[:, 2:3].bitcast(I32), sc[:, 1:2].bitcast(I32), EXPONENT, None, ALU.bitwise_and))
                step(V.tensor_scalar(sc[:, 2:3], sc[:, 2:3], 1.0 / UP, None, ALU.mult))
                if layer == 1:
                    V.tensor_scalar(sc[:, 0:1], sc[:, 2:3], 1.0 / UP_LN, None, ALU.mult)
                V.reciprocal(sc[:, 3:4], sc[:, 2:3]).then_inc(w_scaled, 1)

            def low_w(layer):
                dve.wait_ge(w_hi_ready, layer)
                V.scalar_tensor_tensor(w_lo[w_of[layer]][:, :, :].rearrange("p c n -> p (c n)"), w_raw[:, :],
                                       w_scale[:, layer - 1, 3:4],
                                       w_hi[w_of[layer]][:, :, :].rearrange("p c n -> p (c n)"),
                                       ALU.mult, ALU.subtract).then_inc(w_ready, 1)

            def prepare(t):
                layer, s, s4 = t.phase["layer"], t.slot, t.slot4
                if layer == 1:
                    dve.wait_ge(x_loaded[s], (t.slot_uses + 1) * 16)
                else:
                    dve.wait_ge(in_ready[t.phase["name"]][s], (t.phase_uses + 1) * 16)
                if layer in (1, 3):
                    rows = row_in[s]
                    if layer == 3:
                        rows = pre[s]
                        dve.wait_ge(x_ready[s], (t.layer_uses + 1) * 16)
                        wait(dve, x1_stored[s], t.layer_uses * 16)
                        wait(dve, z_ready, t.g - 1)
                        k = t.count(t.phase["g0"] - NT)
                        V.tensor_tensor(pre[s][:, :], row_in[s][:, :], row_in2[s][:, :], ALU.add).then_inc(in_used, 1)
                        dve.wait_ge(in_used, k + 1)
                        V.tensor_tensor(pre[s][:, :], pre[s][:, :], bias_bc[2][:, :], ALU.add).then_inc(x1_ready, 1)
                        dve.wait_ge(x1_ready, t.pos + 1)
                    k = ln_count(t)
                    for a in range(2):
                        last = V.bn_stats(bn[s][:, 6 * a:6 * a + 6], rows[:, a * HALF:(a + 1) * HALF])
                    last.then_inc(stats_done, 1)
                    dve.wait_ge(stats_done, k + 1)
                    dve.sem_inc(dve_gate, 1)
                    V.bn_aggr(mv[s4][:, :], bn[s][:, :]).then_inc(mean_var, 1)
                    if layer == 3:
                        V.tensor_scalar(grow[s4][:, :], dinv_grow[:, 0, bass.ds(t.pos, 1)], 1.0, None, ALU.mult).then_inc(grow_ready, 1)
                    return
                k = t.count(t.phase["g0"] - NT)
                n = top_count(t)
                wait(dve, z_ready, t.g - 1)
                if layer == 4 and t.i is None and t.pos < 2:
                    dve.wait_ge(x1_stored[s], 16 * (NT // 2 + 1 - s))
                b = bias_bc[layer - 1]
                if layer == 4 and t.phase["mixed"]:
                    V.scalar_tensor_tensor(pre[s][:, :], row_in[s][:, :], dinv[:, bass.ds(t.pos, 1)], b[:, :],
                                           ALU.mult, ALU.add).then_inc(in_used, 1)
                    dve.wait_ge(in_used, k + 1)
                    V.tensor_reduce(top[s4][:, :], pre[s][:, :], AX_X, ALU.max).then_inc(top_found, 1)
                    dve.wait_ge(top_found, t.count(0) + 1)
                else:
                    dve.sem_inc(dve_gate, 1)
                    V.tensor_tensor_reduce(pre[s][:, :], row_in[s][:, :], b[:, :], 1.0, -FAR, ALU.add, ALU.max,
                                           top[s4][:, :]).then_inc(in_used, 1)
                    dve.wait_ge(in_used, k + 1)
                V.tensor_scalar(topc[s4][:, :], top[s4][:, :], TINY, 1.0 / UP, ALU.max, ALU.mult).then_inc(top_kept, 1)
                dve.wait_ge(top_kept, n + 1)
                V.reciprocal(shrink[s4][:, :], topc[s4][:, :]).then_inc(shrink_ready, 1)
                by = w_scale[:, 1, 2:3] if layer == 2 else dinv_grow[:, 1, bass.ds(t.pos, 1)]
                V.tensor_scalar(grow[s4][:, :], topc[s4][:, :], by, None, ALU.mult).then_inc(grow_ready, 1)

            def low_parts(t):
                wait(dve, z_hi_ready, t.g + 1)
                V.tensor_tensor(pair3(z_lo[t.slot]), psum_pair(ps_z), pair3(z_hi[t.slot]), ALU.subtract).then_inc(z_lo_ready, 1)

            def result(t):
                s = t.slot
                wait(dve, row_ready, t.g + 1)
                dve.wait_ge(x1_loaded[s], (t.layer_uses + 1) * 16)
                wait(dve, res_stored[s], t.layer_uses * 16)
                if t.phase["mixed"]:
                    if t.at > 1 or t.i is not None:
                        dve.wait_ge(base_stored[s], t.phase_uses * 16)
                    V.tensor_scalar(base_out[s][:, D:D + 1], dinv[:, bass.ds(t.pos, 1)], 1.0, None, ALU.mult)
                    V.scalar_tensor_tensor(pre_out[s], row_out[s][:, :], dinv[:, bass.ds(t.pos, 1)], row_in2[s][:, :],
                                           ALU.mult, ALU.add).then_inc(x1_used, 1)
                else:
                    V.tensor_tensor(pre_out[s], row_out[s][:, :], row_in2[s][:, :], ALU.add).then_inc(x1_used, 1)
                dve.wait_ge(x1_used, t.pos + 1)
                V.tensor_tensor(pre_out[s][:, :], pre_out[s][:, :], bias_bc[4][:, :], ALU.add).then_inc(res_ready, 1)

            def edge_dots(layer, h, slot, per_slot, which):
                if 0 in which:
                    dve.wait_ge(e_rows[slot], (per_slot + 1) * 32)
                for n in which:
                    rows, att = ((eg[slot][:, 0:D], atts_bc), (eh[slot][:, :], atts_bc), (eh[slot][:, :], attd_bc))[n]
                    V.tensor_tensor_reduce(e_prod[:, :], rows, att[layer][:, :], 1.0, 0.0, ALU.mult, ALU.add,
                                           dots[:, n:n + 1]).then_inc(dots_done, 1)
                    dve.wait_ge(dots_done, h * 3 + (n + 1))

            def edge_scores(h, slot):
                wait(dve, weights_done, h)
                V.tensor_scalar(score[:, :], dots[:, 0:2], dots[:, 2:3], None, ALU.add).then_inc(score_done, 1)
                dve.wait_ge(score_done, h + 1)
                V.scalar_tensor_tensor(lrelu[:, :], score[:, :], NEG_SLOPE, score[:, :], ALU.mult, ALU.max).then_inc(lrelu_done, 1)
                dve.wait_ge(lrelu_done, h + 1)
                V.tensor_copy(lrelu[0:1, 0:1], e_max[1 - slot][0:1, :]).then_inc(score_fixed, 1)
                dve.wait_ge(score_fixed, h + 1)
                V.tensor_scalar(e_diag[:, :], ident[:, :], lrelu[:, 0:1], None, ALU.mult).then_inc(diag_ready, 1)

            def edge_max(h, slot, j):
                dve.wait_ge(score_rows, h + 1)
                V.tensor_tensor(e_arg[:, :], e_small, far_mask[:, bass.ds(j, 1), :].rearrange("p a q -> p (a q)"), ALU.add).then_inc(arg_done, 1)
                dve.wait_ge(arg_done, h + 1)
                V.tensor_reduce(e_top[:, :], e_arg[:, :], AX_X, ALU.max).then_inc(top_done, 1)
                dve.wait_ge(top_done, h + 1)
                V.tensor_tensor(e_max[slot][:, :], e_top[:, :], lrelu[:, 1:2], ALU.max).then_inc(max_done, 1)
                dve.wait_ge(max_done, h + 1)
                V.tensor_scalar(e_negmax[:, :], e_max[slot][:, :], -1.0, None, ALU.mult).then_inc(negmax_ready, 1)

            def edge_sums(layer, h, slot):
                dve.wait_ge(e_summed, h + 2)
                if layer in GATS:
                    V.tensor_tensor(e_den[:, 0:1], e_den_ps, e_self[:, :], ALU.add).then_inc(den_done, 1)
                    dve.wait_ge(den_done, h + 1)
                    V.scalar_tensor_tensor(e_tmp[:, 0:SPLIT], eh[slot][:, 0:SPLIT], e_self[:, 0:1], e_lo, ALU.mult, ALU.add)
                    V.scalar_tensor_tensor(e_tmp[:, SPLIT:D], eh[slot][:, SPLIT:D], e_self[:, 0:1], ps_e[:, 1, 0:D - SPLIT],
                                           ALU.mult, ALU.add).then_inc(edge_done, 1)
                    V.reciprocal(e_den[:, 1:2], e_den[:, 0:1]).then_inc(den_inv, 1)
                else:
                    dve.wait_ge(e_stored, (h + 1) * 16)
                    V.tensor_tensor(e_out[:, 0:SPLIT], eh[slot][:, 0:SPLIT], e_lo, ALU.add)
                    V.tensor_tensor(e_out[:, SPLIT:D], eh[slot][:, SPLIT:D], ps_e[:, 1, 0:D - SPLIT], ALU.add).then_inc(edge_done, 1)

            def edge_plain(h, j):
                dve.wait_ge(e_summed, h + 1)
                V.tensor_scalar(e_wt_t[:, :], same_t[:, bass.ds(j, 1), :].rearrange("p a q -> p (a q)"), 1.0, None,
                                ALU.mult).then_inc(plain_ready, 1)

            def rank_column(c, slot):
                col = bass.ds(c, 1)
                dve.wait_ge(onehot_used, c + 1)
                k = c * 5
                V.scalar_tensor_tensor(row_cmp, row_iota, edge_id[:, col], row_dst, ALU.is_lt, ALU.subtract).then_inc(ranks_step, 1)
                dve.wait_ge(ranks_step, k + 1)
                V.tensor_scalar(row_cmp, row_cmp, e_f[:, 2, col], 0.0, ALU.is_gt, ALU.add, accum_out=e_rank[:, 0, 0:1]).then_inc(ranks_step, 1)
                dve.wait_ge(ranks_step, k + 2)
                V.tensor_scalar(e_rank[:, 3, :], tile_ends[:, :], e_rank[:, 0, 0:1], 0.0, ALU.is_le, ALU.add,
                                accum_out=e_rank[:, 1, 0:1]).then_inc(ranks_step, 1)
                dve.wait_ge(ranks_step, k + 3)
                V.tensor_scalar(e_rank[:, 2, 0:1], e_rank[:, 1, 0:1], -float(SLOTS), e_rank[:, 0, 0:1], ALU.mult, ALU.add).then_inc(ranks_step, 1)
                dve.wait_ge(ranks_step, k + 4)
                o = onehot[:, slot, :]
                V.tensor_scalar(o[:, 0:P], iota_m1[:, :], e_rank[:, 2, 0:1], None, ALU.is_equal).then_inc(ranks_step, 1)
                V.tensor_scalar(sorts[:, slot, 0:ET], iota_c[:, 0:ET], e_rank[:, 1, 0:1], e_f[:, 0, col], ALU.is_equal, ALU.mult)
                V.tensor_scalar(sorts[:, slot, ET:2 * ET], iota_c[:, 0:ET], e_rank[:, 1, 0:1], e_f[:, 1, col], ALU.is_equal, ALU.mult)
                V.tensor_scalar(o[:, P:2 * P], iota_c[:, :], e_f[:, 3, col], None, ALU.is_equal)
                V.tensor_scalar(o[:, 2 * P:2 * P + NT], iota_c[:, 0:NT], e_f[:, 4, col], None, ALU.is_equal)
                dve.wait_ge(ranks_step, k + 5)
                V.tensor_copy(o[:, 0:1], o[:, P - 1:P]).then_inc(onehot_ready, 1)

            f, cnt = flag_cnt[:, 0, :], flag_cnt[:, 1, :]
            w0, w1, w2, w3 = (work[:, k, :] for k in range(4))

            def keep_ranks():
                dve.wait_ge(onehot_used, 2 + EC)
                V.tensor_copy(sorted_src[:, :], sort_ps[:, 0:ET])
                V.tensor_copy(sorted_dst_i[:, :], sort_ps[:, ET:2 * ET])
                V.tensor_copy(dst_in[:, :], sort_ps[:, ET:2 * ET])
                step(V.tensor_copy(dst_of[:, :], sort_ps[:, ET:2 * ET]))
                V.tensor_copy(dst_in[0:1, 1:ET], dst_of[0:1, 0:ET - 1])
                V.memset(dst_in[0:1, 0:1], -1.0)
                step(V.tensor_copy(cnt, count_ps))
                step(V.tensor_scalar(f, cnt, 0.0, None, ALU.is_gt))
                dve.sem_inc(mid_in, 1)

            def node_positions():
                dve.wait_ge(mid_mm, 2)
                below, total = (ps_e[:, a, 0:2 * NT].rearrange("p (a n) -> p a n", a=2) for a in range(2))
                V.tensor_copy(scan[2][:, :, :], total)
                step(V.tensor_copy(scan[0][:, :, :], total))
                at, d = 0, 1
                while d < NT:
                    V.tensor_copy(scan[1 - at][:, :, 0:d], scan[at][:, :, 0:d])
                    step(V.tensor_tensor(scan[1 - at][:, :, d:NT], scan[at][:, :, d:NT], scan[at][:, :, 0:NT - d], ALU.add))
                    at, d = 1 - at, 2 * d
                incl, before = scan[at], scan[1 - at]
                step(V.tensor_tensor(before[:, :, :], incl[:, :, :], scan[2][:, :, :], ALU.subtract))
                step(V.tensor_tensor(before[:, :, :], before[:, :, :], below, ALU.add))
                A, C = before[:, 0, :], before[:, 1, :]
                step(V.tensor_scalar(w3[:, 0:1], incl[:, 0, NT - 1:NT], -1.0, float(NP), ALU.mult, ALU.add))
                step(V.scalar_tensor_tensor(w0, A, 2.0, node_id[:, :], ALU.mult, ALU.subtract))
                step(V.tensor_scalar(w0, w0, w3[:, 0:1], None, ALU.add))
                step(V.tensor_tensor(w0, w0, f, ALU.mult))
                step(V.tensor_tensor(w1, node_id[:, :], A, ALU.subtract))
                step(V.scalar_tensor_tensor(place[:, 2, 0:NT], C, -1.0, cnt, ALU.add, ALU.add))
                step(V.tensor_tensor(w0, w0, w1, ALU.add))
                dve.sem_inc(mid_in, 1)
                step(V.tensor_copy(place_i[:, 0, :], w0))

            def last_edges():
                dve.wait_ge(mid_mm, 3)
                step(V.tensor_copy(pos_t[0:NT, :], ps_e[0:NT, 0, 0:P]))
                dve.sem_inc(mid_in, 1)
                dve.sem_inc(pos_ready, 1)
                step(V.tensor_copy(w1, place[:, 2, 0:NT]))
                step(V.tensor_copy(w2, w1))
                for j in range(ET):
                    step(V.scalar_tensor_tensor(w2, w1, float(SLOTS * (j + 1)), w2, ALU.is_ge, ALU.add))

            def node_places():
                V.tensor_scalar(place_i[:, 1, :], place_i[:, 0, :], P - 1, None, ALU.bitwise_and)
                step(V.tensor_scalar(place_i[:, 2, :], place_i[:, 0, :], 7, None, ALU.arith_shift_right))
                step(V.memset(place[:, :, :], -1.0))
                V.tensor_copy(place[:, 0, 0:NT], place_i[:, 1, :])
                V.tensor_copy(place[:, 1, 0:NT], place_i[:, 2, :])
                step(V.tensor_scalar(w2, w2, float(AGG + 1), float(ROWS - 1), ALU.add, ALU.min))
                step(V.tensor_tensor(w2, w2, node_id[:, :], ALU.subtract))
                step(V.tensor_tensor(w2, w2, f, ALU.mult))
                step(V.tensor_tensor(place[:, 2, 0:NT], w2, node_id[:, :], ALU.add))
                V.tensor_copy(node_id_pad[:, 0:NT], node_id[:, :])
                step(V.tensor_copy(cnt_pad[:, 0:NT], cnt))
                dve.wait_ge(mid_mm, 4)

            def order_column(c, slot, at):
                dve.wait_ge(place_used, c + 1)
                o, col = onehot[:, slot, :], bass.ds(c, 1)
                V.tensor_scalar(o[:, 0:P], iota_c[:, :], place[:, 0, col], None, ALU.is_equal)
                V.tensor_scalar(o[:, P:P + NT], iota_c[:, 0:NT], place[:, 1, col], node_id_pad[:, col], ALU.is_equal, ALU.mult)
                V.tensor_scalar(o[:, P + NT:P + 2 * NT], iota_c[:, 0:NT], place[:, 1, col], place[:, 2, col], ALU.is_equal, ALU.mult)
                V.tensor_scalar(o[:, P + 2 * NT:P + 3 * NT], iota_c[:, 0:NT], place[:, 1, col], cnt_pad[:, col],
                                ALU.is_equal, ALU.mult).then_inc(place_ready, 1)

            def mask_diag(j):
                col = bass.ds(j, 1)
                V.tensor_scalar(diag2[:, 0, :], ident[:, :], dst_in[:, col], None, ALU.mult)
                V.tensor_scalar(diag2[:, 1, :], ident[:, :], dst_of[:, col], None, ALU.mult).then_inc(dst_diag, 1)

            def mask_make(j):
                col = bass.ds(j, 1)
                far = far_mask[:, col, :].rearrange("p a q -> p (a q)")
                dve.wait_ge(mask_mm, j + 1)
                V.tensor_scalar(e_arg[:, :], mask_ps[:, 0:P], dst_of[:, col], FAR, ALU.is_equal, ALU.mult).then_inc(mask_part, 1)
                V.tensor_scalar(same_t[:, col, :].rearrange("p a q -> p (a q)"), mask_ps[:, P:2 * P], dst_in[:, col], None, ALU.is_equal)
                dve.wait_ge(mask_part, j + 1)
                V.tensor_scalar(far, e_arg[:, :], -FAR, None, ALU.add).then_inc(mask_ready, 1)

            def window(t, side, i, r):
                layer = t.phase["layer"]
                edges, gat, e0 = side == "edges", layer - 1 in GATS, t.phase["edge0"]
                if edges:
                    j, slot, there = edge_tile(i, r // 2, ET)
                    before, slot_before, was_there = edge_tile(i, r // 2 - 1, ET)
                if t.exists(-1) and t.plus(-1).phase["layer"] == 4:
                    result(t.plus(-1))
                if t.exists(1):
                    low_parts(t.plus(1))
                if edges and r % 2 == 0:
                    if gat:
                        if there:
                            edge_dots(layer - 1, j + e0, slot, i + e0 // 2, (0, 1))
                        if was_there:
                            edge_sums(layer - 1, before + e0, slot_before)
                        if there:
                            edge_dots(layer - 1, j + e0, slot, i + e0 // 2, (2,))
                            edge_scores(j + e0, slot)
                    elif there:
                        edge_plain(j + e0, j)
                if edges and gat and r % 2 == 1:
                    edge_max(j + e0, slot, j)
                if side == "order+mask":
                    mask_diag(i * 4 + r)
                if t.exists(3):
                    prepare(t.plus(3))
                if side == "rank" and r % 2 == 0:
                    rank_column(i * 2 + r // 2, r // 2)
                if side in ("order", "order+mask"):
                    base = 0 if side == "order+mask" else ET // 4 * COLS
                    for c in SHARE[r]:
                        order_column(i * COLS + (base + c), c, c)
                if side == "order+mask":
                    mask_make(i * 4 + r)
                if edges and not gat and r % 2 == 1:
                    edge_sums(layer - 1, j + e0, slot)

            V.memset(e_src[:, :], PAD)
            V.memset(e_dst[:, :], PAD)
            V.memset(node_id_pad[:, :], 0.0)
            V.memset(cnt_pad[:, :], 0.0)
            for s in range(2):
                V.memset(e_max[s][:, :], 0.0)
            V.memset(row_cmp[:, E:EP].bitcast(I32), PAD).then_inc(graph_padded, 1)
            dve.sem_inc(edge_done, 2)
            dve.sem_inc(onehot_used, 2)
            dve.sem_inc(place_used, COLS)
            dve.wait_ge(consts_ready, 2)
            max_w(1)
            scale_w(1)
            dve.wait_ge(graph_loaded, 48)
            V.tensor_scalar(row_dst, row_cmp.bitcast(I32), 2.0, None, ALU.mult)
            V.tensor_copy(e_f[:, 0, :], e_src[:, :])
            V.tensor_copy(e_f[:, 1, :], e_dst[:, :])
            V.tensor_scalar(e_f[:, 2, :], e_dst[:, :], -2.0, None, ALU.mult)
            V.tensor_scalar(e_part[:, 0, :], e_dst[:, :], P - 1, None, ALU.bitwise_and)
            step(V.tensor_scalar(e_part[:, 1, :], e_dst[:, :], 7, None, ALU.arith_shift_right))
            V.tensor_copy(e_f[:, 3, :], e_part[:, 0, :])
            step(V.tensor_copy(e_f[:, 4, :], e_part[:, 1, :]))

            def start_order():
                dve.wait_ge(mid_mm, 1)
            def order_complete():
                dve.wait_ge(place_used, COLS + COLS * (-(-NT // COLS)))
                step(V.tensor_copy(perm_f[:, :, :], perm_ps.rearrange("p (a n) -> p a n", a=3)))
                V.tensor_copy(perm_agg[:, :], perm_f[:, 1, :])
                V.tensor_copy(perm[:, :], perm_f[:, 0, :])
                V.scalar_tensor_tensor(perm_out[:, :], perm_f[:, 2, :], float(NP), perm_f[:, 0, :], ALU.mult, ALU.add)
                V.tensor_scalar(perm_x[:, :], perm_f[:, 0, :], float(N - 1), None, ALU.min)
                step(V.tensor_scalar(work[:, 0, :], perm_f[:, 2, :], 0.0, None, ALU.is_gt))
                step(V.tensor_tensor(work[:, 1, :], perm_f[:, 1, :], node_id[:, :], ALU.subtract))
                step(V.tensor_tensor(work[:, 1, :], work[:, 1, :], work[:, 0, :], ALU.mult))
                step(V.tensor_tensor(pos_agg[:, :], work[:, 1, :], node_id[:, :], ALU.add))
                for s in range(2):
                    step(V.memset(eg[s][:, D:D + 1], 1.0))
                dve.sem_inc(perm_ready, 1)

            def degrees():
                dve.wait_ge(params_loaded, 16 * 8)
                step(V.tensor_scalar(perm_f[:, 2, :], perm_f[:, 2, :], 1.0, None, ALU.add))
                step(V.memset(work[:, 2, :], -0.5))
                dve.sem_inc(sqrt_in, 1)

            def dinv_exact():
                dve.wait_ge(sqrt_done, 1)
                step(V.tensor_tensor(work[:, 0, :], dinv[:, :], dinv[:, :], ALU.mult))
                step(V.tensor_tensor(work[:, 0, :], work[:, 0, :], perm_f[:, 2, :], ALU.mult))
                step(V.tensor_scalar(work[:, 0, :], work[:, 0, :], -0.5, 1.5, ALU.mult, ALU.add))
                step(V.tensor_tensor(dinv[:, :], dinv[:, :], work[:, 0, :], ALU.mult))

            run_windows(dve, phases["1"], window,
                        {-1: lambda: low_w(1), 0: start_order, 2: lambda: max_w(2), RANKED: lambda: (scale_w(2), keep_ranks()), RANKED + 1: node_positions,
                         RANKED + 2: last_edges, RANKED + 3: node_places,
                         ORDER + ET: lambda: low_w(2),
                         ORDERED: order_complete, ORDERED + 2: degrees})

            def grow3():
                scale_w(3)
                step(V.tensor_scalar(dinv_grow[:, 0, :], dinv[:, :], w_scale[:, 2, 2:3], 1.0 / UP_LN, ALU.mult, ALU.mult))

            def grow4():
                scale_w(4)
                step(V.tensor_scalar(dinv_grow[:, 1, :], dinv[:, :], w_scale[:, 3, 2:3], None, ALU.mult))

            for phase in chain:
                run_windows(dve, phase, window, {"2f": {0: lambda: (dinv_exact(), max_w(3)), 43: grow3, 55: lambda: low_w(3)},
                                                 "2m": {0: lambda: max_w(4), 15: grow4, 16: lambda: low_w(4)}}.get(phase["name"]))

            def last_result(j, at, turn):
                h, s, base = j + 3 * ET, at % 2, last_base[at % 4]
                dve.wait_ge(e_summed, h + 2)
                if not isinstance(j, int) or j < ET - 1:
                    dve.wait_ge(carry_ready, h + 2)
                wait(dve, last_stored[s], (turn * 2 + at // 2) * 16)
                V.tensor_copy(idx_o[s][:, :], sorted_dst_i[:, bass.ds(j, 1)])
                by = base[:, D:D + 1]
                V.scalar_tensor_tensor(pre_out[s][:, 0:SPLIT], ps_h[s][:, 0, 0:SPLIT], by, base[:, 0:SPLIT], ALU.mult, ALU.add)
                V.scalar_tensor_tensor(pre_out[s][:, SPLIT:D], ps_h[s][:, 1, 0:D - SPLIT], by, base[:, SPLIT:D],
                                       ALU.mult, ALU.add).then_inc(edge_done, 1)

            V.tensor_scalar(pos_base[:, :], pos_dst[:, :], -FREE * P, None, ALU.add).then_inc(base_idx_ready, 1)
            dve.wait_ge(base_idx_ready, 1)

            def last_indices(j, at):
                V.tensor_copy(last_idx[at % 4][:, 0:1], pos_src[:, bass.ds(j, 1)])
                V.tensor_copy(last_idx[at % 4][:, 1:2], pos_base[:, bass.ds(j, 1)]).then_inc(last_idx_ready, 1)

            for s, v in all_slots(phases["4f"]["g0"], NT):
                dve.wait_ge(res_stored[s], v)
            for s, v in all_slots(phases["4m"]["g0"], MIXED):
                dve.wait_ge(base_stored[s], v)
            def last_turn(at, i=None, more=True):
                j = at if i is None else i * 4 + at
                if i is not None or at < ET - 1:
                    edge_plain(j + (1 + 3 * ET), j + 1)
                last_result(j, at, 0 if i is None else i)
                if more:
                    last_indices(j + 4, at)

            for at in range(4):
                last_indices(at, at)
            edge_plain(3 * ET, 0)
            for at in range(3):
                last_turn(at)
            with dve.Fori(0, ET // 4 - 2) as i:
                for at in range(3, 7):
                    last_turn(at, i)
            for at in range(ET - 5, ET):
                last_turn(at, more=at < ET - 4)


_INS = ["x", "src", "dst", "L0_gnn_W1", "L0_gnn_att_src1", "L0_gnn_att_dst1", "L0_gnn_b1", "L0_gnn_W2", "L0_gnn_att_src2",
        "L0_gnn_att_dst2", "L0_gnn_b2", "L1_gnn_W1", "L1_gnn_b1", "L1_gnn_W2", "L1_gnn_b2"]


def kernel(**inputs):
    import numpy as _np
    import concourse.bacc as _bacc
    from concourse import mybir as _mybir
    from concourse.bass_utils import run_bass_kernel_spmd as _run

    nc = _bacc.Bacc("TRN2", target_bir_lowering=False, num_devices=1)
    arrays, a = {}, {}
    for name in _INS:
        v = _np.ascontiguousarray(inputs[name])
        arrays[f"in_{name}"] = v
        a[name] = nc.dram_tensor(f"in_{name}", v.shape, _mybir.dt.from_np(v.dtype), kind="ExternalInput").ap()
    out = nc.dram_tensor("out", inputs["x"].shape, _mybir.dt.float32, kind="ExternalOutput").ap()
    build(nc, a["x"], a["src"], a["dst"],
          {1: a["L0_gnn_W1"], 2: a["L0_gnn_W2"], 3: a["L1_gnn_W1"], 4: a["L1_gnn_W2"]},
          {1: a["L0_gnn_att_src1"], 2: a["L0_gnn_att_src2"]}, {1: a["L0_gnn_att_dst1"], 2: a["L0_gnn_att_dst2"]},
          {1: a["L0_gnn_b1"], 2: a["L0_gnn_b2"], 3: a["L1_gnn_b1"], 4: a["L1_gnn_b2"]}, out)
    r = _run(nc, [arrays], core_ids=[0])
    return r.results[0]["out"]
```
